# Optimizing a Trainium2 kernel written in Bass

```python
import numpy as np
import jax
import jax.numpy as jnp

def _softmax(x, axis=-1):
    return jax.nn.softmax(x, axis=axis)

def _gelu(x):
    return jax.nn.gelu(x, approximate=True)

def _silu(x):
    return jax.nn.silu(x)

def _sigmoid(x):
    return jax.nn.sigmoid(x)

def _layernorm(x, axis=-1, eps=1e-05):
    m = jnp.mean(x, axis=axis, keepdims=True)
    v = jnp.var(x, axis=axis, keepdims=True)
    return (x - m) / jnp.sqrt(v + eps)

def _scatter_add(tgt, idx, src, axis=0):
    return tgt.at[idx].add(src)

def _segment_sum(src, seg, n):
    return jax.ops.segment_sum(src, seg, n)
kernel_name = 'mk_recurrent_d1_jaxref_r8_ce7b84'

def setup_inputs(seed: int=0):
    np.random.seed(seed)
    _w = jnp.asarray

    def _L0_attn_setup():
        import jax, jax.numpy as jnp
        import numpy as np
        from jax.scipy.linalg import expm
        EPS = 1e-05

        def _layernorm(x, g, b):
            m = x.mean(-1, keepdims=True)
            v = ((x - m) ** 2).mean(-1, keepdims=True)
            return (x - m) / jnp.sqrt(v + EPS) * g + b
        H, S, K = (128, 64, 3)
        B, T = (4, 512)
        key = jax.random.key(seed)
        ks = jax.random.split(key, 12)
        sc = 0.02
        inp = {'x': jax.random.normal(ks[0], (B, T, H), jnp.float32), 'A': -jnp.abs(jax.random.normal(ks[1], (S, S), jnp.float32) * sc), 'dt_A': jnp.asarray(0.1, jnp.float32), 'B_w': jax.random.normal(ks[2], (S, H), jnp.float32) * sc, 'B_b': jnp.zeros((S,), jnp.float32), 'C_w': jax.random.normal(ks[3], (S, H), jnp.float32) * sc, 'C_b': jnp.zeros((S,), jnp.float32), 'D_w': jax.random.normal(ks[4], (H, S), jnp.float32) * sc, 'D_b': jnp.zeros((H,), jnp.float32), 'conv_w': jax.random.normal(ks[5], (H, 1, K), jnp.float32) * sc, 'conv_b': jnp.zeros((H,), jnp.float32), 'gate_w': jax.random.normal(ks[6], (2 * H, H), jnp.float32) * sc, 'gate_b': jnp.zeros((2 * H,), jnp.float32), 'ln_in_g': jnp.ones((H,), jnp.float32), 'ln_in_b': jnp.zeros((H,), jnp.float32), 'ln_st_g': jnp.ones((S,), jnp.float32), 'ln_st_b': jnp.zeros((S,), jnp.float32)}
        return inp
    _L0_attn_in = _L0_attn_setup()

    def _L0_ffn_setup():
        import jax, jax.numpy as jnp
        import numpy as np
        from jax.scipy.linalg import expm
        B, S, D, E, K, NROT = (2, 256, 128, 8, 2, 3)
        EPS = 1e-05

        def _gelu(x):
            return jax.nn.gelu(x, approximate=False)

        def _forward(x, ln_gamma, ln_beta, abel_w, abel_b, moe_gate_w, moe_gate_b, ew1, eb1, ew2, eb2, gens, gc_w, gc_b):
            residual = x
            mu = jnp.mean(x, axis=-1, keepdims=True)
            var = jnp.mean((x - mu) ** 2, axis=-1, keepdims=True)
            xn = (x - mu) * jax.lax.rsqrt(var + EPS) * ln_gamma + ln_beta
            abel_out = _gelu(xn @ abel_w + abel_b)
            logits = xn @ moe_gate_w + moe_gate_b
            topw, topi = jax.lax.top_k(logits, K)
            topw = jax.nn.softmax(topw, axis=-1)
            w_dense = jnp.sum(jax.nn.one_hot(topi, E, dtype=xn.dtype) * topw[..., None], axis=-2)
            h = _gelu(jnp.einsum('bsd,edh->ebsh', xn, ew1) + eb1[:, None, None, :])
            eo = jnp.einsum('ebsh,ehd->ebsd', h, ew2) + eb2[:, None, None, :]
            moe_out = jnp.einsum('ebsd,bse->bsd', eo, w_dense)
            for i in range(NROT):
                moe_out = moe_out @ expm(gens[i])
            combined = jnp.concatenate([abel_out, moe_out], axis=-1)
            gate = jax.nn.sigmoid(combined @ gc_w + gc_b)
            mixed = abel_out * (1.0 - gate) + moe_out * gate
            return residual + mixed
        key = jax.random.key(seed)
        ks = jax.random.split(key, 16)
        sc = 0.02
        x = jax.random.normal(ks[0], (B, S, D), jnp.float32)
        ln_gamma = 1.0 + sc * jax.random.normal(ks[1], (D,), jnp.float32)
        ln_beta = sc * jax.random.normal(ks[2], (D,), jnp.float32)
        abel_w = sc * jax.random.normal(ks[3], (D, D), jnp.float32)
        abel_b = sc * jax.random.normal(ks[4], (D,), jnp.float32)
        moe_gate_w = sc * jax.random.normal(ks[5], (D, E), jnp.float32)
        moe_gate_b = sc * jax.random.normal(ks[6], (E,), jnp.float32)
        ew1 = sc * jax.random.normal(ks[7], (E, D, 2 * D), jnp.float32)
        eb1 = sc * jax.random.normal(ks[8], (E, 2 * D), jnp.float32)
        ew2 = sc * jax.random.normal(ks[9], (E, 2 * D, D), jnp.float32)
        eb2 = sc * jax.random.normal(ks[10], (E, D), jnp.float32)
        g = sc * jax.random.normal(ks[11], (NROT, D, D), jnp.float32)
        gens = 0.5 * (g - jnp.swapaxes(g, -1, -2))
        gc_w = sc * jax.random.normal(ks[12], (2 * D, 1), jnp.float32)
        gc_b = sc * jax.random.normal(ks[13], (1,), jnp.float32)
        return dict(x=x, ln_gamma=ln_gamma, ln_beta=ln_beta, abel_w=abel_w, abel_b=abel_b, moe_gate_w=moe_gate_w, moe_gate_b=moe_gate_b, ew1=ew1, eb1=eb1, ew2=ew2, eb2=eb2, gens=gens, gc_w=gc_w, gc_b=gc_b)
    _L0_ffn_in = _L0_ffn_setup()
    _d = {'L0_attn_x': _L0_attn_in['x'], 'L0_attn_A': _L0_attn_in['A'], 'L0_attn_dt_A': _L0_attn_in['dt_A'], 'L0_attn_B_w': _L0_attn_in['B_w'], 'L0_attn_B_b': _L0_attn_in['B_b'], 'L0_attn_C_w': _L0_attn_in['C_w'], 'L0_attn_C_b': _L0_attn_in['C_b'], 'L0_attn_D_w': _L0_attn_in['D_w'], 'L0_attn_D_b': _L0_attn_in['D_b'], 'L0_attn_conv_w': _L0_attn_in['conv_w'], 'L0_attn_conv_b': _L0_attn_in['conv_b'], 'L0_attn_gate_w': _L0_attn_in['gate_w'], 'L0_attn_gate_b': _L0_attn_in['gate_b'], 'L0_attn_ln_in_g': _L0_attn_in['ln_in_g'], 'L0_attn_ln_in_b': _L0_attn_in['ln_in_b'], 'L0_attn_ln_st_g': _L0_attn_in['ln_st_g'], 'L0_attn_ln_st_b': _L0_attn_in['ln_st_b'], 'L0_ffn_ln_gamma': _L0_ffn_in['ln_gamma'], 'L0_ffn_ln_beta': _L0_ffn_in['ln_beta'], 'L0_ffn_abel_w': _L0_ffn_in['abel_w'], 'L0_ffn_abel_b': _L0_ffn_in['abel_b'], 'L0_ffn_moe_gate_w': _L0_ffn_in['moe_gate_w'], 'L0_ffn_moe_gate_b': _L0_ffn_in['moe_gate_b'], 'L0_ffn_ew1': _L0_ffn_in['ew1'], 'L0_ffn_eb1': _L0_ffn_in['eb1'], 'L0_ffn_ew2': _L0_ffn_in['ew2'], 'L0_ffn_eb2': _L0_ffn_in['eb2'], 'L0_ffn_gens': _L0_ffn_in['gens'], 'L0_ffn_gc_w': _L0_ffn_in['gc_w'], 'L0_ffn_gc_b': _L0_ffn_in['gc_b']}
    _x0 = _d['L0_attn_x']
    _d['L0_attn_x'] = jax.random.normal(jax.random.fold_in(jax.random.key(seed), 1), (8, 512, 128), dtype=_x0.dtype)
    del _x0
    return _d

def reference(L0_attn_x, L0_attn_A, L0_attn_dt_A, L0_attn_B_w, L0_attn_B_b, L0_attn_C_w, L0_attn_C_b, L0_attn_D_w, L0_attn_D_b, L0_attn_conv_w, L0_attn_conv_b, L0_attn_gate_w, L0_attn_gate_b, L0_attn_ln_in_g, L0_attn_ln_in_b, L0_attn_ln_st_g, L0_attn_ln_st_b, L0_ffn_ln_gamma, L0_ffn_ln_beta, L0_ffn_abel_w, L0_ffn_abel_b, L0_ffn_moe_gate_w, L0_ffn_moe_gate_b, L0_ffn_ew1, L0_ffn_eb1, L0_ffn_ew2, L0_ffn_eb2, L0_ffn_gens, L0_ffn_gc_w, L0_ffn_gc_b):

    def _L0_attn_ref(x, A, dt_A, B_w, B_b, C_w, C_b, D_w, D_b, conv_w, conv_b, gate_w, gate_b, ln_in_g, ln_in_b, ln_st_g, ln_st_b):
        import jax, jax.numpy as jnp
        import numpy as np
        from jax.scipy.linalg import expm
        EPS = 1e-05

        def _layernorm(x, g, b):
            m = x.mean(-1, keepdims=True)
            v = ((x - m) ** 2).mean(-1, keepdims=True)
            return (x - m) / jnp.sqrt(v + EPS) * g + b
        Bt, T, H = x.shape
        K = conv_w.shape[-1]
        pad = K // 2
        x_norm = _layernorm(x, ln_in_g, ln_in_b)
        xc = jnp.transpose(x_norm, (0, 2, 1))
        xc = jax.lax.conv_general_dilated(xc, conv_w, window_strides=(1,), padding=[(pad, pad)], dimension_numbers=('NCH', 'OIH', 'NCH'), feature_group_count=H)
        xc = xc + conv_b[None, :, None]
        x_norm = x_norm + jnp.transpose(xc, (0, 2, 1))
        gate_all = x_norm @ gate_w.T + gate_b
        gate, input_gate = (gate_all[..., :H], gate_all[..., H:])
        gate = jax.nn.sigmoid(gate)
        Bm = x_norm * jax.nn.sigmoid(input_gate) @ B_w.T + B_b
        Cm = x_norm @ C_w.T + C_b
        A_bar = expm(dt_A * A)

        def step(state, bc):
            b_t, c_t = bc
            s = state @ A_bar + b_t
            s = _layernorm(s, ln_st_g, ln_st_b)
            return (s, c_t * s)
        state0 = jnp.zeros((Bt, A.shape[0]), x.dtype)
        _, ys = jax.lax.scan(step, state0, (jnp.transpose(Bm, (1, 0, 2)), jnp.transpose(Cm, (1, 0, 2))))
        ssm = jnp.transpose(ys, (1, 0, 2))
        ssm = ssm @ D_w.T + D_b
        return ssm * gate

    def _L0_ffn_ref(x, ln_gamma, ln_beta, abel_w, abel_b, moe_gate_w, moe_gate_b, ew1, eb1, ew2, eb2, gens, gc_w, gc_b):
        import jax, jax.numpy as jnp
        import numpy as np
        from jax.scipy.linalg import expm
        B, S, D, E, K, NROT = (2, 256, 128, 8, 2, 3)
        EPS = 1e-05

        def _gelu(x):
            return jax.nn.gelu(x, approximate=False)

        def _forward(x, ln_gamma, ln_beta, abel_w, abel_b, moe_gate_w, moe_gate_b, ew1, eb1, ew2, eb2, gens, gc_w, gc_b):
            residual = x
            mu = jnp.mean(x, axis=-1, keepdims=True)
            var = jnp.mean((x - mu) ** 2, axis=-1, keepdims=True)
            xn = (x - mu) * jax.lax.rsqrt(var + EPS) * ln_gamma + ln_beta
            abel_out = _gelu(xn @ abel_w + abel_b)
            logits = xn @ moe_gate_w + moe_gate_b
            topw, topi = jax.lax.top_k(logits, K)
            topw = jax.nn.softmax(topw, axis=-1)
            w_dense = jnp.sum(jax.nn.one_hot(topi, E, dtype=xn.dtype) * topw[..., None], axis=-2)
            h = _gelu(jnp.einsum('bsd,edh->ebsh', xn, ew1) + eb1[:, None, None, :])
            eo = jnp.einsum('ebsh,ehd->ebsd', h, ew2) + eb2[:, None, None, :]
            moe_out = jnp.einsum('ebsd,bse->bsd', eo, w_dense)
            for i in range(NROT):
                moe_out = moe_out @ expm(gens[i])
            combined = jnp.concatenate([abel_out, moe_out], axis=-1)
            gate = jax.nn.sigmoid(combined @ gc_w + gc_b)
            mixed = abel_out * (1.0 - gate) + moe_out * gate
            return residual + mixed
        return _forward(x, ln_gamma, ln_beta, abel_w, abel_b, moe_gate_w, moe_gate_b, ew1, eb1, ew2, eb2, gens, gc_w, gc_b)
    x = L0_attn_x
    xn = _layernorm(x, axis=-1)
    s = _L0_attn_ref(xn, L0_attn_A, L0_attn_dt_A, L0_attn_B_w, L0_attn_B_b, L0_attn_C_w, L0_attn_C_b, L0_attn_D_w, L0_attn_D_b, L0_attn_conv_w, L0_attn_conv_b, L0_attn_gate_w, L0_attn_gate_b, L0_attn_ln_in_g, L0_attn_ln_in_b, L0_attn_ln_st_g, L0_attn_ln_st_b)
    g = _silu(_L0_ffn_ref(xn, L0_ffn_ln_gamma, L0_ffn_ln_beta, L0_ffn_abel_w, L0_ffn_abel_b, L0_ffn_moe_gate_w, L0_ffn_moe_gate_b, L0_ffn_ew1, L0_ffn_eb1, L0_ffn_ew2, L0_ffn_eb2, L0_ffn_gens, L0_ffn_gc_w, L0_ffn_gc_b))
    x = x + s * g
    return x

_drawn_inputs = setup_inputs


def setup_inputs(seed=0):
    import zlib

    import numpy as np

    out = dict(_drawn_inputs(seed))
    spreads = {'L0_attn_B_b': (0.0, 0.53),
     'L0_attn_C_b': (0.0, 0.676),
     'L0_attn_D_b': (0.0, 0.269),
     'L0_attn_conv_b': (0.0, 0.8),
     'L0_attn_gate_b': (0.0, 0.8),
     'L0_attn_ln_in_g': (1.0, 0.6),
     'L0_attn_ln_in_b': (0.0, 0.8),
     'L0_attn_ln_st_g': (1.0, 0.6),
     'L0_attn_ln_st_b': (0.0, 0.362)}
    factors = {'L0_attn_A': 8.0,
     'L0_attn_B_w': 8.0,
     'L0_attn_C_w': 3.028,
     'L0_attn_conv_w': 8.0,
     'L0_attn_gate_w': 8.0,
     'L0_ffn_ln_gamma': 8.0,
     'L0_ffn_ln_beta': 8.0,
     'L0_ffn_abel_w': 8.0,
     'L0_ffn_abel_b': 37.479,
     'L0_ffn_moe_gate_w': 8.0,
     'L0_ffn_moe_gate_b': 8.0,
     'L0_ffn_ew1': 8.0,
     'L0_ffn_eb1': 8.0,
     'L0_ffn_ew2': 8.0,
     'L0_ffn_eb2': 60.857,
     'L0_ffn_gens': 8.0,
     'L0_ffn_gc_w': 8.0}
    for name, (base, spread) in spreads.items():
        noise = np.random.default_rng([zlib.crc32(name.encode()), seed]).standard_normal(out[name].shape)
        drawn = base * np.exp(spread * noise) if base else spread * noise
        out[name] = jnp.asarray(drawn.astype(out[name].dtype))
    for name, factor in factors.items():
        out[name] = (out[name] * factor).astype(out[name].dtype)
    return out
```

```python
from contextlib import ExitStack

import concourse.bass as bass
from concourse import mybir

ALU = mybir.AluOpType
ACT = mybir.ActivationFunctionType
AX_X = mybir.AxisListType.X
F32 = mybir.dt.float32
U32 = mybir.dt.uint32

P = 128
EPS = 1e-5
SCALE_STEPS = 5
TAYLOR = 10
UNROLL = 8
RENORM = 4
SEG = 16
ROUNDS = 7
TOLERANCE = 3e-5
ds = bass.ds


def build(nc, I, out):
    NB, T, H = I["L0_attn_x"].shape
    S = I["L0_attn_A"].shape[0]
    E, _, F = I["L0_ffn_ew1"].shape
    NROT = I["L0_ffn_gens"].shape[0]
    K = F // P
    SUB = T // P
    NS = NB * SUB
    SX = S + 1
    L = T // SEG
    assert NB * SEG == P and L % UNROLL == 0 and UNROLL % RENORM == 0 and S == 64
    assert H == P and T % P == 0 and F % P == 0 and NROT + 1 == 4 and SUB == 4 and E == 8

    with ExitStack() as ctx:
        sems = {}

        def sem(name):
            if name not in sems:
                sems[name] = ctx.enter_context(nc.semaphore(name))
            return sems[name]

        def sb(name, shape, dt=F32):
            return ctx.enter_context(nc.sbuf_tensor(name, shape, dt))

        banks = [ctx.enter_context(nc.psum_tensor(f"bank{i}", [P, 512], F32)) for i in range(8)]

        ident = sb("ident", [P, P])
        ones = sb("ones", [P, P])
        shift = sb("shift", [P, P])
        first_col = sb("first_col", [P, 1])
        start_add = sb("start_add", [P, SX])
        center = sb("center", [S, S])
        iota_i = sb("iota_i", [P, SUB * E], mybir.dt.int32)
        iota_f = sb("iota_f", [P, SUB, E])
        eps_col = sb("eps_col", [P, 1])
        junk_col = sb("junk_col", [P, 1])
        cols = sb("cols", [P, 24])
        names = ["ln_in_g", "ln_in_b", "conv_b", "gate_b_in", "ln_gamma", "ln_beta", "B_b", "ln_st_g", "ln_st_b"]
        col = {n: cols[:, i:i + 1] for i, n in enumerate(names)}
        conv_w = cols[:, 10:13]
        conv_w1 = cols[:, 13:14]
        dt_col = cols[0:S, 14:15]
        row_mean = cols[:, 18:19]
        row_mean_b = cols[:, 19:20]
        half_gc_b = cols[:, 20:21]
        eb1_col = sb("eb1_col", [P, E, K])
        eb1_rows = sb("eb1_rows", [E * K, P])
        rows = sb("rows", [1, 5 * P + E + 2 + 3 * S])
        abel_b_row, D_b_row, gate_b_row = (rows[:, i * P:(i + 1) * P] for i in range(3))
        gc_w_row = rows[:, 3 * P:5 * P]
        mgb_row = rows[:, 5 * P:5 * P + E]
        gc_b_row = rows[:, 5 * P + E:5 * P + E + 1]
        dt_row = rows[:, 5 * P + E + 1:5 * P + E + 2]
        st_rows = rows[:, 5 * P + E + 2:5 * P + E + 2 + 3 * S]
        bcast = sb("bcast", [P, 2 * P + E + 1 + 3 * S])
        gc_w_all = bcast[:, 0:2 * P]
        mgb_all = bcast[:, 2 * P:2 * P + E]
        C_b_all, st_g_all, st_b_all = (bcast[:, 2 * P + E + 1 + i * S:2 * P + E + 1 + (i + 1) * S] for i in range(3))
        bias_src = sb("bias_src", [S, 2, P])
        bias_all = sb("bias_all", [P, 3, S])

        gate_w = sb("gate_w", [P, 2, P])
        gate_wT = sb("gate_wT", [P, 2, P])
        BC_w = sb("BC_w", [S, 2, P])
        BC_wT = sb("BC_wT", [P, 2, S])
        D_w = sb("D_w", [P, 2, S])
        D_wT = sb("D_wT", [P, 2, P])
        abel_w = sb("abel_w", [P, P])
        router_w = sb("router_w", [P, E])
        ew1 = sb("ew1", [P, E, F])
        ew2 = sb("ew2", [P, E, K, P])
        eb2 = sb("eb2", [E, P])
        eb2T = sb("eb2T", [P, E])
        eb2r = sb("eb2r", [E, P])
        Mx = sb("Mx", [S, SX])
        pick = sb("pick", [S, 2, P])
        Mrep = sb("Mrep", [P, 2, SX])
        AbC = sb("AbC", [S, S])
        R23 = sb("R23", [P, P])
        Rall = sb("Rall", [P, P])

        X = sb("X", [P, NS, P])
        st = sb("st", [P, NS, 6])
        lnv = sb("lnv", [P, 8, NS])
        xpad = sb("xpad", [P, L + 2, P])
        xaT = sb("xaT", [P, NB, T])
        xfT = sb("xfT", [P, NB, T])
        gi = sb("gi", [P, NB, T])
        Dv = sb("Dv", [P, L, SX])
        Wst = sb("Wst", [P, L, SX])
        Rho = sb("Rho", [P, L + 1])
        gC = sb("gC", [P, L, S])
        bC = sb("bC", [P, L, S])
        CL = gi[:, 4:8, :].rearrange("p a b -> p (a b)").rearrange("p (k n) -> p k n", n=S)

        ew2T = xaT[:, 0:4, :].rearrange("p a b -> p (a b)").rearrange("p (e k f) -> p e k f", e=E, k=K)
        ex = xfT[:, :, :].rearrange("p a b -> p (a b)")
        XE = ex[:, 0:512].rearrange("p (m n) -> p m n", m=4)
        XT = ex[:, 512:1024].rearrange("p (m n) -> p m n", m=4)
        EX = ex[:, 1024:1536].rearrange("p (m n) -> p m n", m=4)
        ET = ex[:, 1536:2048].rearrange("p (m n) -> p m n", m=4)
        gens = ex[:, 2048:2432].rearrange("p (m n) -> p m n", m=3)
        A_in = ex[0:S, 2432:2432 + S]

        zbuf = sb("zbuf", [P, 2, SUB, P])

        ident4 = ident[:, :].unsqueeze(1).broadcast_to([P, 4, P])

        N_W = 30
        with nc.Block() as setup:
            @setup.sync
            def _(sp):
                xr = I["L0_attn_x"].rearrange("b (q k) h -> (b q) k h", k=L)

                def load(dst, src):
                    sp.dma_start(dst, src).then_inc(sem("weights_loaded"), 16)

                def as_col(name):
                    return I[name].rearrange("(p a) -> p a", a=1)

                load(gens, I["L0_ffn_gens"].rearrange("m p n -> p m n"))
                load(A_in, I["L0_attn_A"])
                load(dt_row, I["L0_attn_dt_A"])
                load(gate_w[:, :, :], I["L0_attn_gate_w"].rearrange("(j p) h -> p j h", p=P))
                load(BC_w[:, 0, :], I["L0_attn_B_w"])
                load(BC_w[:, 1, :], I["L0_attn_C_w"])
                load(D_w[:, 0, :], I["L0_attn_D_w"])
                load(D_w[:, 1, :], I["L0_attn_D_w"])
                load(col["ln_in_g"], as_col("L0_attn_ln_in_g"))
                load(col["ln_in_b"], as_col("L0_attn_ln_in_b"))
                load(col["conv_b"], as_col("L0_attn_conv_b"))
                load(conv_w, I["L0_attn_conv_w"].rearrange("h a k -> h (a k)"))
                load(col["gate_b_in"], I["L0_attn_gate_b"][P:2 * P].rearrange("(p a) -> p a", a=1))
                load(gate_b_row, I["L0_attn_gate_b"][0:P].rearrange("(a p) -> a p", a=1))
                load(col["ln_gamma"], as_col("L0_ffn_ln_gamma"))
                load(col["ln_beta"], as_col("L0_ffn_ln_beta"))
                for i, name in enumerate(("L0_attn_C_b", "L0_attn_ln_st_g", "L0_attn_ln_st_b")):
                    load(st_rows[:, i * S:(i + 1) * S], I[name].rearrange("(a p) -> a p", a=1))
                load(col["B_b"][0:S], as_col("L0_attn_B_b"))
                load(col["ln_st_g"][0:S], as_col("L0_attn_ln_st_g"))
                load(col["ln_st_b"][0:S], as_col("L0_attn_ln_st_b"))
                load(eb2[:, :], I["L0_ffn_eb2"])
                load(eb1_rows[:, :], I["L0_ffn_eb1"].rearrange("e (k p) -> (e k) p", p=P))
                load(ew2[:, :, :, :], I["L0_ffn_ew2"].rearrange("e (k p) d -> p e k d", p=P))
                load(abel_b_row, I["L0_ffn_abel_b"].rearrange("(a p) -> a p", a=1))
                load(D_b_row, I["L0_attn_D_b"].rearrange("(a p) -> a p", a=1))
                load(gc_w_row, I["L0_ffn_gc_w"].rearrange("p a -> a p"))
                load(mgb_row, I["L0_ffn_moe_gate_b"].rearrange("(a p) -> a p", a=1))
                load(gc_b_row, I["L0_ffn_gc_b"].rearrange("(a p) -> a p", a=1))
                for b in range(NB):
                    sp.dma_start(X[:, b * SUB:(b + 1) * SUB, :], xr[:, b * SUB:(b + 1) * SUB, :]).then_inc(sem("x_loaded"), 16)
                sp.dma_start(abel_w[:, :], I["L0_ffn_abel_w"]).then_inc(sem("ffn_loaded"), 16)
                sp.dma_start(router_w[:, :], I["L0_ffn_moe_gate_w"]).then_inc(sem("ffn_loaded"), 16)
                sp.dma_start(ew1[:, :, :], I["L0_ffn_ew1"].rearrange("e d f -> d e f")).then_inc(sem("ffn_loaded"), 16)

            @setup.gpsimd
            def _(pool):
                pool.memset(ident[:, :], 0.0).then_inc(sem("ident_zero"), 1)
                pool.wait_ge(sem("ident_zero"), 1)
                pool.affine_select(out=ident[:, :], in_=ident[:, :], compare_op=ALU.not_equal, fill=1.0, base=0,
                                   pattern=[[-1, P]], channel_multiplier=1).then_inc(sem("ident_ready"), 1)
                pool.memset(ones[:, :], 1.0).then_inc(sem("ones_ready"), 1)
                pool.memset(shift[:, :], 0.0).then_inc(sem("shift_zero"), 1)
                pool.wait_ge(sem("shift_zero"), 1)
                pool.affine_select(out=shift[:, :], in_=shift[:, :], compare_op=ALU.not_equal, fill=1.0, base=1,
                                   pattern=[[-1, P]], channel_multiplier=1).then_inc(sem("shift_ones"), 1)
                pool.wait_ge(sem("shift_ones"), 1)
                pool.memset(shift[:, 0:P:SEG], 0.0).then_inc(sem("const_ready"), 1)
                pool.memset(eps_col[:, :], EPS).then_inc(sem("const_ready"), 1)
                pool.memset(XE[:, 3, :], 0.0).then_inc(sem("expm_zero"), 1)
                pool.memset(XT[:, 3, :], 0.0).then_inc(sem("expm_zero"), 1)
                pool.iota(iota_i[:, :], pattern=[[0, SUB], [1, E]], base=0, channel_multiplier=0).then_inc(sem("iota_ready"), 1)
                pool.wait_ge(sem("iota_ready"), 1)
                pool.tensor_copy(iota_f[:, :, :], iota_i[:, :].rearrange("p (s e) -> p s e", s=SUB)).then_inc(sem("const_ready"), 1)

            @setup.tensor
            def _(pe):
                pe.wait_ge(sem("weights_loaded"), 16 * N_W)
                pe.wait_ge(sem("ident_ready"), 1)
                pe.wait_ge(sem("ones_ready"), 1)
                for m in range(NROT):
                    pe.transpose(banks[1][:, m * P:(m + 1) * P], gens[:, m, :], ident[:, :])
                pe.transpose(banks[1][0:S, 384:384 + S], A_in, ident[0:S, 0:S])
                pe.matmul(banks[2][0:S, 0:1], ones[0:1, 0:S], dt_row, start=True, stop=True).then_inc(sem("expm_in"), 1)
                for j in range(2):
                    pe.transpose(banks[0][:, j * P:(j + 1) * P], gate_w[:, j, :], ident[:, :])
                for j in range(2):
                    pe.transpose(banks[0][:, 2 * P + j * S:2 * P + (j + 1) * S], BC_w[:, j, :], ident[0:S, 0:S])
                pe.transpose(banks[0][:, 384:512], D_w[:, :, :].rearrange("p j n -> p (j n)"), ident[:, :]).then_inc(sem("small_T"), 1)
                pe.transpose(banks[7][:, 464:464 + E], eb2[:, :], ident[0:E, 0:E])
                pe.transpose(banks[7][:, 480:480 + E * K], eb1_rows[:, :], ident[0:E * K, 0:E * K])
                pe.matmul(banks[7][:, 0:2 * P], ones[0:1, :], gc_w_row, start=True, stop=True)
                pe.matmul(banks[7][:, 2 * P:2 * P + E], ones[0:1, :], mgb_row, start=True, stop=True)
                pe.matmul(banks[7][:, 2 * P + E:2 * P + E + 1], ones[0:1, :], gc_b_row, start=True, stop=True)
                pe.matmul(banks[7][:, 2 * P + E + 1:2 * P + E + 1 + 3 * S], ones[0:1, :], st_rows, start=True, stop=True).then_inc(sem("rows_all"), 1)
                for e in range(E):
                    for k in range(K):
                        q = e * K + k
                        t = pe.transpose(banks[3 + q // 4][:, (q % 4) * P:(q % 4 + 1) * P], ew2[:, e, k, :], ident[:, :])
                    if e % 2:
                        t.then_inc(sem("ew2_T"), 1)
                for k in range(TAYLOR - 1, 0, -1):
                    pe.wait_ge(sem("taylor"), TAYLOR - k)
                    for m in range(4):
                        t = pe.matmul(banks[1][:, m * P:(m + 1) * P], XT[:, m, :], EX[:, m, :], start=True, stop=True)
                    t.then_inc(sem("taylor_product"), 1)
                pe.wait_ge(sem("taylor"), TAYLOR)
                for m in range(4):
                    t = pe.transpose(banks[2][:, m * P:(m + 1) * P], EX[:, m, :], ident[:, :])
                t.then_inc(sem("exp_T"), 1)
                for k in range(SCALE_STEPS):
                    if k:
                        pe.wait_ge(sem("squared"), k)
                    pe.wait_ge(sem("squared_T"), k + 1)
                    for m in range(4):
                        t = pe.matmul(banks[1][:, m * P:(m + 1) * P], ET[:, m, :], EX[:, m, :], start=True, stop=True)
                    t.then_inc(sem("square"), 1)
                    for m in range(4):
                        t = pe.matmul(banks[2][:, m * P:(m + 1) * P], EX[:, m, :], ET[:, m, :], start=True, stop=True)
                    t.then_inc(sem("square_T"), 1)
                pe.wait_ge(sem("squared"), SCALE_STEPS)
                pe.wait_ge(sem("squared_T"), SCALE_STEPS + 1)
                pe.matmul(banks[1][:, 0:P], ET[:, 1, :], EX[:, 2, :], start=True, stop=True).then_inc(sem("rot23"), 1)
                pe.wait_ge(sem("rot23_copied"), 1)
                pe.matmul(banks[1][:, P:2 * P], ET[:, 0, :], R23[:, :], start=True, stop=True).then_inc(sem("rot"), 1)
                pe.wait_ge(sem("rot_copied"), 1)
                pe.wait_ge(sem("ew2T_copied"), 4)
                for q in range(E * K):
                    t = pe.matmul(banks[3 + q // 4][:, (q % 4) * P:(q % 4 + 1) * P], ew2T[:, q // K, q % K, :], Rall[:, :], start=True, stop=True)
                    if q % 4 == 3:
                        t.then_inc(sem("ew2_rotated"), 1)
                pe.wait_ge(sem("rows_copied"), 1)
                pe.matmul(banks[0][0:E, 0:P], eb2T[:, :], Rall[:, :], start=True, stop=True).then_inc(sem("eb2_rotated"), 1)
                pe.wait_ge(sem("scan_matrix"), 2)
                for i, m in enumerate((center, AbC)):
                    pe.matmul(banks[7][:, i * S:(i + 1) * S], bias_src[:, i, :], m[:, :], start=True, stop=True)
                for c in range(2):
                    t = pe.matmul(banks[7][:, 2 * S + c * SX:2 * S + (c + 1) * SX], pick[:, c, :], Mx[:, :], start=True, stop=True)
                t.then_inc(sem("scan_bias"), 1)

            @setup.scalar
            def _(act):
                act.wait_ge(sem("small_T"), 1)
                act.copy(gate_wT[:, :, :], banks[0][:, 0:2 * P].rearrange("p (j h) -> p j h", j=2))
                act.copy(BC_wT[:, :, :], banks[0][:, 2 * P:2 * P + 2 * S].rearrange("p (j h) -> p j h", j=2)).then_inc(sem("BC_T"), 1)
                act.wait_ge(sem("D_zero"), 1)
                act.copy(D_wT[0:S, 0, :], banks[0][0:S, 384:512])
                act.copy(D_wT[S:P, 1, :], banks[0][S:P, 384:512]).then_inc(sem("small_copied"), 1)
                act.wait_ge(sem("rows_all"), 1)
                act.copy(bcast[:, :], banks[7][:, 0:2 * P + E + 1 + 3 * S]).then_inc(sem("rows_copied_a"), 1)
                act.copy(eb1_col[:, :, :], banks[7][:, 480:480 + E * K].rearrange("p (e k) -> p e k", e=E))
                act.copy(eb2T[:, :], banks[7][:, 464:464 + E]).then_inc(sem("rows_copied"), 1)
                act.wait_ge(sem("rows_copied_a"), 1)
                act.mul(half_gc_b, bcast[:, 2 * P + E:2 * P + E + 1], 0.5).then_inc(sem("small_copied"), 1)
                for q in range(4):
                    act.wait_ge(sem("ew2_T"), q + 1)
                    act.copy(ew2T[:, 2 * q:2 * q + 2, :, :], banks[3 + q][:, :].rearrange("p (e k f) -> p e k f", e=2, k=K)).then_inc(sem("ew2T_copied"), 1)
                for k in range(SCALE_STEPS + 1):
                    if k == 0:
                        act.wait_ge(sem("exp_T"), 1)
                    else:
                        act.wait_ge(sem("square_T"), k)
                    act.copy(ET[:, :, :], banks[2][:, :].rearrange("p (m n) -> p m n", m=4)).then_inc(sem("squared_T"), 1)
                for q in range(4):
                    act.wait_ge(sem("ew2_rotated"), q + 1)
                    act.copy(ew2[:, 2 * q:2 * q + 2, :, :], banks[3 + q][:, :].rearrange("p (e k f) -> p e k f", e=2, k=K)).then_inc(sem("ew2r_ready"), 1)
                act.wait_ge(sem("eb2_rotated"), 1)
                act.copy(eb2r[:, :], banks[0][0:E, 0:P]).then_inc(sem("ew2r_ready"), 1)

            @setup.vector
            def _(dve):
                dve.memset(D_wT[:, :, :], 0.0).then_inc(sem("D_zero"), 1)
                dve.memset(Dv[:, :, S:SX], (S * EPS) ** 0.5)
                dve.memset(start_add[:, :], 0.0).then_inc(sem("start_zero"), 1)
                dve.wait_ge(sem("ident_ready"), 1)
                dve.tensor_reduce(first_col[:, :], ident[:, 0:P:SEG], AX_X, ALU.add).then_inc(sem("first_col"), 1)
                dve.wait_ge(sem("first_col"), 1)
                dve.wait_ge(sem("start_zero"), 1)
                dve.tensor_scalar(start_add[:, S:SX], first_col[:, :], float(S) ** 0.5, None, ALU.mult)
                for c in range(2):
                    dve.tensor_copy(pick[:, c, :].rearrange("k (a i) -> k a i", a=4),
                                    ident[0:S, 32 * c:32 * c + 32].unsqueeze(1).broadcast_to([S, 4, 32]))
                dve.tensor_scalar(center[:, :], ident[0:S, 0:S], -1.0 / S, None, ALU.add).then_inc(sem("center"), 1)
                dve.wait_ge(sem("weights_loaded"), 16 * N_W)
                dve.tensor_scalar(conv_w1, conv_w[:, 1:2], 1.0, None, ALU.add).then_inc(sem("center"), 1)
                dve.wait_ge(sem("ones_ready"), 1)
                dve.tensor_scalar(bias_src[:, 0, :], ones[0:S, :], col["B_b"][0:S], None, ALU.mult)
                dve.tensor_scalar(bias_src[:, 1, :], ones[0:S, :], col["ln_st_b"][0:S], None, ALU.mult)
                dve.wait_ge(sem("expm_in"), 1)
                dve.wait_ge(sem("expm_zero"), 2)
                dve.tensor_copy(dt_col, banks[2][0:S, 0:1]).then_inc(sem("dt"), 1)
                half = 0.5 ** SCALE_STEPS
                dve.tensor_scalar(XE[:, 0:3, :], gens, half, None, ALU.mult)
                dve.tensor_scalar(XT[:, 0:3, :], banks[1][:, 0:384].rearrange("p (m n) -> p m n", m=3), half, None, ALU.mult)
                dve.wait_ge(sem("dt"), 1)
                dve.tensor_scalar(XE[0:S, 3, 0:S], A_in, dt_col, half, ALU.mult, ALU.mult)
                dve.tensor_scalar(XT[0:S, 3, 0:S], banks[1][0:S, 384:384 + S], dt_col, half, ALU.mult, ALU.mult).then_inc(sem("expm_arg"), 1)
                dve.wait_ge(sem("expm_arg"), 1)
                dve.scalar_tensor_tensor(out=EX, in0=XE, scalar=1.0 / TAYLOR, in1=ident4, op0=ALU.mult, op1=ALU.add).then_inc(sem("taylor"), 1)
                for k in range(TAYLOR - 1, 0, -1):
                    dve.wait_ge(sem("taylor_product"), TAYLOR - k)
                    dve.scalar_tensor_tensor(out=EX, in0=banks[1][:, :].rearrange("p (m n) -> p m n", m=4), scalar=1.0 / k, in1=ident4,
                                             op0=ALU.mult, op1=ALU.add).then_inc(sem("taylor"), 1)
                for k in range(SCALE_STEPS):
                    dve.wait_ge(sem("square_T"), k + 1)
                    dve.tensor_copy(EX, banks[1][:, :].rearrange("p (m n) -> p m n", m=4)).then_inc(sem("squared"), 1)
                dve.wait_ge(sem("squared"), SCALE_STEPS)
                dve.tensor_reduce(row_mean[0:S], EX[0:S, 3, 0:S], AX_X, ALU.add).then_inc(sem("row_sum"), 1)
                dve.wait_ge(sem("row_sum"), 1)
                dve.tensor_scalar(row_mean[0:S], row_mean[0:S], 1.0 / S, None, ALU.mult).then_inc(sem("row_sum"), 1)
                dve.memset(Mx[:, :], 0.0).then_inc(sem("m_zero"), 1)
                dve.wait_ge(sem("row_sum"), 2)
                dve.tensor_scalar(AbC[:, :], EX[0:S, 3, 0:S], row_mean[0:S], None, ALU.subtract).then_inc(sem("scan_matrix"), 1)
                dve.wait_ge(sem("m_zero"), 1)
                dve.wait_ge(sem("scan_matrix"), 1)
                dve.tensor_scalar(Mx[:, 0:S], AbC[:, :], col["ln_st_g"][0:S], None, ALU.mult).then_inc(sem("scan_matrix"), 1)
                dve.wait_ge(sem("rot23"), 1)
                dve.tensor_copy(R23[:, :], banks[1][:, 0:P]).then_inc(sem("rot23_copied"), 1)
                dve.wait_ge(sem("rot"), 1)
                dve.tensor_copy(Rall[:, :], banks[1][:, P:2 * P]).then_inc(sem("rot_copied"), 1)
                dve.wait_ge(sem("BC_T"), 1)
                dve.tensor_reduce(row_mean_b, BC_wT[:, 0, :], AX_X, ALU.add).then_inc(sem("row_sum_b"), 1)
                dve.wait_ge(sem("row_sum_b"), 1)
                dve.tensor_scalar(row_mean_b, row_mean_b, 1.0 / S, None, ALU.mult).then_inc(sem("row_sum_b"), 1)
                dve.wait_ge(sem("row_sum_b"), 2)
                dve.tensor_scalar(BC_wT[:, 0, :], BC_wT[:, 0, :], row_mean_b, None, ALU.subtract)
                dve.wait_ge(sem("scan_bias"), 1)
                dve.tensor_copy(Mrep[:, :, :], banks[7][:, 2 * S:2 * S + 2 * SX].rearrange("p (c n) -> p c n", c=2))
                dve.tensor_copy(bias_all[:, 0:2, :], banks[7][:, 0:2 * S].rearrange("p (c n) -> p c n", c=2)).then_inc(sem("bias_copied"), 1)
                dve.wait_ge(sem("bias_copied"), 1)
                dve.tensor_tensor(bias_all[:, 2, :], bias_all[:, 0, :], bias_all[:, 1, :], ALU.add)
                dve.wait_ge(sem("x_loaded"), 16 * NB)
                for s in range(NS):
                    t = dve.bn_stats(st[:, s, :], X[:, s, :])
                t.then_inc(sem("stats"), 1)


        mean, var, r1, nm1, rz, nmz, tmp, tmp2 = (lnv[:, i, :] for i in range(8))
        with nc.Block() as block:

            @block.vector
            def _(dve):
                dve.tensor_tensor(mean, st[:, :, 1], st[:, :, 4], ALU.add)
                dve.tensor_tensor(tmp, st[:, :, 1], st[:, :, 4], ALU.subtract)
                dve.tensor_tensor(var, st[:, :, 2], st[:, :, 5], ALU.add).then_inc(sem("ln_a"), 1)
                dve.wait_ge(sem("ln_a"), 1)
                dve.tensor_tensor(tmp2, tmp, tmp, ALU.mult)
                dve.tensor_scalar(mean, mean, 0.5, None, ALU.mult)
                dve.tensor_scalar(var, var, 1.0 / H, None, ALU.mult).then_inc(sem("ln_a"), 1)
                dve.wait_ge(sem("ln_a"), 2)
                dve.scalar_tensor_tensor(out=var, in0=tmp2, scalar=0.25, in1=var, op0=ALU.mult, op1=ALU.add).then_inc(sem("var_ready"), 1)
                dve.wait_ge(sem("std_ready"), 1)
                dve.reciprocal(r1, tmp).then_inc(sem("ln_a"), 1)
                dve.wait_ge(sem("ln_a"), 3)
                dve.tensor_tensor(tmp2, r1, r1, ALU.mult).then_inc(sem("ln_a"), 1)
                dve.wait_ge(sem("ln_a"), 4)
                dve.tensor_tensor(tmp2, tmp2, var, ALU.mult).then_inc(sem("var_ready"), 1)
                dve.scalar_tensor_tensor(out=nm1, in0=mean, scalar=-1.0, in1=r1, op0=ALU.mult, op1=ALU.mult)
                dve.wait_ge(sem("std_ready"), 2)
                dve.reciprocal(rz, tmp).then_inc(sem("ln_a"), 1)
                dve.wait_ge(sem("ln_a"), 5)
                dve.tensor_tensor(rz, rz, r1, ALU.mult).then_inc(sem("ln_a"), 1)
                dve.wait_ge(sem("ln_a"), 6)
                dve.scalar_tensor_tensor(out=nmz, in0=mean, scalar=-1.0, in1=rz, op0=ALU.mult, op1=ALU.mult).then_inc(sem("ln_a"), 1)
                dve.wait_ge(sem("ln_a"), 7)
                with dve.Fori(0, NB // 2) as i:
                    for u in range(2):
                        n = i * 2 + u
                        dve.wait_ge(sem("zT_free"), n + 1)
                        for s in range(SUB):
                            q = n * SUB + s
                            t = dve.tensor_scalar(zbuf[:, u, s, :], X[:, ds(q, 1), :], rz[:, ds(q, 1)], nmz[:, ds(q, 1)], ALU.mult, ALU.add)
                        t.then_inc(sem("z_ready"), 1)
                dve.wait_ge(sem("edges"), 4)
                with dve.Fori(0, NB) as n:
                    o = xaT[:, ds(n, 1), :].squeeze(1).rearrange("p (k n) -> p k n", k=SUB)
                    dve.tensor_scalar(o, xpad[:, ds(n * SUB + 1, SUB), :], conv_w1, col["conv_b"], ALU.mult, ALU.add).then_inc(sem("conv0"), 1)
                    dve.wait_ge(sem("conv0"), n + 1)
                    dve.scalar_tensor_tensor(out=o, in0=xpad[:, ds(n * SUB, SUB), :], scalar=conv_w[:, 0:1], in1=o, op0=ALU.mult, op1=ALU.add).then_inc(sem("conv1"), 1)
                    dve.wait_ge(sem("conv1"), n + 1)
                    dve.scalar_tensor_tensor(out=o, in0=xpad[:, ds(n * SUB + 2, SUB), :], scalar=conv_w[:, 2:3], in1=o, op0=ALU.mult, op1=ALU.add).then_inc(sem("conv"), 1)
                dve.wait_ge(sem("conv"), NB)
                with dve.Fori(0, NB) as n:
                    dve.wait_ge(sem("gate_free"), n + 3)
                    dve.tensor_tensor(gi[:, ds(n, 1), :], xaT[:, ds(n, 1), :], gi[:, ds(n, 1), :], ALU.mult).then_inc(sem("gated"), 1)
                for g in range(4):
                    dve.wait_ge(sem("B_proj"), g + 1)
                    t = dve.tensor_tensor(Dv[:, g * 8:g * 8 + 8, 0:S], banks[6 + g % 2][:, :].rearrange("p (k n) -> p k n", n=S),
                                          bias_all[:, 2, :].unsqueeze(1).broadcast_to([P, 8, S]), ALU.add).then_inc(sem("B_copied"), 1)
                dve.wait_ge(sem("B_copied"), 1)
                dve.tensor_scalar(bias_all[:, 1, :], bias_all[:, 1, :], first_col[:, :], None, ALU.mult).then_inc(sem("first_bias"), 1)
                dve.wait_ge(sem("first_bias"), 1)
                dve.tensor_tensor(Dv[:, 0, 0:S], Dv[:, 0, 0:S], bias_all[:, 1, :], ALU.subtract)
                for g in range(4):
                    dve.wait_ge(sem("C_proj"), g + 1)
                    dve.tensor_tensor(CL[:, g * 8:g * 8 + 8, :], banks[4 + g % 2][:, :].rearrange("p (k n) -> p k n", n=S),
                                      C_b_all.unsqueeze(1).broadcast_to([P, 8, S]), ALU.add).then_inc(sem("C_copied"), 1)

            @block.gpsimd
            def _(pool):
                pool.wait_ge(sem("affine"), NB)
                pool.tensor_copy(xpad[:, 0, 1:P], xpad[:, L, 0:P - 1]).then_inc(sem("edges"), 1)
                pool.wait_ge(sem("edges"), 1)
                pool.memset(xpad[:, 0, 0:P:SEG], 0.0).then_inc(sem("edges"), 1)
                pool.tensor_copy(xpad[:, L + 1, 0:P - 1], xpad[:, 1, 1:P]).then_inc(sem("edges"), 1)
                pool.wait_ge(sem("edges"), 3)
                pool.memset(xpad[:, L + 1, SEG - 1:P:SEG], 0.0).then_inc(sem("edges"), 1)

            @block.tensor
            def _(pe):
                with pe.Fori(0, NB // 2) as i:
                    for u in range(2):
                        n = i * 2 + u
                        pe.wait_ge(sem("z_ready"), n + 1)
                        pe.wait_ge(sem("zT_free"), n + 1)
                        for s in range(SUB):
                            t = pe.transpose(banks[u][:, s * P:(s + 1) * P], zbuf[:, u, s, :], ident[:, :])
                        t.then_inc(sem("zT"), 1)
                with pe.Fori(0, NB // 2) as i:
                    for u in range(2):
                        n = i * 2 + u
                        pe.wait_ge(sem("conv"), n + 1)
                        pe.wait_ge(sem("gate_free"), n + 1)
                        pe.matmul(banks[2 + u][:, :], gate_wT[:, 1, :], xaT[:, ds(n, 1), :].squeeze(1), start=True, stop=True).then_inc(sem("gate_in"), 1)
                for g in range(4):
                    pe.wait_ge(sem("gated"), 2 * g + 2)
                    if g >= 2:
                        pe.wait_ge(sem("B_copied"), g - 1)
                    for k in range(8):
                        x = gi[:, 2 * g + k // 4, (k % 4) * P:(k % 4 + 1) * P]
                        t = pe.matmul(banks[6 + g % 2][:, k * S:(k + 1) * S], x, BC_wT[:, 0, :], start=True, stop=True)
                    t.then_inc(sem("B_proj"), 1)
                for g in range(4):
                    if g >= 2:
                        pe.wait_ge(sem("C_copied"), g - 1)
                    for k in range(8):
                        x = xaT[:, 2 * g + k // 4, (k % 4) * P:(k % 4 + 1) * P]
                        t = pe.matmul(banks[4 + g % 2][:, k * S:(k + 1) * S], x, BC_wT[:, 1, :], start=True, stop=True)
                    t.then_inc(sem("C_proj"), 1)

            @block.scalar
            def _(act):
                act.sem_inc(sem("zT_free"), 2)
                act.sem_inc(sem("gate_free"), 2)
                act.wait_ge(sem("var_ready"), 1)
                act.activation(tmp, var, ACT.Sqrt, bias=eps_col[:, :]).then_inc(sem("std_ready"), 1)
                act.wait_ge(sem("var_ready"), 2)
                act.activation(tmp, tmp2, ACT.Sqrt, bias=eps_col[:, :]).then_inc(sem("std_ready"), 1)
                with act.Fori(0, NB // 2) as i:
                    for u in range(2):
                        n = i * 2 + u
                        act.wait_ge(sem("zT"), n + 1)
                        act.activation(xpad[:, ds(n * SUB + 1, SUB), :], banks[u][:, :].rearrange("p (k n) -> p k n", k=SUB), ACT.Identity, bias=col["ln_in_b"],
                                       scale=col["ln_in_g"]).then_inc(sem("affine"), 1)
                        act.activation(xfT[:, ds(n, 1), :], banks[u][:, :].unsqueeze(1), ACT.Identity, bias=col["ln_beta"],
                                       scale=col["ln_gamma"]).then_inc(sem("zT_free"), 1)
                with act.Fori(0, NB // 2) as i:
                    for u in range(2):
                        n = i * 2 + u
                        act.wait_ge(sem("gate_in"), n + 1)
                        act.activation(gi[:, ds(n, 1), :], banks[2 + u][:, :].unsqueeze(1), ACT.Sigmoid, bias=col["gate_b_in"])\
                           .then_inc(sem("gate_free"), 1)

        ring = sb("ring", [P, UNROLL, SX])
        rho = sb("rho", [P, UNROLL])
        wT = sb("wT", [P, S])
        n2 = sb("n2", [P, 2])
        kappa = sb("kappa", [P, 1])
        sqj = sb("sqj", [P, SX])
        start_now = sb("start_now", [P, SX])
        start_old = sb("start_old", [P, SX])
        drift = sb("drift", [P, 2])
        drift1 = sb("drift1", [1, 2])
        agreed = sb("agreed", [1, 1], mybir.dt.int32)
        HALF = UNROLL // 2
        PER = L + 1
        psY, psS, psF = banks[0][:, 0:SX], banks[1][:, 0:SX], banks[2][0:1, 0:P]
        last = ring[:, UNROLL - 1, :]

        def vector_round(dve, r):
            with dve.Fori(0, L // UNROLL) as j:
                for u in range(UNROLL):
                    k = j * UNROLL + u
                    n = r * L + k
                    prev = ring[:, (u - 1) % UNROLL, :]
                    dve.wait_ge(sem("state"), r * PER + k + 1)
                    dve.transpose(wT[:, :], prev[:, 0:S]).then_inc(sem("state_T"), 1)
                    dve.tensor_tensor_reduce(sqj[:, :], prev, prev, 1.0 / S, 0.0, ALU.mult, ALU.add, n2[:, 0:1]).then_inc(sem("norm"), 1)
                    if u % HALF == 0:
                        dve.wait_ge(sem("stored"), r * (2 * L // HALF) + j * 4 + 2 * (u // HALF) + 2)
                    dve.wait_ge(sem("scale"), n + 1)
                    d = Dv[:, ds(k, 1), :].squeeze(1)
                    if u % RENORM == 0:
                        dve.reciprocal(kappa[:, :], rho[:, u:u + 1]).then_inc(sem("kappa"), 1)
                        dve.wait_ge(sem("kappa"), r * (L // RENORM) + j * (UNROLL // RENORM) + u // RENORM + 1)
                        dve.wait_ge(sem("product"), n + 1)
                        dve.scalar_tensor_tensor(out=ring[:, u, :], in0=psY, scalar=kappa[:, :], in1=d, op0=ALU.mult, op1=ALU.add)\
                           .then_inc(sem("state"), 1)
                    else:
                        dve.wait_ge(sem("product"), n + 1)
                        dve.scalar_tensor_tensor(out=ring[:, u, :], in0=d, scalar=rho[:, u:u + 1], in1=psY, op0=ALU.mult, op1=ALU.add)\
                           .then_inc(sem("state"), 1)
            dve.wait_ge(sem("state"), r * PER + L + 1)
            dve.tensor_tensor_reduce(sqj[:, :], last, last, 1.0 / S, 0.0, ALU.mult, ALU.add, n2[:, 1:2]).then_inc(sem("last_norm"), 1)
            dve.wait_ge(sem("last_norm"), r + 1)
            dve.tensor_copy(start_old[:, :], start_now[:, :]).then_inc(sem("old_start"), 1)
            dve.wait_ge(sem("old_start"), r + 1)
            dve.wait_ge(sem("last_scale"), r + 1)
            dve.reciprocal(kappa[:, :], Rho[:, L:L + 1]).then_inc(sem("last_kappa"), 1)
            dve.wait_ge(sem("last_kappa"), r + 1)
            dve.tensor_scalar(sqj[:, :], last, kappa[:, :], None, ALU.mult).then_inc(sem("end"), 1)
            dve.wait_ge(sem("shifted"), r + 1)
            dve.wait_ge(sem("stored"), (r + 1) * (2 * L // HALF) + 4)
            dve.tensor_tensor(start_now[:, :], psS, start_add[:, :], ALU.add).then_inc(sem("new_start"), 1)
            dve.tensor_tensor(last, psS, start_add[:, :], ALU.add).then_inc(sem("state"), 1)

        def tensor_round(pe, r):
            with pe.Fori(0, L // UNROLL) as j:
                for u in range(UNROLL):
                    n = r * L + j * UNROLL + u
                    pe.wait_ge(sem("state_T"), n + 1)
                    pe.sem_inc(sem("tick"), 1)
                    for c in range(2):
                        for a in range(4):
                            q = slice(32 * a, 32 * a + 32)
                            t = pe.matmul(psY[q], wT[q, 32 * c:32 * c + 32], Mrep[q, c, :], start=(c == 0), stop=(c == 1))
                    t.then_inc(sem("product"), 1)
            pe.wait_ge(sem("end"), r + 1)
            pe.matmul(psS, shift[:, :], sqj[:, :], start=True, stop=True).then_inc(sem("shifted"), 1)

        def scalar_round(act, r):
            with act.Fori(0, L // UNROLL) as j:
                for u in range(UNROLL):
                    n = r * L + j * UNROLL + u
                    if u % HALF == 0:
                        act.wait_ge(sem("stored"), r * (2 * L // HALF) + j * 4 + 2 * (u // HALF) + 2)
                    act.wait_ge(sem("norm"), n + 1)
                    act.activation(rho[:, u:u + 1], n2[:, 0:1], ACT.Sqrt).then_inc(sem("scale"), 1)
            act.wait_ge(sem("last_norm"), r + 1)
            act.activation(Rho[:, L:L + 1], n2[:, 1:2], ACT.Sqrt).then_inc(sem("last_scale"), 1)

        def pool_round(pool, r):
            with pool.Fori(0, L // UNROLL) as j:
                for h in range(2):
                    at = j * UNROLL + h * HALF
                    part = slice(h * HALF, (h + 1) * HALF)
                    pool.wait_ge(sem("state"), r * PER + j * UNROLL + (h + 1) * HALF + 1)
                    pool.tensor_copy(Wst[:, ds(at, HALF), :], ring[:, part, :]).then_inc(sem("stored"), 1)
                    pool.tensor_copy(Rho[:, ds(at, HALF)], rho[:, part]).then_inc(sem("stored"), 1)

        def rounds(eng, one_round):
            with eng.Fori(0, ROUNDS) as r:
                one_round(eng, r)
            if one_round is vector_round:
                eng.wait_ge(sem("new_start"), ROUNDS)
                eng.tensor_tensor(sqj[:, :], start_now[:, :], start_old[:, :], ALU.subtract).then_inc(sem("drift"), 1)
                eng.wait_ge(sem("drift"), 1)
                eng.tensor_reduce(drift[:, 0:1], sqj[:, :], AX_X, ALU.max, apply_absolute_value=True).then_inc(sem("drift_col"), 1)
                eng.wait_ge(sem("drift_row"), 1)
                eng.tensor_reduce(drift1[:, 0:1], psF, AX_X, ALU.max).then_inc(sem("drift"), 1)
                eng.wait_ge(sem("drift"), 2)
                eng.tensor_scalar(agreed[:, :], drift1[:, 0:1], TOLERANCE, None, ALU.is_le).then_inc(sem("agreed"), 1)
            if one_round is tensor_round:
                eng.wait_ge(sem("drift_col"), 1)
                eng.transpose(psF, drift[:, 0:1], ident[:, :]).then_inc(sem("drift_row"), 1)
            eng.wait_ge(sem("agreed"), 1)
            settled = eng.value_load(agreed[0:1, 0:1], min_val=0, max_val=1)
            with eng.If(settled < 1):
                with eng.Fori(ROUNDS, SEG) as r:
                    one_round(eng, r)
            eng.end_ifs()

        with nc.Block() as block:
            @block.vector
            def _(dve):
                dve.memset(start_now[:, :], 0.0).then_inc(sem("scan_zero"), 1)
                dve.memset(last, 0.0).then_inc(sem("scan_zero"), 1)
                dve.wait_ge(sem("scan_zero"), 2)
                dve.memset(ring[:, UNROLL - 1, S:SX], float(S) ** 0.5).then_inc(sem("state"), 1)
                rounds(dve, vector_round)

            @block.tensor
            def _(pe):
                rounds(pe, tensor_round)

            @block.scalar
            def _(act):
                act.activation(junk_col[:, :], eps_col[:, :], ACT.Sqrt)
                rounds(act, scalar_round)

            @block.gpsimd
            def _(pool):
                pool.sem_inc(sem("stored"), 4)
                rounds(pool, pool_round)

        fx = xpad[:, :, :].rearrange("p a b -> p (a b)")[:, 0:4096]
        def buf(i):
            return fx[:, i * 512:(i + 1) * 512].rearrange("p (s h) -> p s h", s=SUB)
        abel, gated, attn, acc, fbuf, th, obuf, junk = (buf(i) for i in range(8))
        hT = sb("hT", [P, 2, K, T])
        xf_cur = sb("xf_cur", [P, SUB, P])
        xa_cur = sb("xa_cur", [P, SUB, P])
        cs_cur = sb("cs_cur", [P, 2, P])
        csT = gi[:, 0:4, :].rearrange("p a b -> p (a b)").rearrange("p (k n) -> p k n", n=P)
        small = sb("small", [P, 12, SUB, E])
        lg, m8, oh1, lg2, m8b, oh2, wd, wt = (small[:, i] for i in range(8))
        four = sb("four", [P, 10, SUB])
        ix1, ix2, dm, tw, w1, w2, gca, gcm, gc, gg = (four[:, i] for i in range(10))
        ixu = sb("ixu", [P, 2, SUB, 8], U32)
        wdT = sb("wdT", [E, SUB, P])
        bH = [banks[0], banks[1], banks[2], banks[3]]
        bE = [banks[4], banks[5]]
        bM, bR = banks[6], banks[7]
        bR4 = bR[:, :].rearrange("p (s h) -> p s h", s=SUB)

        def b4(ap):
            return ap.unsqueeze(2).broadcast_to([P, SUB, P])

        def b8(ap):
            return ap.unsqueeze(2).broadcast_to([P, SUB, E])

        with nc.Block() as block:
            @block.vector
            def _(dve):
                dve.reciprocal(Rho[:, 1:L + 1], Rho[:, 1:L + 1])
                dve.tensor_tensor(gC[:, :, :], CL, st_g_all.unsqueeze(1).broadcast_to([P, L, S]), ALU.mult)
                dve.tensor_tensor(bC[:, :, :], CL, st_b_all.unsqueeze(1).broadcast_to([P, L, S]), ALU.mult).then_inc(sem("cs_a"), 1)
                dve.wait_ge(sem("cs_a"), 1)
                dve.tensor_tensor(gC[:, :, :], gC[:, :, :], Rho[:, 1:L + 1].unsqueeze(2).broadcast_to([P, L, S]), ALU.mult).then_inc(sem("cs_a"), 1)
                dve.wait_ge(sem("cs_a"), 2)
                dve.tensor_tensor(gC[:, :, :], gC[:, :, :], Wst[:, :, 0:S], ALU.mult).then_inc(sem("cs_a"), 1)
                dve.wait_ge(sem("cs_a"), 3)
                dve.tensor_tensor(gC[:, :, :], gC[:, :, :], bC[:, :, :], ALU.add).then_inc(sem("cs_all"), 1)

            @block.tensor
            def _(pe):
                pe.wait_ge(sem("cs_all"), 1)
                for q in range(L // 2):
                    t = pe.transpose(banks[q // 4][:, (q % 4) * P:(q % 4 + 1) * P], gC[:, 2 * q:2 * q + 2, :].rearrange("p k n -> p (k n)"), ident[:, :])
                    if q % 4 == 3:
                        t.then_inc(sem("cs_T"), 1)

            @block.scalar
            def _(act):
                for g in range(4):
                    act.wait_ge(sem("cs_T"), g + 1)
                    act.copy(csT[:, g * 4:g * 4 + 4, :], banks[g][:, :].rearrange("p (k n) -> p k n", k=4))

        with nc.Block() as block:
            @block.sync
            def _(sp):
                sp.wait_ge(sem("ffn_loaded"), 48)
                for n in range(NB):
                    sp.wait_ge(sem("xf_free"), n + 1)
                    sp.dma_start(xf_cur[:, :, :].rearrange("p s h -> p (s h)"), xfT[:, n, :]).then_inc(sem("xf_cur"), 16)
                    sp.wait_ge(sem("xa_free"), n + 1)
                    sp.dma_start(xa_cur[:, :, :].rearrange("p s h -> p (s h)"), xaT[:, n, :]).then_inc(sem("xa_cur"), 16)
                    sp.wait_ge(sem("cs_free"), n + 1)
                    sp.dma_start(cs_cur[:, :, :], csT[:, 2 * n:2 * n + 2, :]).then_inc(sem("cs_cur"), 16)
                    sp.wait_ge(sem("out_row"), n + 1)
                    sp.dma_start(out.rearrange("b (q k) h -> (b q) k h", k=L)[:, n * SUB:(n + 1) * SUB, :], obuf).then_inc(sem("out_stored"), 16)
                sp.wait_ge(sem("out_stored"), 16 * (NB + 1))

            @block.tensor
            def _(pe):
                pe.sem_inc(sem("xf_free"), 1)
                pe.sem_inc(sem("xa_free"), 1)
                pe.sem_inc(sem("cs_free"), 1)
                with pe.Fori(0, NB) as n:
                    xf = xfT[:, ds(n, 1), :].squeeze(1)

                    def layer1(e):
                        pe.wait_ge(sem("hidden"), n * E + e + 1)
                        for k in range(K):
                            t = pe.matmul(bH[(e % 2) * 2 + k][:, :], ew1[:, e, k * P:(k + 1) * P], xf, start=True, stop=True)
                        t.then_inc(sem("pre_hidden"), 1)

                    def layer2(e):
                        pe.wait_ge(sem("hidden"), n * E + e + 3)
                        pe.wait_ge(sem("summed"), n * E + e + 1)
                        for s in range(SUB):
                            for k in range(K):
                                t = pe.matmul(bE[e % 2][:, s * P:(s + 1) * P], hT[:, e % 2, k, s * P:(s + 1) * P], ew2[:, e, k, :],
                                              start=(k == 0), stop=(k == K - 1))
                        t.then_inc(sem("expert_out"), 1)

                    def row_product(x, w, bias, name):
                        for s in range(SUB):
                            pe.matmul(bR[:, s * P:(s + 1) * P], x[:, s, :], w, start=True, stop=False)
                            t = pe.matmul(bR[:, s * P:(s + 1) * P], ones[0:1, :], bias, start=False, stop=True)
                        t.then_inc(sem(name), 1)

                    pe.wait_ge(sem("xf_cur"), 16 * (n + 1))
                    for s in range(SUB):
                        t = pe.matmul(bM[:, s * E:(s + 1) * E], xf_cur[:, s, :], router_w[:, :], start=True, stop=True)
                    t.then_inc(sem("router"), 1)
                    layer1(0)
                    pe.wait_ge(sem("row_free"), n + 1)
                    row_product(xf_cur, abel_w[:, :], abel_b_row, "abel_pre")
                    pe.wait_ge(sem("abel_pre"), n + 1)
                    pe.sem_inc(sem("xf_free"), 1)
                    layer1(1)
                    layer2(0)
                    pe.wait_ge(sem("abel"), n + 1)
                    pe.wait_ge(sem("weights"), n + 1)
                    for s in range(SUB):
                        t = pe.transpose(bR[0:E, s * P:(s + 1) * P], wd[:, s, :], ident[:, :])
                    t.then_inc(sem("weights_T"), 1)
                    layer1(2)
                    layer2(1)
                    pe.wait_ge(sem("wdT"), n + 1)
                    for s in range(SUB):
                        t = pe.matmul(bR[:, s * P:(s + 1) * P], wdT[:, s, :], eb2r[:, :], start=True, stop=True)
                    t.then_inc(sem("expert_bias"), 1)
                    layer1(3)
                    layer2(2)
                    pe.wait_ge(sem("bias_added"), n + 1)
                    pe.wait_ge(sem("xa_cur"), 16 * (n + 1))
                    row_product(xa_cur, gate_wT[:, 0, :], gate_b_row, "gate_pre")
                    pe.wait_ge(sem("gate_pre"), n + 1)
                    pe.sem_inc(sem("xa_free"), 1)
                    layer1(4)
                    layer2(3)
                    pe.wait_ge(sem("gate"), n + 1)
                    pe.wait_ge(sem("cs_cur"), 16 * (n + 1))
                    for s in range(SUB):
                        pe.matmul(bR[:, s * P:(s + 1) * P], cs_cur[:, s // 2, :], D_wT[:, s % 2, :], start=True, stop=False)
                        t = pe.matmul(bR[:, s * P:(s + 1) * P], ones[0:1, :], D_b_row, start=False, stop=True)
                    t.then_inc(sem("ssm"), 1)
                    pe.wait_ge(sem("ssm"), n + 1)
                    pe.sem_inc(sem("cs_free"), 1)
                    for e in range(5, E):
                        layer1(e)
                        layer2(e - 1)
                    layer2(E - 1)

            @block.scalar
            def _(act):
                act.sem_inc(sem("hidden"), 2)
                act.activation(junk_col[:, :], eps_col[:, :], ACT.Gelu)
                with act.Fori(0, NB) as n:
                    def gelus(e):
                        act.wait_ge(sem("pre_hidden"), n * E + e + 1)
                        act.wait_ge(sem("hT_free"), n * E + e + 1)
                        for k in range(K):
                            t = act.activation(hT[:, e % 2, k, :], bH[(e % 2) * 2 + k][:, :], ACT.Gelu, bias=eb1_col[:, e, k:k + 1])
                        t.then_inc(sem("hidden"), 1)

                    gelus(0)
                    act.wait_ge(sem("abel_pre"), n + 1)
                    act.wait_ge(sem("abel_free"), n + 1)
                    act.activation(abel, bR4, ACT.Gelu).then_inc(sem("abel"), 1)
                    act.wait_ge(sem("margin"), n + 1)
                    act.activation(tw, dm, ACT.Tanh, scale=-0.5).then_inc(sem("margin_tanh"), 1)
                    gelus(1)
                    gelus(2)
                    gelus(3)
                    act.wait_ge(sem("gate_pre"), n + 1)
                    act.activation(gated, bR4, ACT.Tanh, scale=0.5).then_inc(sem("gate"), 1)
                    for e in range(4, E):
                        gelus(e)
                    act.wait_ge(sem("mix_dot"), n + 1)
                    act.activation(gg, gc, ACT.Tanh, scale=0.5, bias=half_gc_b).then_inc(sem("mix_tanh"), 1)
                    act.wait_ge(sem("ffn"), n + 1)
                    act.activation(th, fbuf, ACT.Tanh, scale=0.5).then_inc(sem("silu_tanh"), 1)

            @block.vector
            def _(dve):
                for name, credit in (("summed", 2), ("hT_free", 2), ("row_free", 1), ("abel_free", 1)):
                    dve.sem_inc(sem(name), credit)
                dve.sem_inc(sem("out_stored"), 16)
                with dve.Fori(0, NB) as n:
                    def step(ins, name, count=n + 1):
                        ins.then_inc(sem(name), 1)
                        dve.wait_ge(sem(name), count)

                    dve.wait_ge(sem("router"), n + 1)
                    step(dve.tensor_tensor(lg, bM[:, 0:SUB * E].rearrange("p (s e) -> p s e", s=SUB),
                                           mgb_all.unsqueeze(1).broadcast_to([P, SUB, E]), ALU.add), "logits")
                    dve.tensor_copy(junk[:, 0, 0:1], lg[:, 0, 0:1])
                    for s in range(SUB):
                        t = dve.max(m8[:, s, :], lg[:, s, :])
                    step(t, "top1")
                    dve.tensor_copy(junk[:, 0, 0:1], m8[:, 0, 0:1])
                    for s in range(SUB):
                        t = dve.max_index(ixu[:, 0, s, :], m8[:, s, :], lg[:, s, :])
                    step(t, "index1")
                    step(dve.tensor_copy(ix1, ixu[:, 0, :, 0]), "index1_f")
                    step(dve.tensor_tensor(oh1, iota_f[:, :, :], b8(ix1), ALU.is_equal), "onehot1")
                    step(dve.scalar_tensor_tensor(out=lg2, in0=oh1, scalar=-3e38, in1=lg, op0=ALU.mult, op1=ALU.add), "rest")
                    dve.tensor_copy(junk[:, 0, 0:1], lg2[:, 0, 0:1])
                    for s in range(SUB):
                        t = dve.max(m8b[:, s, :], lg2[:, s, :])
                    step(t, "top2")
                    dve.tensor_tensor(dm, m8b[:, :, 0], m8[:, :, 0], ALU.subtract).then_inc(sem("margin"), 1)
                    for s in range(SUB):
                        t = dve.max_index(ixu[:, 1, s, :], m8b[:, s, :], lg2[:, s, :])
                    step(t, "index2")
                    step(dve.tensor_copy(ix2, ixu[:, 1, :, 0]), "index2_f")
                    dve.tensor_tensor(oh2, iota_f[:, :, :], b8(ix2), ALU.is_equal)
                    dve.wait_ge(sem("margin_tanh"), n + 1)
                    dve.tensor_scalar(w1, tw, 0.5, 0.5, ALU.mult, ALU.add)
                    step(dve.tensor_scalar(w2, tw, -0.5, 0.5, ALU.mult, ALU.add), "pair")
                    dve.tensor_tensor(wd, oh1, b8(w1), ALU.mult)
                    step(dve.tensor_tensor(wt, oh2, b8(w2), ALU.mult), "weighted")
                    step(dve.tensor_tensor(wd, wd, wt, ALU.add), "weights")

                    def add_expert(e):
                        dve.wait_ge(sem("expert_out"), n * E + e + 1)
                        if e:
                            dve.wait_ge(sem("summed"), n * E + e + 2)
                        for s in range(SUB):
                            src = bE[e % 2][:, s * P:(s + 1) * P]
                            if e == 0:
                                t = dve.tensor_scalar(acc[:, s, :], src, wd[:, s, 0:1], None, ALU.mult)
                            else:
                                t = dve.scalar_tensor_tensor(out=acc[:, s, :], in0=src, scalar=wd[:, s, e:e + 1], in1=acc[:, s, :],
                                                             op0=ALU.mult, op1=ALU.add)
                        t.then_inc(sem("summed"), 1)
                        dve.sem_inc(sem("hT_free"), 1)

                    add_expert(0)
                    dve.wait_ge(sem("weights_T"), n + 1)
                    dve.tensor_copy(wdT[:, :, :], bR[0:E, :].rearrange("p (s h) -> p s h", s=SUB)).then_inc(sem("wdT"), 1)
                    add_expert(1)
                    dve.wait_ge(sem("expert_bias"), n + 1)
                    dve.wait_ge(sem("summed"), n * E + 4)
                    step(dve.tensor_tensor(acc, acc, bR4, ALU.add), "bias_added")
                    add_expert(2)
                    add_expert(3)
                    dve.wait_ge(sem("abel"), n + 1)
                    for s in range(SUB):
                        t = dve.tensor_tensor_reduce(junk[:, s, :], abel[:, s, :], gc_w_all[:, 0:P], 1.0, 0.0, ALU.mult, ALU.add, gca[:, s:s + 1])
                    t.then_inc(sem("dot_abel"), 1)
                    dve.wait_ge(sem("ssm"), n + 1)
                    dve.wait_ge(sem("gate"), n + 1)
                    dve.scalar_tensor_tensor(out=attn, in0=gated, scalar=1.0, in1=bR4, op0=ALU.add, op1=ALU.mult).then_inc(sem("row_free"), 1)
                    for e in range(4, E):
                        add_expert(e)
                    dve.wait_ge(sem("summed"), n * E + E + 2)
                    for s in range(SUB):
                        t = dve.tensor_tensor_reduce(junk[:, s, :], acc[:, s, :], gc_w_all[:, P:2 * P], 1.0, 0.0, ALU.mult, ALU.add, gcm[:, s:s + 1])
                    step(t, "dot_moe")
                    dve.tensor_tensor(gc, gca, gcm, ALU.add).then_inc(sem("mix_dot"), 1)
                    step(dve.tensor_tensor(acc, acc, abel, ALU.subtract), "difference")
                    for s in range(SUB):
                        q = n * SUB + s
                        t = dve.tensor_scalar(fbuf[:, s, :], X[:, ds(q, 1), :].squeeze(1), r1[:, ds(q, 1)], nm1[:, ds(q, 1)], ALU.mult, ALU.add)
                    step(t, "residual")
                    step(dve.tensor_tensor(fbuf, fbuf, abel, ALU.add), "residual_abel")
                    dve.wait_ge(sem("mix_tanh"), n + 1)
                    step(dve.tensor_scalar(gg, gg, 0.5, 0.5, ALU.mult, ALU.add), "mix_gate")
                    for s in range(SUB):
                        t = dve.scalar_tensor_tensor(out=fbuf[:, s, :], in0=acc[:, s, :], scalar=gg[:, s:s + 1], in1=fbuf[:, s, :], op0=ALU.mult, op1=ALU.add)
                    step(t, "ffn")
                    dve.sem_inc(sem("abel_free"), 1)
                    dve.wait_ge(sem("silu_tanh"), n + 1)
                    step(dve.scalar_tensor_tensor(out=fbuf, in0=th, scalar=1.0, in1=fbuf, op0=ALU.add, op1=ALU.mult), "silu")
                    step(dve.tensor_tensor(fbuf, fbuf, attn, ALU.mult), "gated_ffn")
                    dve.wait_ge(sem("out_stored"), 16 * (n + 1))
                    dve.scalar_tensor_tensor(out=obuf, in0=fbuf, scalar=0.25, in1=X[:, ds(n * SUB, SUB), :], op0=ALU.mult, op1=ALU.add)\
                       .then_inc(sem("out_row"), 1)


_INS = ["L0_attn_x", "L0_attn_A", "L0_attn_dt_A", "L0_attn_B_w", "L0_attn_B_b", "L0_attn_C_w", "L0_attn_C_b", "L0_attn_D_w",
        "L0_attn_D_b", "L0_attn_conv_w", "L0_attn_conv_b", "L0_attn_gate_w", "L0_attn_gate_b", "L0_attn_ln_in_g",
        "L0_attn_ln_in_b", "L0_attn_ln_st_g", "L0_attn_ln_st_b", "L0_ffn_ln_gamma", "L0_ffn_ln_beta", "L0_ffn_abel_w",
        "L0_ffn_abel_b", "L0_ffn_moe_gate_w", "L0_ffn_moe_gate_b", "L0_ffn_ew1", "L0_ffn_eb1", "L0_ffn_ew2", "L0_ffn_eb2",
        "L0_ffn_gens", "L0_ffn_gc_w", "L0_ffn_gc_b"]


def kernel(**inputs):
    import numpy as _np
    import concourse.bacc as _bacc
    from concourse import mybir as _mybir
    from concourse.bass_utils import run_bass_kernel_spmd as _run

    nc = _bacc.Bacc("TRN2", target_bir_lowering=False, num_devices=1)
    arrays, I = {}, {}
    for name in _INS:
        a = _np.ascontiguousarray(inputs[name])
        if a.ndim == 0 or name == "L0_attn_dt_A":
            a = a.reshape(1, 1)
        arrays[f"in_{name}"] = a
        I[name] = nc.dram_tensor(f"in_{name}", a.shape, _mybir.dt.from_np(a.dtype), kind="ExternalInput").ap()
    out = nc.dram_tensor("out_0", inputs["L0_attn_x"].shape, _mybir.dt.float32, kind="ExternalOutput").ap()
    build(nc, I, out)
    r = _run(nc, [arrays], core_ids=[0])
    return r.results[0]["out_0"]
```

```python
from contextlib import ExitStack

import concourse.bass as bass
from concourse import mybir

ALU = mybir.AluOpType
ACT = mybir.ActivationFunctionType
AX_X = mybir.AxisListType.X
F32 = mybir.dt.float32
BF16 = mybir.dt.bfloat16

P = 128
EPS = 1e-5
SCALE_STEPS = 5
TAYLOR = 10
UNROLL = 8
SEG = 16
ROUNDS = 6
TOLERANCE = 3e-5
ds = bass.ds

RSQRT_MAGIC = float(0x5F3759DF)
RSQRT_FACTOR = -27.0 / 1024.0


def build(nc, I, out):
    NB, T, H = I["L0_attn_x"].shape
    S = I["L0_attn_A"].shape[0]
    E, _, F = I["L0_ffn_ew1"].shape
    NROT = I["L0_ffn_gens"].shape[0]
    K = F // P
    SUB = T // P
    NS = NB * SUB
    L = T // SEG
    assert NB * SEG == P and L % UNROLL == 0 and S == 64
    assert H == P and T % P == 0 and F % P == 0 and NROT + 1 == 4 and SUB == 4 and E == 8

    with ExitStack() as ctx:
        sems = {}

        def sem(name):
            if name not in sems:
                sems[name] = ctx.enter_context(nc.semaphore(name))
            return sems[name]

        def sb(name, shape, dt=F32):
            return ctx.enter_context(nc.sbuf_tensor(name, shape, dt))

        banks = [ctx.enter_context(nc.psum_tensor(f"bank{i}", [P, 512], F32)) for i in range(8)]

        ident = sb("ident", [P, P])
        ones = sb("ones", [P, P])
        shift = sb("shift", [P, P])
        first_col = sb("first_col", [P, 1])
        center = sb("center", [S, S])
        iota_i = sb("iota_i", [P, NS * E], mybir.dt.int32)
        rank = sb("rank", [P, NS, E])
        eps_col = sb("eps_col", [P, 1])
        junk_col = sb("junk_col", [P, 1])
        cols = sb("cols", [P, 24])
        names = ["ln_in_g", "ln_in_b", "conv_b", "gate_b_in", "ln_gamma", "ln_beta", "B_b", "ln_st_g", "ln_st_b"]
        col = {n: cols[:, i:i + 1] for i, n in enumerate(names)}
        conv_w = cols[:, 10:13]
        conv_w1 = cols[:, 13:14]
        dt_col = cols[0:S, 14:15]
        row_mean = cols[:, 18:19]
        row_mean_b = cols[:, 19:20]
        half_gc_b = cols[:, 20:21]
        eb1_col = sb("eb1_col", [P, E, K])
        eb1_rows = sb("eb1_rows", [E * K, P])
        rows = sb("rows", [1, 2 * P + E + 2 + 3 * S])
        gc_w_row = rows[:, 0:2 * P]
        mgb_row = rows[:, 2 * P:2 * P + E]
        gc_b_row = rows[:, 2 * P + E:2 * P + E + 1]
        dt_row = rows[:, 2 * P + E + 1:2 * P + E + 2]
        st_rows = rows[:, 2 * P + E + 2:2 * P + E + 2 + 3 * S]
        bias_in = sb("bias_in", [3, 3, P])
        bias_rest = sb("bias_rest", [3, 2, 3, P])
        bias_part = sb("bias_part", [3, 2, 3, P], BF16)
        bias_mix = sb("bias_mix", [3, 3, P])
        bias_low = sb("bias_low", [3, 3, P])
        bias3 = sb("bias3", [3, 3, SUB, P], BF16)
        abel_b3, D_b3, gate_b3 = (bias3[:, i].rearrange("a s h -> a (s h)") for i in range(3))
        ones3 = sb("ones3", [3, P], BF16)
        bcast = sb("bcast", [P, 2 * P + E + 1 + 3 * S])
        gc_w_all = bcast[:, 0:2 * P]
        mgb_all = bcast[:, 2 * P:2 * P + E]
        C_b_all, st_g_all, st_b_all = (bcast[:, 2 * P + E + 1 + i * S:2 * P + E + 1 + (i + 1) * S] for i in range(3))
        bias_src = sb("bias_src", [S, 2, P])
        bias_all = sb("bias_all", [P, 3, S])

        gate_w = sb("gate_w", [P, 2, P])
        gate_wT = sb("gate_wT", [P, 2, P])
        BC_w = sb("BC_w", [S, 2, P])
        BC_wT = sb("BC_wT", [P, 2, S])
        D_w = sb("D_w", [P, 2, S])
        D_wT = sb("D_wT", [P, 2, P])
        abel_w = sb("abel_w", [P, P])
        router_w = sb("router_w", [P, E])
        ew1 = sb("ew1", [P, E, F])
        ew2 = sb("ew2", [P, E, K, P])
        eb2 = sb("eb2", [E, P])
        eb2T = sb("eb2T", [P, E])
        eb2r = sb("eb2r", [E, P])
        Mx = sb("Mx", [S, S])
        pick = sb("pick", [S, 2, P])
        Mrep = sb("Mrep", [P, 2, S])
        AbC = sb("AbC", [S, S])
        R23 = sb("R23", [P, P])
        Rall = sb("Rall", [P, P])

        X = sb("X", [P, NS, P])
        st = sb("st", [P, NS, 6])
        lnv = sb("lnv", [P, 8, NS])
        xpad = sb("xpad", [P, L + 2, P])
        xaT = sb("xaT", [P, NB, T])
        xfT = sb("xfT", [P, NB, T])
        gi_all = sb("gi", [P, NB + 1, T])
        gi = gi_all[:, 1:, :]
        Dv = sb("Dv", [P, L, S])
        Wst = sb("Wst", [P, L, S])
        Rho = sb("Rho", [P, L + 1])
        gC = sb("gC", [P, L, S])
        bC = sb("bC", [P, L, S])
        CL = gi[:, 4:8, :].rearrange("p a b -> p (a b)").rearrange("p (k n) -> p k n", n=S)

        ew2T = xaT[:, 0:4, :].rearrange("p a b -> p (a b)").rearrange("p (e k f) -> p e k f", e=E, k=K)
        ex = xfT[:, :, :].rearrange("p a b -> p (a b)")
        XE = ex[:, 0:512].rearrange("p (m n) -> p m n", m=4)
        XT = ex[:, 512:1024].rearrange("p (m n) -> p m n", m=4)
        EX = ex[:, 1024:1536].rearrange("p (m n) -> p m n", m=4)
        ET = ex[:, 1536:2048].rearrange("p (m n) -> p m n", m=4)
        gens = ex[:, 2048:2432].rearrange("p (m n) -> p m n", m=3)
        A_in = ex[0:S, 2432:2432 + S]

        zbuf = sb("zbuf", [P, 2, SUB, P])

        ident4 = ident[:, :].unsqueeze(1).broadcast_to([P, 4, P])

        N_W = 36
        with nc.Block() as setup:
            @setup.sync
            def _(sp):
                xr = I["L0_attn_x"].rearrange("b (q k) h -> (b q) k h", k=L)

                def load(dst, src):
                    sp.dma_start(dst, src).then_inc(sem("weights_loaded"), 16)

                def as_col(name):
                    return I[name].rearrange("(p a) -> p a", a=1)

                load(gens, I["L0_ffn_gens"].rearrange("m p n -> p m n"))
                load(A_in, I["L0_attn_A"])
                load(dt_row, I["L0_attn_dt_A"])
                load(gate_w[:, :, :], I["L0_attn_gate_w"].rearrange("(j p) h -> p j h", p=P))
                load(BC_w[:, 0, :], I["L0_attn_B_w"])
                load(BC_w[:, 1, :], I["L0_attn_C_w"])
                load(D_w[:, 0, :], I["L0_attn_D_w"])
                load(D_w[:, 1, :], I["L0_attn_D_w"])
                load(col["ln_in_g"], as_col("L0_attn_ln_in_g"))
                load(col["ln_in_b"], as_col("L0_attn_ln_in_b"))
                load(col["conv_b"], as_col("L0_attn_conv_b"))
                load(conv_w, I["L0_attn_conv_w"].rearrange("h a k -> h (a k)"))
                load(col["gate_b_in"], I["L0_attn_gate_b"][P:2 * P].rearrange("(p a) -> p a", a=1))
                for i in range(3):
                    load(bias_in[i:i + 1, 2, :], I["L0_attn_gate_b"][0:P].rearrange("(a p) -> a p", a=1))
                load(col["ln_gamma"], as_col("L0_ffn_ln_gamma"))
                load(col["ln_beta"], as_col("L0_ffn_ln_beta"))
                for i, name in enumerate(("L0_attn_C_b", "L0_attn_ln_st_g", "L0_attn_ln_st_b")):
                    load(st_rows[:, i * S:(i + 1) * S], I[name].rearrange("(a p) -> a p", a=1))
                load(col["B_b"][0:S], as_col("L0_attn_B_b"))
                load(col["ln_st_g"][0:S], as_col("L0_attn_ln_st_g"))
                load(col["ln_st_b"][0:S], as_col("L0_attn_ln_st_b"))
                load(eb2[:, :], I["L0_ffn_eb2"])
                load(eb1_rows[:, :], I["L0_ffn_eb1"].rearrange("e (k p) -> (e k) p", p=P))
                load(ew2[:, :, :, :], I["L0_ffn_ew2"].rearrange("e (k p) d -> p e k d", p=P))
                for i in range(3):
                    load(bias_in[i:i + 1, 0, :], I["L0_ffn_abel_b"].rearrange("(a p) -> a p", a=1))
                    load(bias_in[i:i + 1, 1, :], I["L0_attn_D_b"].rearrange("(a p) -> a p", a=1))
                load(gc_w_row, I["L0_ffn_gc_w"].rearrange("p a -> a p"))
                load(mgb_row, I["L0_ffn_moe_gate_b"].rearrange("(a p) -> a p", a=1))
                load(gc_b_row, I["L0_ffn_gc_b"].rearrange("(a p) -> a p", a=1))
                for b in range(NB):
                    sp.dma_start(X[:, b * SUB:(b + 1) * SUB, :], xr[:, b * SUB:(b + 1) * SUB, :]).then_inc(sem("x_loaded"), 16)
                sp.dma_start(abel_w[:, :], I["L0_ffn_abel_w"]).then_inc(sem("ffn_loaded"), 16)
                sp.dma_start(router_w[:, :], I["L0_ffn_moe_gate_w"]).then_inc(sem("ffn_loaded"), 16)
                sp.dma_start(ew1[:, :, :], I["L0_ffn_ew1"].rearrange("e d f -> d e f")).then_inc(sem("ffn_loaded"), 16)

            @setup.gpsimd
            def _(pool):
                pool.memset(ident[:, :], 0.0).then_inc(sem("ident_zero"), 1)
                pool.wait_ge(sem("ident_zero"), 1)
                pool.affine_select(out=ident[:, :], in_=ident[:, :], compare_op=ALU.not_equal, fill=1.0, base=0,
                                   pattern=[[-1, P]], channel_multiplier=1).then_inc(sem("ident_ready"), 1)
                pool.memset(ones[:, :], 1.0).then_inc(sem("ones_ready"), 1)
                pool.memset(shift[:, :], 0.0).then_inc(sem("shift_zero"), 1)
                pool.wait_ge(sem("shift_zero"), 1)
                pool.affine_select(out=shift[:, :], in_=shift[:, :], compare_op=ALU.not_equal, fill=1.0, base=1,
                                   pattern=[[-1, P]], channel_multiplier=1).then_inc(sem("shift_ones"), 1)
                pool.wait_ge(sem("shift_ones"), 1)
                pool.memset(shift[:, 0:P:SEG], 0.0).then_inc(sem("const_ready"), 1)
                pool.memset(eps_col[:, :], EPS).then_inc(sem("const_ready"), 1)
                pool.memset(XE[:, 3, :], 0.0).then_inc(sem("expm_zero"), 1)
                pool.memset(XT[:, 3, :], 0.0).then_inc(sem("expm_zero"), 1)
                pool.iota(iota_i[:, :], pattern=[[0, NS], [-1, E]], base=E, channel_multiplier=0).then_inc(sem("iota_ready"), 1)
                pool.wait_ge(sem("iota_ready"), 1)
                pool.tensor_copy(rank[:, :, :], iota_i[:, :].rearrange("p (s e) -> p s e", s=NS)).then_inc(sem("const_ready"), 1)

            @setup.tensor
            def _(pe):
                pe.wait_ge(sem("weights_loaded"), 16 * N_W)
                pe.wait_ge(sem("ident_ready"), 1)
                pe.wait_ge(sem("ones_ready"), 1)
                for m in range(NROT):
                    pe.transpose(banks[1][:, m * P:(m + 1) * P], gens[:, m, :], ident[:, :])
                pe.transpose(banks[1][0:S, 384:384 + S], A_in, ident[0:S, 0:S])
                pe.matmul(banks[2][0:S, 0:1], ones[0:1, 0:S], dt_row, start=True, stop=True).then_inc(sem("expm_in"), 1)
                for j in range(2):
                    pe.transpose(banks[0][:, j * P:(j + 1) * P], gate_w[:, j, :], ident[:, :])
                for j in range(2):
                    pe.transpose(banks[0][:, 2 * P + j * S:2 * P + (j + 1) * S], BC_w[:, j, :], ident[0:S, 0:S])
                pe.transpose(banks[0][:, 384:512], D_w[:, :, :].rearrange("p j n -> p (j n)"), ident[:, :]).then_inc(sem("small_T"), 1)
                pe.transpose(banks[7][:, 464:464 + E], eb2[:, :], ident[0:E, 0:E])
                pe.transpose(banks[7][:, 480:480 + E * K], eb1_rows[:, :], ident[0:E * K, 0:E * K])
                pe.matmul(banks[7][:, 0:2 * P], ones[0:1, :], gc_w_row, start=True, stop=True)
                pe.matmul(banks[7][:, 2 * P:2 * P + E], ones[0:1, :], mgb_row, start=True, stop=True)
                pe.matmul(banks[7][:, 2 * P + E:2 * P + E + 1], ones[0:1, :], gc_b_row, start=True, stop=True)
                pe.matmul(banks[7][:, 2 * P + E + 1:2 * P + E + 1 + 3 * S], ones[0:1, :], st_rows, start=True, stop=True).then_inc(sem("rows_all"), 1)
                for e in range(E):
                    for k in range(K):
                        q = e * K + k
                        t = pe.transpose(banks[3 + q // 4][:, (q % 4) * P:(q % 4 + 1) * P], ew2[:, e, k, :], ident[:, :])
                    if e % 2:
                        t.then_inc(sem("ew2_T"), 1)
                for k in range(TAYLOR - 1, 0, -1):
                    pe.wait_ge(sem("taylor"), TAYLOR - k)
                    for m in range(4):
                        t = pe.matmul(banks[1][:, m * P:(m + 1) * P], XT[:, m, :], EX[:, m, :], start=True, stop=True)
                    t.then_inc(sem("taylor_product"), 1)
                pe.wait_ge(sem("taylor"), TAYLOR)
                for m in range(4):
                    t = pe.transpose(banks[2][:, m * P:(m + 1) * P], EX[:, m, :], ident[:, :])
                t.then_inc(sem("exp_T"), 1)
                for k in range(SCALE_STEPS):
                    if k:
                        pe.wait_ge(sem("squared"), k)
                    pe.wait_ge(sem("squared_T"), k + 1)
                    for m in range(4):
                        t = pe.matmul(banks[1][:, m * P:(m + 1) * P], ET[:, m, :], EX[:, m, :], start=True, stop=True)
                    t.then_inc(sem("square"), 1)
                    for m in range(4):
                        t = pe.matmul(banks[2][:, m * P:(m + 1) * P], EX[:, m, :], ET[:, m, :], start=True, stop=True)
                    t.then_inc(sem("square_T"), 1)
                pe.wait_ge(sem("squared"), SCALE_STEPS)
                pe.wait_ge(sem("squared_T"), SCALE_STEPS + 1)
                pe.matmul(banks[1][:, 0:P], ET[:, 1, :], EX[:, 2, :], start=True, stop=True).then_inc(sem("rot23"), 1)
                pe.wait_ge(sem("rot23_copied"), 1)
                pe.matmul(banks[1][:, P:2 * P], ET[:, 0, :], R23[:, :], start=True, stop=True).then_inc(sem("rot"), 1)
                pe.wait_ge(sem("rot_copied"), 1)
                pe.wait_ge(sem("ew2T_copied"), 4)
                for q in range(E * K):
                    t = pe.matmul(banks[3 + q // 4][:, (q % 4) * P:(q % 4 + 1) * P], ew2T[:, q // K, q % K, :], Rall[:, :], start=True, stop=True)
                    if q % 4 == 3:
                        t.then_inc(sem("ew2_rotated"), 1)
                pe.wait_ge(sem("rows_copied"), 1)
                pe.matmul(banks[0][0:E, 0:P], eb2T[:, :], Rall[:, :], start=True, stop=True).then_inc(sem("eb2_rotated"), 1)
                pe.wait_ge(sem("scan_matrix"), 2)
                for i, m in enumerate((center, AbC)):
                    pe.matmul(banks[7][:, i * S:(i + 1) * S], bias_src[:, i, :], m[:, :], start=True, stop=True)
                for c in range(2):
                    t = pe.matmul(banks[7][:, 2 * S + c * S:2 * S + (c + 1) * S], pick[:, c, :], Mx[:, :], start=True, stop=True)
                t.then_inc(sem("scan_bias"), 1)

            @setup.scalar
            def _(act):
                act.wait_ge(sem("small_T"), 1)
                act.copy(gate_wT[:, :, :], banks[0][:, 0:2 * P].rearrange("p (j h) -> p j h", j=2))
                act.copy(BC_wT[:, :, :], banks[0][:, 2 * P:2 * P + 2 * S].rearrange("p (j h) -> p j h", j=2)).then_inc(sem("BC_T"), 1)
                act.wait_ge(sem("D_zero"), 1)
                act.copy(D_wT[0:S, 0, :], banks[0][0:S, 384:512])
                act.copy(D_wT[S:P, 1, :], banks[0][S:P, 384:512]).then_inc(sem("small_copied"), 1)
                act.wait_ge(sem("rows_all"), 1)
                act.copy(bcast[:, :], banks[7][:, 0:2 * P + E + 1 + 3 * S]).then_inc(sem("rows_copied_a"), 1)
                act.copy(eb1_col[:, :, :], banks[7][:, 480:480 + E * K].rearrange("p (e k) -> p e k", e=E))
                act.copy(eb2T[:, :], banks[7][:, 464:464 + E]).then_inc(sem("rows_copied"), 1)
                act.wait_ge(sem("rows_copied_a"), 1)
                act.mul(half_gc_b, bcast[:, 2 * P + E:2 * P + E + 1], 0.5).then_inc(sem("small_copied"), 1)
                for q in range(4):
                    act.wait_ge(sem("ew2_T"), q + 1)
                    act.copy(ew2T[:, 2 * q:2 * q + 2, :, :], banks[3 + q][:, :].rearrange("p (e k f) -> p e k f", e=2, k=K)).then_inc(sem("ew2T_copied"), 1)
                for k in range(SCALE_STEPS + 1):
                    if k == 0:
                        act.wait_ge(sem("exp_T"), 1)
                    else:
                        act.wait_ge(sem("square_T"), k)
                    act.copy(ET[:, :, :], banks[2][:, :].rearrange("p (m n) -> p m n", m=4)).then_inc(sem("squared_T"), 1)
                for q in range(4):
                    act.wait_ge(sem("ew2_rotated"), q + 1)
                    act.copy(ew2[:, 2 * q:2 * q + 2, :, :], banks[3 + q][:, :].rearrange("p (e k f) -> p e k f", e=2, k=K)).then_inc(sem("ew2r_ready"), 1)
                act.wait_ge(sem("eb2_rotated"), 1)
                act.copy(eb2r[:, :], banks[0][0:E, 0:P]).then_inc(sem("ew2r_ready"), 1)

            @setup.vector
            def _(dve):
                dve.memset(D_wT[:, :, :], 0.0).then_inc(sem("D_zero"), 1)
                dve.wait_ge(sem("ident_ready"), 1)
                dve.tensor_reduce(first_col[:, :], ident[:, 0:P:SEG], AX_X, ALU.add).then_inc(sem("first_col"), 1)
                for c in range(2):
                    dve.tensor_copy(pick[:, c, :].rearrange("k (a i) -> k a i", a=4),
                                    ident[0:S, 32 * c:32 * c + 32].unsqueeze(1).broadcast_to([S, 4, 32]))
                dve.tensor_scalar(center[:, :], ident[0:S, 0:S], -1.0 / S, None, ALU.add).then_inc(sem("center"), 1)
                dve.wait_ge(sem("weights_loaded"), 16 * N_W)
                dve.tensor_scalar(conv_w1, conv_w[:, 1:2], 1.0, None, ALU.add).then_inc(sem("center"), 1)
                dve.wait_ge(sem("ones_ready"), 1)
                dve.tensor_scalar(bias_src[:, 0, :], ones[0:S, :], col["B_b"][0:S], None, ALU.mult)
                dve.tensor_scalar(bias_src[:, 1, :], ones[0:S, :], col["ln_st_b"][0:S], None, ALU.mult)
                dve.tensor_copy(ones3[:, :], ones[0:3, :])
                x = bias_in[:, :, :]
                for j in range(2):
                    dve.tensor_copy(bias_part[:, j], x).then_inc(sem("bias_parts"), 1)
                    dve.wait_ge(sem("bias_parts"), 2 * j + 1)
                    dve.tensor_tensor(bias_rest[:, j], x, bias_part[:, j], ALU.subtract).then_inc(sem("bias_parts"), 1)
                    dve.wait_ge(sem("bias_parts"), 2 * j + 2)
                    x = bias_rest[:, j]
                dve.tensor_scalar(bias_mix[:, :, :], bias_part[:, 0], ident[0:3, 0:1], None, ALU.mult).then_inc(sem("bias_parts"), 1)
                dve.wait_ge(sem("bias_parts"), 5)
                dve.scalar_tensor_tensor(out=bias_low[:, :, :], in0=bias_part[:, 1], scalar=ident[0:3, 1:2], in1=bias_mix[:, :, :],
                                         op0=ALU.mult, op1=ALU.add).then_inc(sem("bias_parts"), 1)
                dve.wait_ge(sem("bias_parts"), 6)
                for i in range(3):
                    dve.scalar_tensor_tensor(out=bias3[:, i], in0=x[:, i, :].unsqueeze(1).broadcast_to([3, SUB, P]), scalar=ident[0:3, 2:3],
                                             in1=bias_low[:, i, :].unsqueeze(1).broadcast_to([3, SUB, P]), op0=ALU.mult, op1=ALU.add)
                dve.wait_ge(sem("expm_in"), 1)
                dve.wait_ge(sem("expm_zero"), 2)
                dve.tensor_copy(dt_col, banks[2][0:S, 0:1]).then_inc(sem("dt"), 1)
                half = 0.5 ** SCALE_STEPS
                dve.tensor_scalar(XE[:, 0:3, :], gens, half, None, ALU.mult)
                dve.tensor_scalar(XT[:, 0:3, :], banks[1][:, 0:384].rearrange("p (m n) -> p m n", m=3), half, None, ALU.mult)
                dve.wait_ge(sem("dt"), 1)
                dve.tensor_scalar(XE[0:S, 3, 0:S], A_in, dt_col, half, ALU.mult, ALU.mult)
                dve.tensor_scalar(XT[0:S, 3, 0:S], banks[1][0:S, 384:384 + S], dt_col, half, ALU.mult, ALU.mult).then_inc(sem("expm_arg"), 1)
                dve.wait_ge(sem("expm_arg"), 1)
                dve.scalar_tensor_tensor(out=EX, in0=XE, scalar=1.0 / TAYLOR, in1=ident4, op0=ALU.mult, op1=ALU.add).then_inc(sem("taylor"), 1)
                for k in range(TAYLOR - 1, 0, -1):
                    dve.wait_ge(sem("taylor_product"), TAYLOR - k)
                    dve.scalar_tensor_tensor(out=EX, in0=banks[1][:, :].rearrange("p (m n) -> p m n", m=4), scalar=1.0 / k, in1=ident4,
                                             op0=ALU.mult, op1=ALU.add).then_inc(sem("taylor"), 1)
                for k in range(SCALE_STEPS):
                    dve.wait_ge(sem("square_T"), k + 1)
                    dve.tensor_copy(EX, banks[1][:, :].rearrange("p (m n) -> p m n", m=4)).then_inc(sem("squared"), 1)
                dve.wait_ge(sem("squared"), SCALE_STEPS)
                dve.tensor_reduce(row_mean[0:S], EX[0:S, 3, 0:S], AX_X, ALU.add).then_inc(sem("row_sum"), 1)
                dve.wait_ge(sem("row_sum"), 1)
                dve.tensor_scalar(row_mean[0:S], row_mean[0:S], 1.0 / S, None, ALU.mult).then_inc(sem("row_sum"), 1)
                dve.wait_ge(sem("row_sum"), 2)
                dve.tensor_scalar(AbC[:, :], EX[0:S, 3, 0:S], row_mean[0:S], None, ALU.subtract).then_inc(sem("scan_matrix"), 1)
                dve.wait_ge(sem("scan_matrix"), 1)
                dve.tensor_scalar(Mx[:, :], AbC[:, :], col["ln_st_g"][0:S], RSQRT_FACTOR, ALU.mult, ALU.mult).then_inc(sem("scan_matrix"), 1)
                dve.wait_ge(sem("rot23"), 1)
                dve.tensor_copy(R23[:, :], banks[1][:, 0:P]).then_inc(sem("rot23_copied"), 1)
                dve.wait_ge(sem("rot"), 1)
                dve.tensor_copy(Rall[:, :], banks[1][:, P:2 * P]).then_inc(sem("rot_copied"), 1)
                dve.wait_ge(sem("BC_T"), 1)
                dve.tensor_reduce(row_mean_b, BC_wT[:, 0, :], AX_X, ALU.add).then_inc(sem("row_sum_b"), 1)
                dve.wait_ge(sem("row_sum_b"), 1)
                dve.tensor_scalar(row_mean_b, row_mean_b, 1.0 / S, None, ALU.mult).then_inc(sem("row_sum_b"), 1)
                dve.wait_ge(sem("row_sum_b"), 2)
                dve.tensor_scalar(BC_wT[:, 0, :], BC_wT[:, 0, :], row_mean_b, None, ALU.subtract)
                dve.wait_ge(sem("scan_bias"), 1)
                dve.tensor_copy(Mrep[:, :, :], banks[7][:, 2 * S:4 * S].rearrange("p (c n) -> p c n", c=2))
                dve.tensor_copy(bias_all[:, 0:2, :], banks[7][:, 0:2 * S].rearrange("p (c n) -> p c n", c=2)).then_inc(sem("bias_copied"), 1)
                dve.wait_ge(sem("bias_copied"), 1)
                dve.tensor_tensor(bias_all[:, 2, :], bias_all[:, 0, :], bias_all[:, 1, :], ALU.add)
                dve.wait_ge(sem("x_loaded"), 16 * NB)
                for s in range(NS):
                    t = dve.bn_stats(st[:, s, :], X[:, s, :])
                t.then_inc(sem("stats"), 1)


        mean, var, r1, nm1, rz, nmz, tmp, tmp2 = (lnv[:, i, :] for i in range(8))
        with nc.Block() as block:

            @block.vector
            def _(dve):
                dve.tensor_tensor(mean, st[:, :, 1], st[:, :, 4], ALU.add)
                dve.tensor_tensor(tmp, st[:, :, 1], st[:, :, 4], ALU.subtract)
                dve.tensor_tensor(var, st[:, :, 2], st[:, :, 5], ALU.add).then_inc(sem("ln_a"), 1)
                dve.wait_ge(sem("ln_a"), 1)
                dve.tensor_tensor(tmp2, tmp, tmp, ALU.mult)
                dve.tensor_scalar(mean, mean, 0.5, None, ALU.mult)
                dve.tensor_scalar(var, var, 1.0 / H, None, ALU.mult).then_inc(sem("ln_a"), 1)
                dve.wait_ge(sem("ln_a"), 2)
                dve.scalar_tensor_tensor(out=var, in0=tmp2, scalar=0.25, in1=var, op0=ALU.mult, op1=ALU.add).then_inc(sem("var_ready"), 1)
                dve.wait_ge(sem("std_ready"), 1)
                dve.reciprocal(r1, tmp).then_inc(sem("ln_a"), 1)
                dve.wait_ge(sem("ln_a"), 3)
                dve.tensor_tensor(tmp2, r1, r1, ALU.mult).then_inc(sem("ln_a"), 1)
                dve.wait_ge(sem("ln_a"), 4)
                dve.tensor_tensor(tmp2, tmp2, var, ALU.mult).then_inc(sem("var_ready"), 1)
                dve.scalar_tensor_tensor(out=nm1, in0=mean, scalar=-1.0, in1=r1, op0=ALU.mult, op1=ALU.mult)
                dve.wait_ge(sem("std_ready"), 2)
                dve.reciprocal(rz, tmp).then_inc(sem("ln_a"), 1)
                dve.wait_ge(sem("ln_a"), 5)
                dve.tensor_tensor(rz, rz, r1, ALU.mult).then_inc(sem("ln_a"), 1)
                dve.wait_ge(sem("ln_a"), 6)
                dve.scalar_tensor_tensor(out=nmz, in0=mean, scalar=-1.0, in1=rz, op0=ALU.mult, op1=ALU.mult).then_inc(sem("ln_a"), 1)
                dve.wait_ge(sem("ln_a"), 7)
                with dve.Fori(0, NB // 2) as i:
                    for u in range(2):
                        n = i * 2 + u
                        dve.wait_ge(sem("zT_free"), n + 1)
                        for s in range(SUB):
                            q = n * SUB + s
                            t = dve.tensor_scalar(zbuf[:, u, s, :], X[:, ds(q, 1), :], rz[:, ds(q, 1)], nmz[:, ds(q, 1)], ALU.mult, ALU.add)
                        t.then_inc(sem("z_ready"), 1)
                dve.wait_ge(sem("edges"), 4)
                with dve.Fori(0, NB) as n:
                    o = xaT[:, ds(n, 1), :].squeeze(1).rearrange("p (k n) -> p k n", k=SUB)
                    dve.tensor_scalar(o, xpad[:, ds(n * SUB + 1, SUB), :], conv_w1, col["conv_b"], ALU.mult, ALU.add).then_inc(sem("conv0"), 1)
                    dve.wait_ge(sem("conv0"), n + 1)
                    dve.scalar_tensor_tensor(out=o, in0=xpad[:, ds(n * SUB, SUB), :], scalar=conv_w[:, 0:1], in1=o, op0=ALU.mult, op1=ALU.add).then_inc(sem("conv1"), 1)
                    dve.wait_ge(sem("conv1"), n + 1)
                    dve.scalar_tensor_tensor(out=o, in0=xpad[:, ds(n * SUB + 2, SUB), :], scalar=conv_w[:, 2:3], in1=o, op0=ALU.mult, op1=ALU.add).then_inc(sem("conv"), 1)
                dve.wait_ge(sem("conv"), NB)
                with dve.Fori(0, NB) as n:
                    dve.wait_ge(sem("gate_free"), n + 3)
                    dve.tensor_tensor(gi[:, ds(n, 1), :], xaT[:, ds(n, 1), :], gi[:, ds(n, 1), :], ALU.mult).then_inc(sem("gated"), 1)
                for g in range(4):
                    dve.wait_ge(sem("B_proj"), g + 1)
                    t = dve.tensor_tensor(Dv[:, g * 8:g * 8 + 8, 0:S], banks[6 + g % 2][:, :].rearrange("p (k n) -> p k n", n=S),
                                          bias_all[:, 2, :].unsqueeze(1).broadcast_to([P, 8, S]), ALU.add).then_inc(sem("B_copied"), 1)
                dve.wait_ge(sem("B_copied"), 1)
                dve.tensor_scalar(bias_all[:, 1, :], bias_all[:, 1, :], first_col[:, :], None, ALU.mult).then_inc(sem("first_bias"), 1)
                dve.wait_ge(sem("first_bias"), 1)
                dve.tensor_tensor(Dv[:, 0, 0:S], Dv[:, 0, 0:S], bias_all[:, 1, :], ALU.subtract)
                for g in range(4):
                    dve.wait_ge(sem("C_proj"), g + 1)
                    dve.tensor_tensor(CL[:, g * 8:g * 8 + 8, :], banks[4 + g % 2][:, :].rearrange("p (k n) -> p k n", n=S),
                                      C_b_all.unsqueeze(1).broadcast_to([P, 8, S]), ALU.add).then_inc(sem("C_copied"), 1)
                dve.wait_ge(sem("C_copied"), 4)
                dve.scalar_tensor_tensor(out=gC[:, :, :], in0=CL, scalar=RSQRT_FACTOR, in1=st_g_all.unsqueeze(1).broadcast_to([P, L, S]),
                                         op0=ALU.mult, op1=ALU.mult)
                dve.tensor_tensor(bC[:, :, :], CL, st_b_all.unsqueeze(1).broadcast_to([P, L, S]), ALU.mult)

            @block.gpsimd
            def _(pool):
                pool.wait_ge(sem("affine"), NB)
                pool.tensor_copy(xpad[:, 0, 1:P], xpad[:, L, 0:P - 1]).then_inc(sem("edges"), 1)
                pool.wait_ge(sem("edges"), 1)
                pool.memset(xpad[:, 0, 0:P:SEG], 0.0).then_inc(sem("edges"), 1)
                pool.tensor_copy(xpad[:, L + 1, 0:P - 1], xpad[:, 1, 1:P]).then_inc(sem("edges"), 1)
                pool.wait_ge(sem("edges"), 3)
                pool.memset(xpad[:, L + 1, SEG - 1:P:SEG], 0.0).then_inc(sem("edges"), 1)

            @block.tensor
            def _(pe):
                with pe.Fori(0, NB // 2) as i:
                    for u in range(2):
                        n = i * 2 + u
                        pe.wait_ge(sem("z_ready"), n + 1)
                        pe.wait_ge(sem("zT_free"), n + 1)
                        for s in range(SUB):
                            t = pe.transpose(banks[u][:, s * P:(s + 1) * P], zbuf[:, u, s, :], ident[:, :])
                        t.then_inc(sem("zT"), 1)
                with pe.Fori(0, NB // 2) as i:
                    for u in range(2):
                        n = i * 2 + u
                        pe.wait_ge(sem("conv"), n + 1)
                        pe.wait_ge(sem("gate_free"), n + 1)
                        pe.matmul(banks[2 + u][:, :], gate_wT[:, 1, :], xaT[:, ds(n, 1), :].squeeze(1), start=True, stop=True).then_inc(sem("gate_in"), 1)
                for g in range(4):
                    pe.wait_ge(sem("gated"), 2 * g + 2)
                    if g >= 2:
                        pe.wait_ge(sem("B_copied"), g - 1)
                    for k in range(8):
                        x = gi[:, 2 * g + k // 4, (k % 4) * P:(k % 4 + 1) * P]
                        t = pe.matmul(banks[6 + g % 2][:, k * S:(k + 1) * S], x, BC_wT[:, 0, :], start=True, stop=True)
                    t.then_inc(sem("B_proj"), 1)
                for g in range(4):
                    if g >= 2:
                        pe.wait_ge(sem("C_copied"), g - 1)
                    for k in range(8):
                        x = xaT[:, 2 * g + k // 4, (k % 4) * P:(k % 4 + 1) * P]
                        t = pe.matmul(banks[4 + g % 2][:, k * S:(k + 1) * S], x, BC_wT[:, 1, :], start=True, stop=True)
                    t.then_inc(sem("C_proj"), 1)

            @block.scalar
            def _(act):
                act.sem_inc(sem("zT_free"), 2)
                act.sem_inc(sem("gate_free"), 2)
                act.wait_ge(sem("var_ready"), 1)
                act.activation(tmp, var, ACT.Sqrt, bias=eps_col[:, :]).then_inc(sem("std_ready"), 1)
                act.wait_ge(sem("var_ready"), 2)
                act.activation(tmp, tmp2, ACT.Sqrt, bias=eps_col[:, :]).then_inc(sem("std_ready"), 1)
                with act.Fori(0, NB // 2) as i:
                    for u in range(2):
                        n = i * 2 + u
                        act.wait_ge(sem("zT"), n + 1)
                        act.activation(xpad[:, ds(n * SUB + 1, SUB), :], banks[u][:, :].rearrange("p (k n) -> p k n", k=SUB), ACT.Identity, bias=col["ln_in_b"],
                                       scale=col["ln_in_g"]).then_inc(sem("affine"), 1)
                        act.activation(xfT[:, ds(n, 1), :], banks[u][:, :].unsqueeze(1), ACT.Identity, bias=col["ln_beta"],
                                       scale=col["ln_gamma"]).then_inc(sem("zT_free"), 1)
                with act.Fori(0, NB // 2) as i:
                    for u in range(2):
                        n = i * 2 + u
                        act.wait_ge(sem("gate_in"), n + 1)
                        act.activation(gi[:, ds(n, 1), :], banks[2 + u][:, :].unsqueeze(1), ACT.Sigmoid, bias=col["gate_b_in"])\
                           .then_inc(sem("gate_free"), 1)

        lg = sb("lg", [P, NS, E])
        oh1 = sb("oh1", [P, NS, E])
        oh2 = sb("oh2", [P, NS, E])
        wd = sb("wd", [P, NS, E])
        top = sb("top", [P, 7, NS])
        m1, m2, r_1, r_2, tw, w1, w2 = (top[:, i, :] for i in range(7))
        wdT_all = sb("wdT_all", [E, NS, P])

        def per_expert(ap):
            return ap.unsqueeze(2).broadcast_to([P, NS, E])

        with nc.Block() as block:
            @block.tensor
            def _(pe):
                pe.wait_ge(sem("ffn_loaded"), 48)
                for q in range(NS):
                    x = xfT[:, q // SUB, (q % SUB) * P:(q % SUB + 1) * P]
                    t = pe.matmul(banks[0][:, q * E:(q + 1) * E], x, router_w[:, :], start=True, stop=True)
                t.then_inc(sem("router"), 1)
                pe.wait_ge(sem("weights"), 1)
                for q in range(NS):
                    t = pe.transpose(banks[q // SUB][0:E, (q % SUB) * P:(q % SUB + 1) * P], wd[:, q, :], ident[:, :])
                    if q % SUB == SUB - 1:
                        t.then_inc(sem("weights_T"), 1)

            @block.scalar
            def _(act):
                act.wait_ge(sem("margin"), 1)
                act.activation(tw, w1, ACT.Tanh, scale=0.5).then_inc(sem("margin_tanh"), 1)
                for n in range(NB):
                    act.wait_ge(sem("weights_T"), n + 1)
                    act.copy(wdT_all[:, n * SUB:(n + 1) * SUB, :], banks[n][0:E, :].rearrange("p (s h) -> p s h", s=SUB))

            @block.vector
            def _(dve):
                def step(ins, name):
                    ins.then_inc(sem(name), 1)
                    dve.wait_ge(sem(name), 1)

                def largest(logits, m, r, onehot, tag):
                    step(dve.tensor_reduce(m, logits, AX_X, ALU.max), "top" + tag)
                    step(dve.tensor_tensor(onehot, logits, per_expert(m), ALU.is_equal), "equal" + tag)
                    step(dve.tensor_tensor(onehot, onehot, rank[:, :, :], ALU.mult), "ranked" + tag)
                    step(dve.tensor_reduce(r, onehot, AX_X, ALU.max), "first" + tag)
                    step(dve.tensor_tensor(onehot, rank[:, :, :], per_expert(r), ALU.is_equal), "onehot" + tag)

                dve.wait_ge(sem("router"), 1)
                step(dve.tensor_tensor(lg[:, :, :], banks[0][:, 0:NS * E].rearrange("p (s e) -> p s e", s=NS),
                                       mgb_all.unsqueeze(1).broadcast_to([P, NS, E]), ALU.add), "logits")
                largest(lg[:, :, :], m1, r_1, oh1[:, :, :], "1")
                step(dve.scalar_tensor_tensor(out=wd[:, :, :], in0=oh1[:, :, :], scalar=-3e38, in1=lg[:, :, :], op0=ALU.mult, op1=ALU.add), "rest")
                largest(wd[:, :, :], m2, r_2, oh2[:, :, :], "2")
                dve.tensor_tensor(w1, m1, m2, ALU.subtract).then_inc(sem("margin"), 1)
                dve.wait_ge(sem("margin_tanh"), 1)
                dve.tensor_scalar(w1, tw, 0.5, 0.5, ALU.mult, ALU.add)
                step(dve.tensor_scalar(w2, tw, -0.5, 0.5, ALU.mult, ALU.add), "pair")
                dve.tensor_tensor(oh1[:, :, :], oh1[:, :, :], per_expert(w1), ALU.mult)
                step(dve.tensor_tensor(oh2[:, :, :], oh2[:, :, :], per_expert(w2), ALU.mult), "weighted")
                dve.tensor_tensor(wd[:, :, :], oh1[:, :, :], oh2[:, :, :], ALU.add).then_inc(sem("weights"), 1)

        FFN_ROUNDS = 4
        TILE_STEPS = FFN_ROUNDS * L // NB
        TPR = NB // FFN_ROUNDS
        assert TILE_STEPS % UNROLL == 0 and TILE_STEPS == 2 * E
        ring = sb("ring", [P, UNROLL, S])
        rs = sb("rs", [P, UNROLL])
        wT = sb("wT", [P, S])
        qv = sb("qv", [P, 6])
        q_now, y_steps, z_steps = qv[:, 0:1], [qv[:, 1:2], qv[:, 2:3]], [qv[:, 3:4], qv[:, 4:5], qv[:, 5:6]]
        sqj = sb("sqj", [P, S])
        d_now = sb("d_now", [P, 2, S])
        ends = sb("ends", [P, 2, S])
        start_now = sb("start_now", [P, S])
        start_old = sb("start_old", [P, S])
        drift = sb("drift", [P, 1])
        drift1 = sb("drift1", [1, 1])
        agreed = sb("agreed", [1, 1], mybir.dt.int32)
        HALF = UNROLL // 2
        PER = L + 1
        psY, psS, psF = banks[0][:, 0:S], banks[0][:, S:3 * S], banks[0][0:1, 3 * S:3 * S + P]
        last = ring[:, UNROLL - 1, :]

        def rsqrt(dve, y_out, count, during=lambda i: None):
            q = q_now
            y0, y1 = y_steps
            z0, z1, z2 = z_steps
            I32 = mybir.dt.int32

            def step(ins, i):
                ins.then_inc(sem(f"root_{i}"), 1)
                during(i)
                dve.wait_ge(sem(f"root_{i}"), count)

            step(dve.tensor_scalar(y0.bitcast(I32), q.bitcast(I32), -0.5, RSQRT_MAGIC, ALU.mult, ALU.add), 1)
            step(dve.scalar_tensor_tensor(out=z0, in0=y0, scalar=y0, in1=q, op0=ALU.mult, op1=ALU.mult), 2)
            step(dve.scalar_tensor_tensor(out=z1, in0=z0, scalar=-10.0 / 3.0, in1=z0, op0=ALU.add, op1=ALU.mult), 3)
            step(dve.scalar_tensor_tensor(out=y1, in0=z1, scalar=5.0, in1=y0, op0=ALU.add, op1=ALU.mult), 4)
            step(dve.scalar_tensor_tensor(out=z2, in0=y1, scalar=y1, in1=q, op0=ALU.mult, op1=ALU.mult), 5)
            step(dve.scalar_tensor_tensor(out=y_out, in0=z2, scalar=-64.0 / 3.0, in1=y1, op0=ALU.add, op1=ALU.mult), 6)

        def vector_steps(dve, r, k0, count, store, between=None):
            for i in range(count):
                k = k0 + i
                u = i % UNROLL
                turn = r * PER + k + 1
                prev = ring[:, (u - 1) % UNROLL, :]
                dve.wait_ge(sem("state"), turn)
                dve.tensor_tensor_reduce(sqj[:, :], prev, prev, 1.0 / S, EPS, ALU.mult, ALU.add, q_now).then_inc(sem("norm"), 1)
                dve.transpose(wT[:, :], prev).then_inc(sem("state_T"), 1)
                if between:
                    between(i)
                dve.wait_ge(sem("norm"), turn)
                if store and u % HALF == 0:
                    dve.wait_ge(sem("stored"), (r - FFN_ROUNDS) * (2 * L // HALF) + (k0 // HALF) * 2 + 2 * (i // HALF) + 2)

                def during(j):
                    if j == 1:
                        dve.tensor_copy(d_now[:, u % 2, :], Dv[:, ds(k, 1), :].squeeze(1))

                rsqrt(dve, rs[:, u:u + 1], turn, during)
                dve.wait_ge(sem("product"), turn)
                dve.scalar_tensor_tensor(out=ring[:, u, :], in0=psY, scalar=rs[:, u:u + 1], in1=d_now[:, u % 2, :],
                                         op0=ALU.mult, op1=ALU.add).then_inc(sem("state"), 1)

        def vector_boundary(dve, r, store):
            dve.wait_ge(sem("state"), r * PER + L + 1)
            dve.tensor_tensor_reduce(sqj[:, :], last, last, 1.0 / S, EPS, ALU.mult, ALU.add, q_now).then_inc(sem("norm"), 1)
            dve.tensor_copy(ends[:, 0, :], last)
            dve.tensor_copy(start_old[:, :], start_now[:, :])
            dve.wait_ge(sem("norm"), r * PER + L + 1)
            rsqrt(dve, Rho[:, L:L + 1], r * PER + L + 1)
            dve.tensor_scalar(ends[:, 1, :], last, Rho[:, L:L + 1], None, ALU.mult).then_inc(sem("state_T"), 1)
            dve.wait_ge(sem("product"), r * PER + L + 1)
            if store:
                dve.wait_ge(sem("stored"), (r + 1 - FFN_ROUNDS) * (2 * L // HALF) + 4)
            dve.tensor_copy(start_now[:, :], psS[:, S:2 * S]).then_inc(sem("new_start"), 1)
            dve.tensor_copy(last, psS[:, 0:S]).then_inc(sem("state"), 1)

        def tensor_step(pe, n):
            pe.wait_ge(sem("state_T"), n + 1)
            pe.sem_inc(sem("tick"), 1)
            for c in range(2):
                for a in range(4):
                    q = slice(32 * a, 32 * a + 32)
                    t = pe.matmul(psY[q], wT[q, 32 * c:32 * c + 32], Mrep[q, c, :], start=(c == 0), stop=(c == 1))
            t.then_inc(sem("product"), 1)

        def tensor_boundary(pe, r):
            pe.wait_ge(sem("state_T"), r * PER + L + 1)
            pe.matmul(psS, shift[:, :], ends[:, :, :].rearrange("p a s -> p (a s)"), start=True, stop=True).then_inc(sem("product"), 1)

        def vector_round(dve, r):
            with dve.Fori(0, L // UNROLL) as j:
                vector_steps(dve, r, j * UNROLL, UNROLL, True)
            vector_boundary(dve, r, True)

        def tensor_round(pe, r):
            with pe.Fori(0, L // UNROLL) as j:
                for u in range(UNROLL):
                    tensor_step(pe, r * PER + j * UNROLL + u)
            tensor_boundary(pe, r)

        def pool_round(pool, r):
            with pool.Fori(0, L // UNROLL) as j:
                for h in range(2):
                    at = j * UNROLL + h * HALF
                    part = slice(h * HALF, (h + 1) * HALF)
                    pool.wait_ge(sem("state"), r * PER + j * UNROLL + (h + 1) * HALF + 1)
                    pool.tensor_copy(Wst[:, ds(at, HALF), :], ring[:, part, :]).then_inc(sem("stored"), 1)
                    pool.tensor_copy(Rho[:, ds(at, HALF)], rs[:, part]).then_inc(sem("stored"), 1)

        def rounds(eng, one_round):
            with eng.Fori(FFN_ROUNDS, ROUNDS) as r:
                one_round(eng, r)
            if one_round is vector_round:
                eng.wait_ge(sem("new_start"), ROUNDS)
                eng.tensor_tensor(sqj[:, :], start_now[:, :], start_old[:, :], ALU.subtract).then_inc(sem("drift"), 1)
                eng.wait_ge(sem("drift"), 1)
                eng.tensor_reduce(drift[:, 0:1], sqj[:, :], AX_X, ALU.max, apply_absolute_value=True).then_inc(sem("drift_col"), 1)
                eng.wait_ge(sem("drift_row"), 1)
                eng.tensor_reduce(drift1[:, 0:1], psF, AX_X, ALU.max).then_inc(sem("drift"), 1)
                eng.wait_ge(sem("drift"), 2)
                eng.tensor_scalar(agreed[:, :], drift1[:, 0:1], TOLERANCE / abs(RSQRT_FACTOR), None, ALU.is_le).then_inc(sem("agreed"), 1)
            if one_round is tensor_round:
                eng.wait_ge(sem("drift_col"), 1)
                eng.transpose(psF, drift[:, 0:1], ident[:, :]).then_inc(sem("drift_row"), 1)
            eng.wait_ge(sem("agreed"), 1)
            settled = eng.value_load(agreed[0:1, 0:1], min_val=0, max_val=1)
            with eng.If(settled < 1):
                with eng.Fori(ROUNDS, SEG) as r:
                    one_round(eng, r)
            eng.end_ifs()

        fx = xpad[:, :, :].rearrange("p a b -> p (a b)")[:, 0:4096]

        def buf(i):
            return fx[:, i * 512:(i + 1) * 512].rearrange("p (s h) -> p s h", s=SUB)

        abel, gate_t, silu_t, acc, diff, base, sc0, sc1 = (buf(i) for i in range(8))
        scaled = [sc0, sc1]
        pulled = sb("pulled", [P, SUB, P])
        hT = sb("hT", [P, 2, K, T])
        xf_cur, xa_cur = zbuf[:, 0], zbuf[:, 1]
        wdT_cur = sb("wdT_cur", [E, SUB, P])
        dots = sb("dots", [P, 4, SUB])
        dot_a, dot_d, gc, gg = (dots[:, i] for i in range(4))
        gc_w_sum = sb("gc_w_sum", [P, P])
        junk = sb("junk", [P, 2, P])
        factor = gi_all[:, :, :].rearrange("p b (s h) -> p (b s) h", s=SUB)
        bH = banks[1:5]
        bE = banks[5:7]
        bR = banks[7]
        bR4 = bR[:, :].rearrange("p (s h) -> p s h", s=SUB)

        def vector_dot(dve, x, w, o, s, name):
            dve.tensor_tensor_reduce(junk[:, s % 2, :], x[:, s, :], w, 1.0, 0.0, ALU.mult, ALU.add, o[:, s:s + 1]).then_inc(sem(name), 1)

        def vector_mix(dve, n, s):
            if s == 0:
                dve.wait_ge(sem("difference"), n)
            if s in (2, 3):
                dve.wait_ge(sem("dot_moe"), n * SUB + s - 1)
            if s < SUB:
                vector_dot(dve, diff, gc_w_all[:, P:2 * P], dot_d, s, "dot_moe")
            else:
                dve.wait_ge(sem("dot_moe"), (n + 1) * SUB)
                dve.wait_ge(sem("dot_abel"), n * SUB)
                dve.tensor_tensor(gc, dot_a, dot_d, ALU.add).then_inc(sem("mix_dot"), 1)

        def scalar_mix(act, n, part):
            if part == 0:
                act.wait_ge(sem("mix_dot"), n + 1)
                act.activation(gg, gc, ACT.Tanh, scale=0.5, bias=half_gc_b).then_inc(sem("mix_tanh"), 1)
                act.wait_ge(sem("mix_tanh"), n + 1)
                act.activation(gg, gg, ACT.Copy, scale=0.5, bias=0.5).then_inc(sem("mix_gate"), 1)
                act.wait_ge(sem("mix_gate"), n + 1)
                for s in range(SUB):
                    t = act.activation(pulled[:, s, :], diff[:, s, :], ACT.Copy, scale=gg[:, s:s + 1])
                t.then_inc(sem("pulled"), 1)
            else:
                act.wait_ge(sem("ffn"), n + 1)
                act.activation(silu_t, base, ACT.Tanh, scale=0.5).then_inc(sem("silu_tanh"), 1)

        def pool_mix(pool, n, part):
            if part == 0:
                pool.wait_ge(sem("pulled"), n + 1)
                pool.wait_ge(sem("base"), n)
                pool.tensor_tensor(base, base, pulled[:, :, :], ALU.add).then_inc(sem("ffn"), 1)
            elif part == 1:
                pool.wait_ge(sem("silu_tanh"), n + 1)
                pool.tensor_tensor(silu_t, silu_t, base, ALU.mult).then_inc(sem("silu_product"), 1)
            elif part == 2:
                pool.wait_ge(sem("silu_product"), n + 1)
                pool.tensor_tensor(base, silu_t, base, ALU.add).then_inc(sem("silu"), 1)
            elif part == 3:
                pool.wait_ge(sem("silu"), n + 1)
                pool.wait_ge(sem("gate"), n + 1)
                pool.tensor_tensor(gate_t, gate_t, base, ALU.mult).then_inc(sem("gate_product"), 1)
            else:
                pool.wait_ge(sem("gate_product"), n + 1)
                pool.tensor_tensor(factor[:, ds(n * SUB, SUB), :], gate_t, base, ALU.add).then_inc(sem("mixed"), 1)

        with nc.Block() as block:
            @block.sync
            def _(sp):
                for n in range(NB):
                    if n:
                        sp.wait_ge(sem("expert_bias"), n)
                        sp.wait_ge(sem("abel_pre"), n)
                        sp.wait_ge(sem("gate_pre"), n)
                    sp.dma_start(wdT_cur[:, :, :], wdT_all[:, n * SUB:(n + 1) * SUB, :]).then_inc(sem("wdT_cur"), 16)
                    sp.dma_start(xf_cur.rearrange("p s h -> p (s h)"), xfT[:, n, :]).then_inc(sem("xf_cur"), 16)
                    sp.dma_start(xa_cur.rearrange("p s h -> p (s h)"), xaT[:, n, :]).then_inc(sem("xa_cur"), 16)

            @block.tensor
            def _(pe):
                with pe.Fori(0, FFN_ROUNDS) as r:
                    with pe.Fori(0, TPR) as t_:
                        n = r * TPR + t_
                        xf = xfT[:, ds(n, 1), :].squeeze(1)

                        def layer1(e):
                            pe.wait_ge(sem("hidden"), n * E + e + 1)
                            for k in range(K):
                                t = pe.matmul(bH[(e % 2) * 2 + k][:, :], ew1[:, e, k * P:(k + 1) * P], xf, start=True, stop=True)
                            t.then_inc(sem("pre_hidden"), 1)

                        def layer2(e):
                            pe.wait_ge(sem("hidden"), n * E + e + 3)
                            pe.wait_ge(sem("scaled"), n * E + e + 1)
                            for s in range(SUB):
                                for k in range(K):
                                    t = pe.matmul(bE[e % 2][:, s * P:(s + 1) * P], hT[:, e % 2, k, s * P:(s + 1) * P], ew2[:, e, k, :],
                                                  start=(k == 0), stop=(k == K - 1))
                            t.then_inc(sem("expert_out"), 1)

                        def row_product(x, w, bias, name):
                            pe.matmul(bR[:, :], ones3[:, :], bias, start=True, stop=False)
                            for s in range(SUB):
                                t = pe.matmul(bR[:, s * P:(s + 1) * P], x[:, s, :], w, start=False, stop=(s == SUB - 1))
                            t.then_inc(sem(name), 1)

                        def experts_bias():
                            pe.wait_ge(sem("wdT_cur"), 16 * (n + 1))
                            pe.wait_ge(sem("gate"), n + 1)
                            for s in range(SUB):
                                t = pe.matmul(bR[:, s * P:(s + 1) * P], wdT_cur[:, s, :], eb2r[:, :], start=True, stop=True)
                            t.then_inc(sem("expert_bias"), 1)

                        def abel_pre():
                            pe.wait_ge(sem("xf_cur"), 16 * (n + 1))
                            pe.wait_ge(sem("sum_started"), n + 1)
                            row_product(xf_cur, abel_w[:, :], abel_b3, "abel_pre")

                        def gate_pre():
                            pe.wait_ge(sem("xa_cur"), 16 * (n + 1))
                            pe.wait_ge(sem("abel"), n + 1)
                            row_product(xa_cur, gate_wT[:, 0, :], gate_b3, "gate_pre")

                        layer1(0)
                        for i in range(TILE_STEPS):
                            tensor_step(pe, r * PER + t_ * TILE_STEPS + i)
                            if i % 2:
                                if i < TILE_STEPS - 1:
                                    layer2(i // 2)
                            elif i < TILE_STEPS - 2:
                                layer1(i // 2 + 1)
                            else:
                                layer2(E - 1)
                            if i == 0:
                                experts_bias()
                            if i == 7:
                                abel_pre()
                            if i == TILE_STEPS - 1:
                                gate_pre()
                    tensor_boundary(pe, r)
                rounds(pe, tensor_round)

            @block.scalar
            def _(act):
                act.sem_inc(sem("hidden"), 2)
                act.sem_inc(sem("scaled"), 2)
                act.sem_inc(sem("gate"), 1)
                act.activation(junk_col[:, :], eps_col[:, :], ACT.Gelu)
                with act.Fori(0, NB) as n:
                    def gelus(e):
                        act.wait_ge(sem("pre_hidden"), n * E + e + 1)
                        if e >= 2:
                            act.wait_ge(sem("expert_out"), n * E + e - 1)
                        else:
                            act.wait_ge(sem("expert_out_seen"), n * E + e + 1)
                        for k in range(K):
                            t = act.activation(hT[:, e % 2, k, :], bH[(e % 2) * 2 + k][:, :], ACT.Gelu, bias=eb1_col[:, e, k:k + 1])
                        t.then_inc(sem("hidden"), 1)

                    def scale(e):
                        act.wait_ge(sem("expert_out"), n * E + e + 1)
                        act.wait_ge(sem("added"), n * E + e + 1)
                        for s in range(SUB):
                            w = wd[:, ds(n * SUB + s, 1), e:e + 1].squeeze(1)
                            t = act.activation(scaled[e % 2][:, s, :], bE[e % 2][:, s * P:(s + 1) * P], ACT.Copy, scale=w)
                        t.then_inc(sem("scaled"), 1)
                        act.sem_inc(sem("expert_out_seen"), 1)

                    gelus(0)
                    gelus(1)
                    act.wait_ge(sem("expert_bias"), n + 1)
                    act.wait_ge(sem("difference"), n)
                    act.copy(acc, bR4).then_inc(sem("sum_started"), 1)
                    scale(0)
                    gelus(2)
                    scale(1)
                    gelus(3)
                    scale(2)
                    gelus(4)
                    scalar_mix(act, n, 0)
                    act.wait_ge(sem("abel_pre"), n + 1)
                    act.wait_ge(sem("dot_abel"), n * SUB)
                    act.wait_ge(sem("base"), n)
                    act.activation(abel, bR4, ACT.Gelu).then_inc(sem("abel"), 1)
                    scale(3)
                    gelus(5)
                    scale(4)
                    scalar_mix(act, n, 1)
                    gelus(6)
                    scale(5)
                    gelus(7)
                    scale(6)
                    act.wait_ge(sem("mixed"), n + 1)
                    for s in range(SUB):
                        q = n * SUB + s
                        t = act.activation(base[:, s, :], X[:, ds(q, 1), :].squeeze(1), ACT.Identity, scale=r1[:, ds(q, 1)], bias=nm1[:, ds(q, 1)])
                    t.then_inc(sem("residual"), 1)
                    act.wait_ge(sem("gate_pre"), n + 1)
                    act.activation(gate_t, bR4, ACT.Tanh, scale=0.5).then_inc(sem("gate"), 1)
                    scale(7)
                scalar_mix(act, NB, 0)
                scalar_mix(act, NB, 1)
                act.wait_ge(sem("agreed"), 1)

            @block.vector
            def _(dve):
                dve.memset(start_now[:, :], 0.0)
                for b in (diff, base, gate_t, dots[:, :, :]):
                    dve.memset(b, 0.0).then_inc(sem("mix_zero"), 1)
                dve.tensor_tensor(gc_w_sum[:, :], gc_w_all[:, 0:P], gc_w_all[:, P:2 * P], ALU.add).then_inc(sem("gc_sum"), 1)
                dve.wait_ge(sem("mix_zero"), 4)
                dve.wait_ge(sem("gc_sum"), 1)
                dve.memset(last, 0.0).then_inc(sem("state"), 1)
                with dve.Fori(0, FFN_ROUNDS) as r:
                    with dve.Fori(0, TPR) as t_:
                        n = r * TPR + t_

                        def between(i):
                            if 3 <= i <= 3 + SUB:
                                vector_mix(dve, n, i - 3)
                            if 10 <= i < 10 + SUB:
                                dve.wait_ge(sem("abel"), n + 1)
                                vector_dot(dve, abel, gc_w_sum[:, :], dot_a, i - 10, "dot_abel")

                        vector_steps(dve, r, t_ * TILE_STEPS, TILE_STEPS, False, between)
                    vector_boundary(dve, r, False)
                for s in range(SUB + 1):
                    vector_mix(dve, NB, s)
                rounds(dve, vector_round)

            @block.gpsimd
            def _(pool):
                pool.sem_inc(sem("stored"), 4)
                pool.sem_inc(sem("added"), 2)
                pool.sem_inc(sem("expert_out_seen"), 2)
                with pool.Fori(0, NB) as n:
                    def add(e):
                        pool.wait_ge(sem("scaled"), n * E + e + 3)
                        if e == 0:
                            pool.wait_ge(sem("sum_started"), n + 1)
                        else:
                            pool.wait_ge(sem("added"), n * E + e + 2)
                        pool.tensor_tensor(acc, acc, scaled[e % 2], ALU.add).then_inc(sem("added"), 1)

                    add(0)
                    add(1)
                    add(2)
                    pool_mix(pool, n, 0)
                    add(3)
                    add(4)
                    pool_mix(pool, n, 1)
                    pool_mix(pool, n, 2)
                    add(5)
                    pool_mix(pool, n, 3)
                    pool_mix(pool, n, 4)
                    add(6)
                    add(7)
                    pool.wait_ge(sem("added"), n * E + E + 2)
                    pool.wait_ge(sem("abel"), n + 1)
                    pool.wait_ge(sem("pulled"), n + 1)
                    pool.wait_ge(sem("mix_dot"), n + 1)
                    pool.tensor_tensor(diff, acc, abel, ALU.subtract).then_inc(sem("difference"), 1)
                    pool.wait_ge(sem("residual"), n + 1)
                    pool.tensor_tensor(base, base, abel, ALU.add).then_inc(sem("base"), 1)
                for part in range(5):
                    pool_mix(pool, NB, part)
                rounds(pool, pool_round)

        csT = xaT[:, 0:4, :].rearrange("p a b -> p (a b)").rearrange("p (k n) -> p k n", n=P)
        outb = xfT[:, :, :].rearrange("p b (s h) -> p b s h", s=SUB)
        with nc.Block() as block:
            @block.vector
            def _(dve):
                H2 = L // 4
                for g in range(4):
                    part = slice(g * H2, (g + 1) * H2)
                    r = Rho[:, g * H2 + 1:(g + 1) * H2 + 1]
                    dve.tensor_tensor(Wst[:, part, :], Wst[:, part, :], r.unsqueeze(2).broadcast_to([P, H2, S]), ALU.mult).then_inc(sem("cs_a"), 1)
                    dve.wait_ge(sem("cs_a"), g + 1)
                    dve.tensor_tensor(Wst[:, part, :], Wst[:, part, :], gC[:, part, :], ALU.mult).then_inc(sem("cs_b"), 1)
                    dve.wait_ge(sem("cs_b"), g + 1)
                    dve.tensor_tensor(Wst[:, part, :], Wst[:, part, :], bC[:, part, :], ALU.add).then_inc(sem("cs_all"), 1)
                for n in range(NB):
                    dve.wait_ge(sem("ssm"), n + 1)
                    dve.scalar_tensor_tensor(out=outb[:, n], in0=banks[4 + n % 4][:, :].rearrange("p (s h) -> p s h", s=SUB), scalar=0.25,
                                             in1=factor[:, (n + 1) * SUB:(n + 2) * SUB, :], op0=ALU.mult, op1=ALU.mult).then_inc(sem("gated_ssm"), 1)

            @block.gpsimd
            def _(pool):
                for n in range(NB):
                    pool.wait_ge(sem("gated_ssm"), n + 1)
                    pool.tensor_tensor(outb[:, n], outb[:, n], X[:, n * SUB:(n + 1) * SUB, :], ALU.add).then_inc(sem("out_rows"), 1)

            @block.tensor
            def _(pe):
                for g in range(4):
                    pe.wait_ge(sem("cs_all"), g + 1)
                    for q in range(4 * g, 4 * g + 4):
                        t = pe.transpose(banks[g][:, (q % 4) * P:(q % 4 + 1) * P], Wst[:, 2 * q:2 * q + 2, :].rearrange("p k n -> p (k n)"), ident[:, :])
                    t.then_inc(sem("cs_T"), 1)
                for n in range(NB):
                    pe.wait_ge(sem("csT"), n // 2 + 1)
                    if n >= 4:
                        pe.wait_ge(sem("gated_ssm"), n - 3)
                    pe.matmul(banks[4 + n % 4][:, :], ones3[:, :], D_b3, start=True, stop=False)
                    for s in range(SUB):
                        t = pe.matmul(banks[4 + n % 4][:, s * P:(s + 1) * P], csT[:, 2 * n + s // 2, :], D_wT[:, s % 2, :],
                                      start=False, stop=(s == SUB - 1))
                    t.then_inc(sem("ssm"), 1)

            @block.scalar
            def _(act):
                for g in range(4):
                    act.wait_ge(sem("cs_T"), g + 1)
                    act.copy(csT[:, g * 4:g * 4 + 4, :], banks[g][:, :].rearrange("p (k n) -> p k n", k=4)).then_inc(sem("csT"), 1)

            @block.sync
            def _(sp):
                rows_out = out.rearrange("b (q k) h -> (b q) k h", k=L)
                for n in range(NB):
                    sp.wait_ge(sem("out_rows"), n + 1)
                    sp.dma_start(rows_out[:, n * SUB:(n + 1) * SUB, :], outb[:, n]).then_inc(sem("out_stored"), 16)
                sp.wait_ge(sem("out_stored"), 16 * NB)


_INS = ["L0_attn_x", "L0_attn_A", "L0_attn_dt_A", "L0_attn_B_w", "L0_attn_B_b", "L0_attn_C_w", "L0_attn_C_b", "L0_attn_D_w",
        "L0_attn_D_b", "L0_attn_conv_w", "L0_attn_conv_b", "L0_attn_gate_w", "L0_attn_gate_b", "L0_attn_ln_in_g",
        "L0_attn_ln_in_b", "L0_attn_ln_st_g", "L0_attn_ln_st_b", "L0_ffn_ln_gamma", "L0_ffn_ln_beta", "L0_ffn_abel_w",
        "L0_ffn_abel_b", "L0_ffn_moe_gate_w", "L0_ffn_moe_gate_b", "L0_ffn_ew1", "L0_ffn_eb1", "L0_ffn_ew2", "L0_ffn_eb2",
        "L0_ffn_gens", "L0_ffn_gc_w", "L0_ffn_gc_b"]


def kernel(**inputs):
    import numpy as _np
    import concourse.bacc as _bacc
    from concourse import mybir as _mybir
    from concourse.bass_utils import run_bass_kernel_spmd as _run

    nc = _bacc.Bacc("TRN2", target_bir_lowering=False, num_devices=1)
    arrays, I = {}, {}
    for name in _INS:
        a = _np.ascontiguousarray(inputs[name])
        if a.ndim == 0 or name == "L0_attn_dt_A":
            a = a.reshape(1, 1)
        arrays[f"in_{name}"] = a
        I[name] = nc.dram_tensor(f"in_{name}", a.shape, _mybir.dt.from_np(a.dtype), kind="ExternalInput").ap()
    out = nc.dram_tensor("out_0", inputs["L0_attn_x"].shape, _mybir.dt.float32, kind="ExternalOutput").ap()
    build(nc, I, out)
    r = _run(nc, [arrays], core_ids=[0])
    return r.results[0]["out_0"]
```

```python
from contextlib import ExitStack

import concourse.bass as bass
from concourse import mybir

ALU = mybir.AluOpType
ACT = mybir.ActivationFunctionType
AX_X = mybir.AxisListType.X
F32 = mybir.dt.float32
BF16 = mybir.dt.bfloat16
F32R = mybir.dt.float32r

P = 128
EPS = 1e-5
SCALE_STEPS = 5
TAYLOR = 10
UNROLL = 8
SEG = 16
ROUNDS = 6
TOLERANCE = 1e-5
ds = bass.ds

RSQRT_MAGIC = float(0x5F3759DF)
RSQRT_FACTOR = -27.0 / 1024.0


def build(nc, I, out):
    NB, T, H = I["L0_attn_x"].shape
    S = I["L0_attn_A"].shape[0]
    E, _, F = I["L0_ffn_ew1"].shape
    NROT = I["L0_ffn_gens"].shape[0]
    K = F // P
    SUB = T // P
    NS = NB * SUB
    L = T // SEG
    assert NB * SEG == P and L % UNROLL == 0 and S == 64
    assert H == P and T % P == 0 and F % P == 0 and NROT + 1 == 4 and SUB == 4 and E == 8

    with ExitStack() as ctx:
        sems = {}

        def sem(name):
            if name not in sems:
                sems[name] = ctx.enter_context(nc.semaphore(name))
            return sems[name]

        def sb(name, shape, dt=F32):
            return ctx.enter_context(nc.sbuf_tensor(name, shape, dt))

        banks = [ctx.enter_context(nc.psum_tensor(f"bank{i}", [P, 512], F32)) for i in range(8)]

        ident = sb("ident", [P, P])
        ones = sb("ones", [P, P])
        shift = sb("shift", [P, P])
        first_col = sb("first_col", [P, 1])
        center = sb("center", [S, S])
        iota_i = sb("iota_i", [P, NS * E], mybir.dt.int32)
        rank = sb("rank", [P, NS, E])
        eps_col = sb("eps_col", [P, 1])
        junk_col = sb("junk_col", [P, 1])
        cols = sb("cols", [P, 24])
        names = ["ln_in_g", "ln_in_b", "conv_b", "gate_b_in", "ln_gamma", "ln_beta", "B_b", "ln_st_g", "ln_st_b"]
        col = {n: cols[:, i:i + 1] for i, n in enumerate(names)}
        conv_w = cols[:, 10:13]
        conv_w1 = cols[:, 13:14]
        dt_col = cols[0:S, 14:15]
        row_mean = cols[:, 18:19]
        row_mean_b = cols[:, 19:20]
        half_gc_b = cols[:, 20:21]
        half_gate_b = cols[:, 21:22]
        C_b_col = cols[:, 15:16]
        state_gain = cols[:, 16:17]
        eb1_col = sb("eb1_col", [P, E, K])
        eb1_rows = sb("eb1_rows", [E * K, P])
        rows = sb("rows", [1, 2 * P + E + 2])
        gc_w_row = rows[:, 0:2 * P]
        mgb_row = rows[:, 2 * P:2 * P + E]
        gc_b_row = rows[:, 2 * P + E:2 * P + E + 1]
        dt_row = rows[:, 2 * P + E + 1:2 * P + E + 2]
        bias_in = sb("bias_in", [3, 3, P])
        bias_rest = sb("bias_rest", [3, 2, 3, P])
        bias_part = sb("bias_part", [3, 2, 3, P], BF16)
        bias_mix = sb("bias_mix", [3, 3, P])
        bias_low = sb("bias_low", [3, 3, P])
        bias3 = sb("bias3", [3, 3, SUB, P], BF16)
        abel_b3, D_b3, gate_b3 = (bias3[:, i].rearrange("a s h -> a (s h)") for i in range(3))
        ones3 = sb("ones3", [3, P], BF16)
        bcast = sb("bcast", [P, 2 * P + E + 1])
        gc_w_all = bcast[:, 0:2 * P]
        mgb_all = bcast[:, 2 * P:2 * P + E]
        bias_src = sb("bias_src", [S, 2, P])
        bias_all = sb("bias_all", [P, 3, S])

        gate_w = sb("gate_w", [P, 2, P])
        gate_wT = sb("gate_wT", [P, 2, P])
        BC_w = sb("BC_w", [S, 2, P])
        B_wT = sb("B_wT", [P, S])
        C_wT = sb("C_wT", [P, 2, S])
        D_w = sb("D_w", [P, 2, S])
        D_wT = sb("D_wT", [P, 2, P])
        abel_in = sb("abel_in", [P, P])
        abel_w = [sb(name, [P, P], F32R)[:, :] for name in ("abel_high", "abel_rest")]
        router_w = sb("router_w", [P, E])
        ew1 = [sb(name, [P, E, F], F32R)[:, :, :] for name in ("ew1_high", "ew1_rest")]
        ew2 = sb("ew2", [P, E, K, P])
        eb2 = sb("eb2", [E, P])
        eb2T = sb("eb2T", [P, E])
        eb2r = sb("eb2r", [E, P])
        Mx = sb("Mx", [S, S])
        pick = sb("pick", [S, 2, P])
        Mrep = sb("Mrep", [P, 2, S])
        AbC = sb("AbC", [S, S])
        R23 = sb("R23", [P, P])
        Rall = sb("Rall", [P, P])

        X = sb("X", [P, NS, P])
        st = sb("st", [P, NS, 6])
        lnv = sb("lnv", [P, 8, NS])
        xpad = sb("xpad", [P, L + 2, P])
        xaT = sb("xaT", [P, NB, T])
        xf = sb("xf", [P, 2, NB, T], F32R)
        gi_all = sb("gi", [P, NB + 1, T])
        gi = gi_all[:, 1:, :]
        Dv = sb("Dv", [P, L, S])
        late = sb("late", [P, 2 * L * S])
        Wst = late[:, 0:L * S].rearrange("p (k n) -> p k n", n=S)
        CT = late[:, L * S:2 * L * S].rearrange("p (k n) -> p k n", n=P)
        Rho = sb("Rho", [P, L + 1])

        hT = sb("hT", [P, 2, K, T])
        pulled = sb("pulled", [P, SUB, P])
        wdT_all = late[0:E, :].rearrange("e (q p) -> e q p", p=P)

        ew1_in = late[:, L * S:2 * L * S].rearrange("p (e f) -> p e f", e=E)
        ew2T = late[:, 0:E * F].rearrange("p (e k f) -> p e k f", e=E, k=K)
        ex = hT[:, :, :, :].rearrange("p a b c -> p (a b c)")
        XE, XT, EX, ET = (ex[:, i * 512:(i + 1) * 512].rearrange("p (m n) -> p m n", m=4) for i in range(4))
        pulled_cols = pulled[:, :, :].rearrange("p s h -> p (s h)")
        gens = pulled_cols[:, 0:NROT * P].rearrange("p (m n) -> p m n", m=NROT)
        A_in = pulled_cols[0:S, NROT * P:NROT * P + S]

        fx = xpad[:, :, :].rearrange("p a b -> p (a b)")[:, 0:4096]

        def buf(i):
            return fx[:, i * 512:(i + 1) * 512].rearrange("p (s h) -> p s h", s=SUB)

        abel, gate_t, silu_t, acc, diff, base, sc0, sc1 = (buf(i) for i in range(8))
        scaled = [sc0, sc1]
        dots = sb("dots", [P, 4, SUB])
        dot_a, dot_d, gc, gg = (dots[:, i] for i in range(4))

        zbuf = sb("zbuf", [P, 2, SUB, P])

        N_W = 19
        ident4 = ident[:, :].unsqueeze(1).broadcast_to([P, 4, P])

        mean, var, r1, nm1, rz, nmz, tmp, tmp2 = (lnv[:, i, :] for i in range(8))
        scratch = sb("scratch", [P, T])
        lg, oh1 = (scratch[:, i * NS * E:(i + 1) * NS * E].rearrange("p (q e) -> p q e", e=E) for i in range(2))
        oh2 = sb("oh2", [P, NS, E])
        wd = sb("wd", [P, NS, E])
        top = sb("top", [P, 7, NS])
        m1, m2, r_1, r_2, tw, w1, w2 = (top[:, i, :] for i in range(7))
        conv_order = list(range(1, NB)) + [0]
        group_order = [1, 2, 3, 0]

        def per_expert(ap):
            return ap.unsqueeze(2).broadcast_to([P, NS, E])

        def split_product(pe, o, a, b, start=True, stop=True):
            pe.matmul(o, a[0], b[0], start=start, stop=False)
            pe.matmul(o, a[0], b[1], start=False, stop=False)
            return pe.matmul(o, a[1], b[0], start=False, stop=stop)

        def conv_tile(n):
            return xaT[:, n, :].rearrange("p (k n) -> p k n", k=SUB)

        with nc.Block() as front:
            @front.sync
            def _(sp):
                def load(dst, src, name="weights_loaded"):
                    sp.dma_start(dst, src).then_inc(sem(name), 16)

                def as_col(name):
                    return I[name].rearrange("(p a) -> p a", a=1)

                load(gens, I["L0_ffn_gens"].rearrange("m p n -> p m n"), "expm_loaded")
                load(A_in, I["L0_attn_A"], "expm_loaded")
                load(dt_row, I["L0_attn_dt_A"], "expm_loaded")
                load(gate_w[:, :, :], I["L0_attn_gate_w"].rearrange("(j p) h -> p j h", p=P), "matrices_loaded")
                load(BC_w[:, 0, :], I["L0_attn_B_w"], "matrices_loaded")
                load(BC_w[:, 1, :], I["L0_attn_C_w"], "matrices_loaded")
                load(D_w[:, 0, :], I["L0_attn_D_w"], "matrices_loaded")
                load(D_w[:, 1, :], I["L0_attn_D_w"], "matrices_loaded")
                load(ew2[:, :, :, :], I["L0_ffn_ew2"].rearrange("e (k p) d -> p e k d", p=P), "ew2_loaded")
                load(col["ln_in_g"], as_col("L0_attn_ln_in_g"))
                load(col["ln_in_b"], as_col("L0_attn_ln_in_b"))
                load(col["conv_b"], as_col("L0_attn_conv_b"))
                load(conv_w, I["L0_attn_conv_w"].rearrange("h a k -> h (a k)"))
                load(col["gate_b_in"], I["L0_attn_gate_b"][P:2 * P].rearrange("(p a) -> p a", a=1))
                load(col["ln_gamma"], as_col("L0_ffn_ln_gamma"))
                load(col["ln_beta"], as_col("L0_ffn_ln_beta"))
                load(col["B_b"][0:S], as_col("L0_attn_B_b"))
                for half in (slice(0, S), slice(S, P)):
                    load(col["ln_st_g"][half], as_col("L0_attn_ln_st_g"))
                    load(col["ln_st_b"][half], as_col("L0_attn_ln_st_b"))
                    load(C_b_col[half], as_col("L0_attn_C_b"))
                load(eb2[:, :], I["L0_ffn_eb2"])
                load(eb1_rows[:, :], I["L0_ffn_eb1"].rearrange("e (k p) -> (e k) p", p=P))
                load(gc_w_row, I["L0_ffn_gc_w"].rearrange("p a -> a p"))
                load(mgb_row, I["L0_ffn_moe_gate_b"].rearrange("(a p) -> a p", a=1))
                load(gc_b_row, I["L0_ffn_gc_b"].rearrange("(a p) -> a p", a=1))
                for i in range(3):
                    load(bias_in[i:i + 1, 0, :], I["L0_ffn_abel_b"].rearrange("(a p) -> a p", a=1), "biases_loaded")
                    load(bias_in[i:i + 1, 1, :], I["L0_attn_D_b"].rearrange("(a p) -> a p", a=1), "biases_loaded")
                    load(bias_in[i:i + 1, 2, :], I["L0_attn_gate_b"][0:P].rearrange("(a p) -> a p", a=1), "biases_loaded")
                load(abel_in[:, :], I["L0_ffn_abel_w"], "small_loaded")
                load(router_w[:, :], I["L0_ffn_moe_gate_w"], "small_loaded")
                load(ew1_in[:, :, :], I["L0_ffn_ew1"].rearrange("e d f -> d e f"), "ew1_loaded")

            @front.gpsimd
            def _(pool):
                pool.memset(ident[:, :], 0.0).then_inc(sem("ident_zero"), 1)
                pool.wait_ge(sem("ident_zero"), 1)
                pool.affine_select(out=ident[:, :], in_=ident[:, :], compare_op=ALU.not_equal, fill=1.0, base=0,
                                   pattern=[[-1, P]], channel_multiplier=1).then_inc(sem("ident_ready"), 1)
                pool.memset(ones[:, :], 1.0).then_inc(sem("ones_ready"), 1)
                pool.memset(XE[:, 3, :], 0.0).then_inc(sem("expm_zero"), 1)
                pool.memset(XT[:, 3, :], 0.0).then_inc(sem("expm_zero"), 1)
                pool.memset(eps_col[:, :], EPS).then_inc(sem("eps_ready"), 1)
                pool.memset(shift[:, :], 0.0).then_inc(sem("shift_zero"), 1)
                pool.wait_ge(sem("shift_zero"), 1)
                pool.affine_select(out=shift[:, :], in_=shift[:, :], compare_op=ALU.not_equal, fill=1.0, base=1,
                                   pattern=[[-1, P]], channel_multiplier=1).then_inc(sem("shift_ones"), 1)
                pool.wait_ge(sem("shift_ones"), 1)
                pool.memset(shift[:, 0:P:SEG], 0.0)
                pool.iota(iota_i[:, :], pattern=[[0, NS], [-1, E]], base=E, channel_multiplier=0).then_inc(sem("iota_ready"), 1)
                pool.wait_ge(sem("iota_ready"), 1)
                pool.tensor_copy(rank[:, :, :], iota_i[:, :].rearrange("p (s e) -> p s e", s=NS)).then_inc(sem("rank_ready"), 1)

                parts = []

                def split(high, low, value):
                    pool.tensor_copy(high, value).then_inc(sem("split_high"), 1)
                    parts.append(high)
                    pool.wait_ge(sem("split_high"), len(parts))
                    pool.tensor_tensor(low, value, high.bitcast(F32), ALU.subtract).then_inc(sem("split"), 1)

                def split_tile(n):
                    pool.wait_ge(sem("zT_used"), n + 1)
                    split(xf[:, 0, n, :], xf[:, 1, n, :], gi[:, n, :])

                pool.wait_ge(sem("small_loaded"), 32)
                split(abel_w[0], abel_w[1], abel_in[:, :])
                pool.wait_ge(sem("biases_loaded"), 144)
                bias_steps = []

                def bias_step(ins):
                    bias_steps.append(ins)
                    ins.then_inc(sem("bias_parts"), 1)
                    pool.wait_ge(sem("bias_parts"), len(bias_steps))

                def own(i, shape):
                    return ident[0:3, i:i + 1].unsqueeze(2).broadcast_to([3] + shape)

                x = bias_in[:, :, :]
                for j in range(2):
                    bias_step(pool.tensor_copy(bias_part[:, j], x))
                    bias_step(pool.tensor_tensor(bias_rest[:, j], x, bias_part[:, j], ALU.subtract))
                    x = bias_rest[:, j]
                pool.tensor_tensor(bias_mix[:, :, :], bias_part[:, 0], own(0, [3, P]), ALU.mult)
                bias_step(pool.tensor_tensor(bias_low[:, :, :], bias_part[:, 1], own(1, [3, P]), ALU.mult))
                pool.tensor_tensor(bias_rest[:, 0], x, own(2, [3, P]), ALU.mult)
                bias_step(pool.tensor_tensor(bias_mix[:, :, :], bias_mix[:, :, :], bias_low[:, :, :], ALU.add))
                for i in range(3):
                    pool.tensor_tensor(bias3[:, i], bias_mix[:, i, :].unsqueeze(1).broadcast_to([3, SUB, P]),
                                       bias_rest[:, 0, i, :].unsqueeze(1).broadcast_to([3, SUB, P]), ALU.add)
                for n in range(NB - 3):
                    split_tile(n)
                pool.wait_ge(sem("affine"), NB)
                pool.tensor_copy(xpad[:, L + 1, 0:P - 1], xpad[:, 1, 1:P]).then_inc(sem("edges"), 1)
                pool.wait_ge(sem("edges"), 1)
                pool.memset(xpad[:, L + 1, SEG - 1:P:SEG], 0.0).then_inc(sem("edges"), 1)
                pool.tensor_copy(xpad[:, 0, 1:P], xpad[:, L, 0:P - 1]).then_inc(sem("edges"), 1)
                pool.wait_ge(sem("edges"), 3)
                pool.memset(xpad[:, 0, 0:P:SEG], 0.0).then_inc(sem("edges"), 1)
                for n in range(NB - 3, NB):
                    split_tile(n)
                pool.wait_ge(sem("ew1_loaded"), 16)
                for e in range(E):
                    if e == E // 2:
                        pool.wait_ge(sem("conv"), NB)
                        for b in (diff, base, gate_t, dots[:, :, :]):
                            pool.memset(b, 0.0)
                    split(ew1[0][:, e, :], ew1[1][:, e, :], ew1_in[:, e, :])

            @front.tensor
            def _(pe):
                def z_transposes(n):
                    pe.wait_ge(sem("z_ready"), n + 1)
                    if n >= 2:
                        pe.wait_ge(sem("zT_used"), n - 1)
                    for s in range(SUB):
                        t = pe.transpose(banks[7 * (n % 2)][:, s * P:(s + 1) * P], zbuf[:, n % 2, s, :], ident[:, :])
                    t.then_inc(sem("zT"), 1)

                def ew2_transposes(q):
                    if q == 0:
                        pe.wait_ge(sem("ew2_loaded"), 16)
                    for i in range(4):
                        t = pe.transpose(banks[3 + q][:, i * P:(i + 1) * P], ew2[:, 2 * q + i // K, i % K, :], ident[:, :])
                    t.then_inc(sem("ew2_T"), 1)

                def gate_in(i):
                    pe.wait_ge(sem("conv"), i + 1)
                    if i < 2:
                        pe.wait_ge(sem("ew2T_copied"), i + 1)
                    else:
                        pe.wait_ge(sem("gate_read"), i - 1)
                    pe.matmul(banks[3 + i % 2][:, :], gate_wT[:, 1, :], xaT[:, conv_order[i], :], start=True, stop=True).then_inc(sem("gate_in"), 1)

                def tokens_product(bank, src, w, i, name):
                    g = group_order[i]
                    for k in range(8):
                        x = src[:, 2 * g + k // 4, (k % 4) * P:(k % 4 + 1) * P]
                        t = pe.matmul(banks[bank][:, k * S:(k + 1) * S], x, w, start=True, stop=True)
                    t.then_inc(sem(name), 1)

                def B_product(i):
                    pe.wait_ge(sem("gated"), min(2 * i + 3, NB))
                    if i >= 2:
                        pe.wait_ge(sem("B_copied"), i - 1)
                    elif i == 0:
                        pe.wait_ge(sem("ew2T_copied"), 3)
                        pe.wait_ge(sem("B_centred"), 1)
                    tokens_product(5 * (1 - i % 2), gi, B_wT[:, :], i, "B_proj")

                def ew2_rotation(q):
                    if q >= 2:
                        pe.wait_ge(sem("ew2r_ready"), q - 1)
                    for i in range(4 * q, 4 * q + 4):
                        t = pe.matmul(banks[1 + q % 2][:, (i % 4) * P:(i % 4 + 1) * P], ew2T[:, i // K, i % K, :], Rall[:, :], start=True, stop=True)
                    t.then_inc(sem("ew2_rotated"), 1)

                def router(n):
                    if n == 0:
                        pe.wait_ge(sem("small_loaded"), 32)
                        pe.wait_ge(sem("ew2T_copied"), 4)
                    pe.wait_ge(sem("zT_used"), n + 1)
                    for q in range(n * SUB, (n + 1) * SUB):
                        x = gi[:, n, (q % SUB) * P:(q % SUB + 1) * P]
                        t = pe.matmul(banks[6][:, q * E:(q + 1) * E], x, router_w[:, :], start=True, stop=True)
                    t.then_inc(sem("router"), 1)

                pe.wait_ge(sem("expm_loaded"), 48)
                pe.wait_ge(sem("ident_ready"), 1)
                pe.wait_ge(sem("ones_ready"), 1)
                for m in range(NROT):
                    pe.transpose(banks[1][:, m * P:(m + 1) * P], gens[:, m, :], ident[:, :])
                pe.transpose(banks[1][0:S, 384:384 + S], A_in, ident[0:S, 0:S])
                pe.matmul(banks[2][0:S, 0:1], ones[0:1, 0:S], dt_row, start=True, stop=True).then_inc(sem("expm_in"), 1)
                for k in range(TAYLOR - 1, 0, -1):
                    pe.wait_ge(sem("taylor"), TAYLOR - k)
                    for m in range(4):
                        t = pe.matmul(banks[1][:, m * P:(m + 1) * P], XT[:, m, :], EX[:, m, :], start=True, stop=True)
                    t.then_inc(sem("taylor_product"), 1)
                    if k == 8:
                        pe.wait_ge(sem("matrices_loaded"), 80)
                        for j in range(2):
                            pe.transpose(banks[0][:, j * P:(j + 1) * P], gate_w[:, j, :], ident[:, :])
                        for j in range(2):
                            pe.transpose(banks[0][:, 2 * P + j * S:2 * P + (j + 1) * S], BC_w[:, j, :], ident[0:S, 0:S])
                        pe.transpose(banks[0][:, 384:512], D_w[:, :, :].rearrange("p j n -> p (j n)"), ident[:, :]).then_inc(sem("small_T"), 1)
                    if 4 <= k <= 7:
                        ew2_transposes(7 - k)
                    if k == 3:
                        pe.wait_ge(sem("weights_loaded"), 16 * N_W)
                        pe.transpose(banks[7][:, 464:464 + E], eb2[:, :], ident[0:E, 0:E])
                        pe.transpose(banks[7][:, 480:480 + E * K], eb1_rows[:, :], ident[0:E * K, 0:E * K])
                        pe.matmul(banks[7][:, 0:2 * P], ones[0:1, :], gc_w_row, start=True, stop=True)
                        pe.matmul(banks[7][:, 2 * P:2 * P + E], ones[0:1, :], mgb_row, start=True, stop=True)
                        pe.matmul(banks[7][:, 2 * P + E:2 * P + E + 1], ones[0:1, :], gc_b_row, start=True, stop=True).then_inc(sem("rows_all"), 1)
                pe.wait_ge(sem("taylor"), TAYLOR)
                for m in range(4):
                    t = pe.transpose(banks[2][:, m * P:(m + 1) * P], EX[:, m, :], ident[:, :])
                t.then_inc(sem("exp_T"), 1)
                pe.wait_ge(sem("small_copied"), 1)
                z_transposes(0)
                pe.wait_ge(sem("rows_copied"), 1)
                for k in range(SCALE_STEPS):
                    if k:
                        pe.wait_ge(sem("squared"), k)
                    pe.wait_ge(sem("squared_T"), k + 1)
                    for m in range(4):
                        t = pe.matmul(banks[1][:, m * P:(m + 1) * P], ET[:, m, :], EX[:, m, :], start=True, stop=True)
                    t.then_inc(sem("square"), 1)
                    for m in range(4):
                        t = pe.matmul(banks[2][:, m * P:(m + 1) * P], EX[:, m, :], ET[:, m, :], start=True, stop=True)
                    t.then_inc(sem("square_T"), 1)
                    if k < 3:
                        z_transposes(2 * k + 1)
                        z_transposes(2 * k + 2)
                    elif k == 3:
                        z_transposes(7)
                    else:
                        gate_in(0)
                    if k == 1:
                        router(0)
                    elif k >= 2:
                        router(2 * k - 3)
                        router(2 * k - 2)
                pe.wait_ge(sem("squared"), SCALE_STEPS)
                pe.wait_ge(sem("squared_T"), SCALE_STEPS + 1)
                pe.matmul(banks[1][:, 0:P], ET[:, 1, :], EX[:, 2, :], start=True, stop=True).then_inc(sem("rot23"), 1)
                gate_in(1)
                router(NB - 1)
                pe.wait_ge(sem("rot23_copied"), 1)
                pe.matmul(banks[1][:, P:2 * P], ET[:, 0, :], R23[:, :], start=True, stop=True).then_inc(sem("rot"), 1)
                gate_in(2)
                pe.wait_ge(sem("scan_matrix"), 2)
                pe.wait_ge(sem("zT_used"), NB)
                for i, m in enumerate((center, AbC)):
                    pe.matmul(banks[7][:, i * S:(i + 1) * S], bias_src[:, i, :], m[:, :], start=True, stop=True)
                for c in range(2):
                    t = pe.matmul(banks[7][:, 2 * S + c * S:2 * S + (c + 1) * S], pick[:, c, :], Mx[:, :], start=True, stop=True)
                t.then_inc(sem("scan_bias"), 1)
                gate_in(3)
                gate_in(4)
                gate_in(5)
                gate_in(6)
                gate_in(7)
                B_product(0)
                B_product(1)
                pe.wait_ge(sem("rot_copied"), 1)
                ew2_rotation(0)
                B_product(2)
                ew2_rotation(1)
                ew2_rotation(2)
                B_product(3)
                ew2_rotation(3)
                pe.matmul(banks[7][0:E, 384:384 + P], eb2T[:, :], Rall[:, :], start=True, stop=True).then_inc(sem("eb2_rotated"), 1)
                pe.wait_ge(sem("weights"), 1)
                for n in range(NB):
                    if n < 2:
                        pe.wait_ge(sem("gate_read"), NB)
                    else:
                        pe.wait_ge(sem("wdT_copied"), n - 1)
                    for s in range(SUB):
                        t = pe.transpose(banks[3 + n % 2][0:E, s * P:(s + 1) * P], wd[:, n * SUB + s, :], ident[:, :])
                    t.then_inc(sem("weights_T"), 1)

            @front.scalar
            def _(act):
                xr = I["L0_attn_x"].rearrange("b (q k) h -> (b q) k h", k=L)
                for i in range(4):
                    part = slice(i * NS // 4, (i + 1) * NS // 4)
                    act.dma_start(X[:, part, :], xr[:, part, :]).then_inc(sem("x_loaded"), 16)

                def ew2_copy(q):
                    act.wait_ge(sem("ew2_T"), q + 1)
                    act.copy(ew2T[:, 2 * q:2 * q + 2, :, :], banks[3 + q][:, :].rearrange("p (e k f) -> p e k f", e=2, k=K)).then_inc(sem("ew2T_copied"), 1)

                def affine(n):
                    act.wait_ge(sem("zT"), n + 1)
                    z = banks[7 * (n % 2)][:, :]
                    act.activation(xpad[:, n * SUB + 1:(n + 1) * SUB + 1, :], z.rearrange("p (k n) -> p k n", k=SUB), ACT.Identity,
                                   bias=col["ln_in_b"], scale=col["ln_in_g"]).then_inc(sem("affine"), 1)
                    act.activation(gi[:, n, :], z, ACT.Identity, bias=col["ln_beta"], scale=col["ln_gamma"]).then_inc(sem("zT_used"), 1)

                def conv_centre(i):
                    n = conv_order[i]
                    act.wait_ge(sem("affine"), n + 1)
                    act.activation(conv_tile(n), xpad[:, n * SUB + 1:(n + 1) * SUB + 1, :], ACT.Identity, bias=col["conv_b"], scale=conv_w1)\
                       .then_inc(sem("conv_centre"), 1)

                def gate(i):
                    act.wait_ge(sem("router"), conv_order[i] + 1)
                    act.wait_ge(sem("split"), conv_order[i] + 2)
                    act.wait_ge(sem("gate_in"), i + 1)
                    act.activation(gi[:, conv_order[i], :], banks[3 + i % 2][:, :], ACT.Tanh, scale=0.5, bias=half_gate_b).then_inc(sem("gate_read"), 1)

                def rotated_copy(q):
                    act.wait_ge(sem("ew2_rotated"), q + 1)
                    act.copy(ew2[:, 2 * q:2 * q + 2, :, :], banks[1 + q % 2][:, :].rearrange("p (e k f) -> p e k f", e=2, k=K))\
                       .then_inc(sem("ew2r_ready"), 1)

                act.wait_ge(sem("small_T"), 1)
                act.copy(gate_wT[:, :, :], banks[0][:, 0:2 * P].rearrange("p (j h) -> p j h", j=2))
                act.copy(B_wT[:, :], banks[0][:, 2 * P:2 * P + S]).then_inc(sem("B_T"), 1)
                act.copy(C_wT[:, 0, :], banks[0][:, 2 * P + S:2 * P + 2 * S])
                act.copy(C_wT[:, 1, :], banks[0][:, 2 * P + S:2 * P + 2 * S])
                act.wait_ge(sem("D_zero"), 1)
                act.copy(D_wT[0:S, 0, :], banks[0][0:S, 384:512])
                act.copy(D_wT[S:P, 1, :], banks[0][S:P, 384:512]).then_inc(sem("small_copied"), 1)
                ew2_copy(0)
                ew2_copy(1)
                act.wait_ge(sem("eps_ready"), 1)
                act.wait_ge(sem("var_ready"), 1)
                act.activation(tmp, var, ACT.Sqrt, bias=eps_col[:, :]).then_inc(sem("std_ready"), 1)
                act.wait_ge(sem("var_ready"), 2)
                act.activation(tmp, tmp2, ACT.Sqrt, bias=eps_col[:, :]).then_inc(sem("std_ready"), 1)
                ew2_copy(2)
                ew2_copy(3)
                act.wait_ge(sem("rows_all"), 1)
                act.copy(bcast[:, :], banks[7][:, 0:2 * P + E + 1]).then_inc(sem("rows_copied_a"), 1)
                act.copy(eb1_col[:, :, :], banks[7][:, 480:480 + E * K].rearrange("p (e k) -> p e k", e=E))
                act.copy(eb2T[:, :], banks[7][:, 464:464 + E]).then_inc(sem("rows_copied"), 1)
                act.wait_ge(sem("rows_copied_a"), 1)
                act.mul(half_gc_b, bcast[:, 2 * P + E:2 * P + E + 1], 0.5)
                act.mul(half_gate_b, col["gate_b_in"], 0.5).then_inc(sem("half_biases"), 1)
                for k in range(SCALE_STEPS + 1):
                    if k == 0:
                        act.wait_ge(sem("exp_T"), 1)
                    else:
                        act.wait_ge(sem("square_T"), k)
                    act.copy(ET[:, :, :], banks[2][:, :].rearrange("p (m n) -> p m n", m=4)).then_inc(sem("squared_T"), 1)
                    if k == 0:
                        affine(0)
                        act.wait_ge(sem("half_columns"), 1)
                    elif k <= 3:
                        affine(2 * k - 1)
                        affine(2 * k)
                    elif k == 4:
                        affine(7)
                        for i in range(3):
                            conv_centre(i)
                for i in range(3, 6):
                    conv_centre(i)
                act.wait_ge(sem("half_biases"), 1)
                act.activation(junk_col[:, :], eps_col[:, :], ACT.Gelu)
                gate(0)
                conv_centre(6)
                conv_centre(7)
                gate(1)
                gate(2)
                gate(3)
                gate(4)
                gate(5)
                gate(6)
                gate(7)
                rotated_copy(0)
                rotated_copy(1)
                rotated_copy(2)
                act.wait_ge(sem("margin"), 1)
                act.activation(tw, w1, ACT.Tanh, scale=0.5).then_inc(sem("margin_tanh"), 1)
                rotated_copy(3)
                act.wait_ge(sem("eb2_rotated"), 1)
                act.copy(eb2r[:, :], banks[7][0:E, 384:384 + P])
                act.wait_ge(sem("split"), NB + 1 + E)
                for n in range(NB):
                    act.wait_ge(sem("weights_T"), n + 1)
                    act.copy(wdT_all[:, n * SUB:(n + 1) * SUB, :], banks[3 + n % 2][0:E, :].rearrange("p (s h) -> p s h", s=SUB))\
                       .then_inc(sem("wdT_copied"), 1)

            @front.vector
            def _(dve):
                steps = {"norm_step": 0, "matrix_step": 0, "routing_step": 0}

                def step(ins, name):
                    steps[name] += 1
                    ins.then_inc(sem(name), 1)
                    dve.wait_ge(sem(name), steps[name])

                def stats(n):
                    if n % 2 == 0:
                        dve.wait_ge(sem("x_loaded"), 64)
                    for s in range(SUB):
                        t = dve.bn_stats(st[:, n * SUB + s, :], X[:, n * SUB + s, :])
                    t.then_inc(sem("stats"), 1)

                def z_tile(n):
                    if n >= 2:
                        dve.wait_ge(sem("zT"), n - 1)
                    for s in range(SUB):
                        q = n * SUB + s
                        t = dve.tensor_scalar(zbuf[:, n % 2, s, :], X[:, q, :], rz[:, q:q + 1], nmz[:, q:q + 1], ALU.mult, ALU.add)
                    t.then_inc(sem("z_ready"), 1)

                def conv(*tiles):
                    for i in tiles:
                        n = conv_order[i]
                        dve.wait_ge(sem("conv_centre"), i + 1)
                        if n == NB - 1:
                            dve.wait_ge(sem("edges"), 2)
                        elif n == 0:
                            dve.wait_ge(sem("edges"), 4)
                        else:
                            dve.wait_ge(sem("affine"), n + 2)
                        o = conv_tile(n)
                        dve.scalar_tensor_tensor(out=o, in0=xpad[:, n * SUB:(n + 1) * SUB, :], scalar=conv_w[:, 0:1], in1=o, op0=ALU.mult, op1=ALU.add)\
                           .then_inc(sem("conv_before"), 1)
                    for i in tiles:
                        n = conv_order[i]
                        o = conv_tile(n)
                        dve.wait_ge(sem("conv_before"), i + 1)
                        dve.scalar_tensor_tensor(out=o, in0=xpad[:, n * SUB + 2:(n + 1) * SUB + 2, :], scalar=conv_w[:, 2:3], in1=o, op0=ALU.mult, op1=ALU.add)\
                           .then_inc(sem("conv"), 1)

                def gated(i):
                    n = conv_order[i]
                    dve.wait_ge(sem("gate_read"), i + 1)
                    dve.scalar_tensor_tensor(out=gi[:, n, :], in0=gi[:, n, :], scalar=1.0, in1=xaT[:, n, :], op0=ALU.add, op1=ALU.mult).then_inc(sem("gated"), 1)

                def B_copy(i):
                    g = group_order[i]
                    dve.wait_ge(sem("B_proj"), i + 1)
                    dve.tensor_tensor(Dv[:, g * 8:g * 8 + 8, :], banks[5 * (1 - i % 2)][:, :].rearrange("p (k n) -> p k n", n=S),
                                      bias_all[:, 2, :].unsqueeze(1).broadcast_to([P, 8, S]), ALU.add).then_inc(sem("B_copied"), 1)

                def norm_statistics(part):
                    if part == 0:
                        dve.wait_ge(sem("stats"), NB)
                        dve.tensor_tensor(mean, st[:, :, 1], st[:, :, 4], ALU.add)
                        dve.tensor_tensor(tmp, st[:, :, 1], st[:, :, 4], ALU.subtract)
                        step(dve.tensor_tensor(var, st[:, :, 2], st[:, :, 5], ALU.add), "norm_step")
                        dve.tensor_tensor(tmp2, tmp, tmp, ALU.mult)
                        dve.tensor_scalar(mean, mean, 0.5, None, ALU.mult)
                        step(dve.tensor_scalar(var, var, 1.0 / H, None, ALU.mult), "norm_step")
                        dve.scalar_tensor_tensor(out=var, in0=tmp2, scalar=0.25, in1=var, op0=ALU.mult, op1=ALU.add).then_inc(sem("var_ready"), 1)
                    elif part == 1:
                        dve.wait_ge(sem("std_ready"), 1)
                        step(dve.reciprocal(r1, tmp), "norm_step")
                        step(dve.tensor_tensor(tmp2, r1, r1, ALU.mult), "norm_step")
                        dve.tensor_tensor(tmp2, tmp2, var, ALU.mult).then_inc(sem("var_ready"), 1)
                        dve.scalar_tensor_tensor(out=nm1, in0=mean, scalar=-1.0, in1=r1, op0=ALU.mult, op1=ALU.mult)
                    else:
                        dve.wait_ge(sem("std_ready"), 2)
                        step(dve.reciprocal(rz, tmp), "norm_step")
                        step(dve.tensor_tensor(rz, rz, r1, ALU.mult), "norm_step")
                        step(dve.scalar_tensor_tensor(out=nmz, in0=mean, scalar=-1.0, in1=rz, op0=ALU.mult, op1=ALU.mult), "norm_step")

                dve.memset(D_wT[:, :, :], 0.0).then_inc(sem("D_zero"), 1)
                dve.wait_ge(sem("ident_ready"), 1)
                dve.tensor_reduce(first_col[:, :], ident[:, 0:P:SEG], AX_X, ALU.add)
                for c in range(2):
                    dve.tensor_copy(pick[:, c, :].rearrange("k (a i) -> k a i", a=4),
                                    ident[0:S, 32 * c:32 * c + 32].unsqueeze(1).broadcast_to([S, 4, 32]))
                dve.tensor_scalar(center[:, :], ident[0:S, 0:S], -1.0 / S, None, ALU.add)
                dve.wait_ge(sem("ones_ready"), 1)
                dve.tensor_copy(ones3[:, :], ones[0:3, :])
                dve.wait_ge(sem("expm_in"), 1)
                dve.wait_ge(sem("expm_zero"), 2)
                dve.tensor_copy(dt_col, banks[2][0:S, 0:1]).then_inc(sem("dt"), 1)
                half = 0.5 ** SCALE_STEPS
                dve.tensor_scalar(XE[:, 0:3, :], gens, half, None, ALU.mult)
                dve.tensor_scalar(XT[:, 0:3, :], banks[1][:, 0:384].rearrange("p (m n) -> p m n", m=3), half, None, ALU.mult)
                dve.wait_ge(sem("dt"), 1)
                dve.tensor_scalar(XE[0:S, 3, 0:S], A_in, dt_col, half, ALU.mult, ALU.mult)
                dve.tensor_scalar(XT[0:S, 3, 0:S], banks[1][0:S, 384:384 + S], dt_col, half, ALU.mult, ALU.mult).then_inc(sem("expm_arg"), 1)
                dve.wait_ge(sem("expm_arg"), 1)
                dve.scalar_tensor_tensor(out=EX, in0=XE, scalar=1.0 / TAYLOR, in1=ident4, op0=ALU.mult, op1=ALU.add).then_inc(sem("taylor"), 1)
                for k in range(TAYLOR - 1, 0, -1):
                    if k >= 6:
                        stats(2 * (9 - k))
                        stats(2 * (9 - k) + 1)
                    elif k >= 3:
                        norm_statistics(5 - k)
                    elif k == 2:
                        z_tile(0)
                    else:
                        z_tile(1)
                    dve.wait_ge(sem("taylor_product"), TAYLOR - k)
                    dve.scalar_tensor_tensor(out=EX, in0=banks[1][:, :].rearrange("p (m n) -> p m n", m=4), scalar=1.0 / k, in1=ident4,
                                             op0=ALU.mult, op1=ALU.add).then_inc(sem("taylor"), 1)
                dve.wait_ge(sem("weights_loaded"), 16 * N_W)
                dve.tensor_scalar(conv_w1, conv_w[:, 1:2], 1.0, None, ALU.add).then_inc(sem("half_columns"), 1)
                dve.tensor_scalar(bias_src[:, 0, :], ones[0:S, :], col["B_b"][0:S], None, ALU.mult)
                dve.tensor_scalar(bias_src[:, 1, :], ones[0:S, :], col["ln_st_b"][0:S], None, ALU.mult)
                for k in range(SCALE_STEPS):
                    if k < 3:
                        z_tile(2 * k + 2)
                        if k < 2:
                            z_tile(2 * k + 3)
                    elif k == 3:
                        z_tile(7)
                    else:
                        conv(0)
                    dve.wait_ge(sem("square_T"), k + 1)
                    dve.tensor_copy(EX, banks[1][:, :].rearrange("p (m n) -> p m n", m=4)).then_inc(sem("squared"), 1)
                dve.wait_ge(sem("squared"), SCALE_STEPS)
                step(dve.tensor_reduce(row_mean[0:S], EX[0:S, 3, 0:S], AX_X, ALU.add), "matrix_step")
                step(dve.tensor_scalar(row_mean[0:S], row_mean[0:S], 1.0 / S, None, ALU.mult), "matrix_step")
                dve.tensor_scalar(AbC[:, :], EX[0:S, 3, 0:S], row_mean[0:S], None, ALU.subtract).then_inc(sem("scan_matrix"), 1)
                dve.wait_ge(sem("rot23"), 1)
                dve.tensor_copy(R23[:, :], banks[1][:, 0:P]).then_inc(sem("rot23_copied"), 1)
                dve.wait_ge(sem("scan_matrix"), 1)
                dve.tensor_scalar(Mx[:, :], AbC[:, :], col["ln_st_g"][0:S], RSQRT_FACTOR, ALU.mult, ALU.mult).then_inc(sem("scan_matrix"), 1)
                conv(1, 2)
                dve.wait_ge(sem("rot"), 1)
                dve.tensor_copy(Rall[:, :], banks[1][:, P:2 * P]).then_inc(sem("rot_copied"), 1)
                dve.wait_ge(sem("B_T"), 1)
                step(dve.tensor_reduce(row_mean_b, B_wT[:, :], AX_X, ALU.add), "matrix_step")
                step(dve.tensor_scalar(row_mean_b, row_mean_b, 1.0 / S, None, ALU.mult), "matrix_step")
                dve.tensor_scalar(B_wT[:, :], B_wT[:, :], row_mean_b, 0.5, ALU.subtract, ALU.mult).then_inc(sem("B_centred"), 1)
                dve.tensor_scalar(state_gain, col["ln_st_g"], RSQRT_FACTOR, None, ALU.mult)
                gated(0)
                conv(3, 4)
                dve.wait_ge(sem("scan_bias"), 1)
                dve.tensor_copy(Mrep[:, :, :], banks[7][:, 2 * S:4 * S].rearrange("p (c n) -> p c n", c=2))
                dve.tensor_copy(bias_all[:, 0:2, :], banks[7][:, 0:2 * S].rearrange("p (c n) -> p c n", c=2)).then_inc(sem("bias_copied"), 1)
                gated(1)
                conv(5)
                dve.wait_ge(sem("bias_copied"), 1)
                dve.tensor_tensor(bias_all[:, 2, :], bias_all[:, 0, :], bias_all[:, 1, :], ALU.add).then_inc(sem("bias_sum"), 1)
                gated(2)
                conv(6, 7)
                for i in range(3, NB):
                    gated(i)
                dve.wait_ge(sem("bias_sum"), 1)
                dve.tensor_scalar(bias_all[:, 1, :], bias_all[:, 1, :], first_col[:, :], None, ALU.mult).then_inc(sem("first_bias"), 1)

                def largest(logits, m, r, onehot):
                    step(dve.tensor_reduce(m, logits, AX_X, ALU.max), "routing_step")
                    step(dve.tensor_tensor(onehot, logits, per_expert(m), ALU.is_equal), "routing_step")
                    step(dve.tensor_tensor(onehot, onehot, rank[:, :, :], ALU.mult), "routing_step")
                    step(dve.tensor_reduce(r, onehot, AX_X, ALU.max), "routing_step")
                    step(dve.tensor_tensor(onehot, rank[:, :, :], per_expert(r), ALU.is_equal), "routing_step")

                dve.wait_ge(sem("router"), NB)
                dve.wait_ge(sem("rank_ready"), 1)
                step(dve.tensor_tensor(lg, banks[6][:, 0:NS * E].rearrange("p (s e) -> p s e", s=NS),
                                       mgb_all.unsqueeze(1).broadcast_to([P, NS, E]), ALU.add), "routing_step")
                B_copy(0)
                largest(lg, m1, r_1, oh1)
                B_copy(1)
                step(dve.scalar_tensor_tensor(out=wd[:, :, :], in0=oh1, scalar=-3e38, in1=lg, op0=ALU.mult, op1=ALU.add), "routing_step")
                largest(wd[:, :, :], m2, r_2, oh2[:, :, :])
                dve.tensor_tensor(w1, m1, m2, ALU.subtract).then_inc(sem("margin"), 1)
                B_copy(2)
                B_copy(3)
                dve.wait_ge(sem("margin_tanh"), 1)
                dve.tensor_scalar(w1, tw, 0.5, 0.5, ALU.mult, ALU.add)
                step(dve.tensor_scalar(w2, tw, -0.5, 0.5, ALU.mult, ALU.add), "routing_step")
                dve.tensor_tensor(oh1, oh1, per_expert(w1), ALU.mult)
                step(dve.tensor_tensor(oh2[:, :, :], oh2[:, :, :], per_expert(w2), ALU.mult), "routing_step")
                dve.tensor_tensor(wd[:, :, :], oh1, oh2[:, :, :], ALU.add).then_inc(sem("weights"), 1)
                dve.wait_ge(sem("B_copied"), 4)
                dve.wait_ge(sem("first_bias"), 1)
                dve.tensor_tensor(Dv[:, 0, :], Dv[:, 0, :], bias_all[:, 1, :], ALU.subtract)

        FFN_ROUNDS = 4
        TILE_STEPS = FFN_ROUNDS * L // NB
        TPR = NB // FFN_ROUNDS
        assert (ROUNDS - FFN_ROUNDS) * L // UNROLL == NB
        assert TILE_STEPS % UNROLL == 0 and TILE_STEPS == 2 * E
        ring = sb("ring", [P, UNROLL, S])
        rs = sb("rs", [P, UNROLL])
        wT = sb("wT", [P, S])
        qv = sb("qv", [P, 6])
        q_now, y_steps, z_steps = qv[:, 0:1], [qv[:, 1:2], qv[:, 2:3]], [qv[:, 3:4], qv[:, 4:5], qv[:, 5:6]]
        sqj = sb("sqj", [P, S])
        d_now = sb("d_now", [P, 2, S])
        ends = sb("ends", [P, 2, S])
        start_now = sb("start_now", [P, S])
        start_old = sb("start_old", [P, S])
        drift = sb("drift", [P, 1])
        drift1 = sb("drift1", [1, 1])
        agreed = sb("agreed", [1, 1], mybir.dt.int32)
        HALF = UNROLL // 2
        PER = L + 1
        psY, psS, psF = banks[0][:, 0:S], banks[0][:, S:3 * S], banks[0][0:1, 3 * S:3 * S + P]
        last = ring[:, UNROLL - 1, :]

        def rsqrt(dve, y_out, count, during=lambda i: None):
            q = q_now
            y0, y1 = y_steps
            z0, z1, z2 = z_steps
            I32 = mybir.dt.int32

            def step(ins, i):
                ins.then_inc(sem(f"root_{i}"), 1)
                during(i)
                dve.wait_ge(sem(f"root_{i}"), count)

            step(dve.tensor_scalar(y0.bitcast(I32), q.bitcast(I32), -0.5, RSQRT_MAGIC, ALU.mult, ALU.add), 1)
            step(dve.scalar_tensor_tensor(out=z0, in0=y0, scalar=y0, in1=q, op0=ALU.mult, op1=ALU.mult), 2)
            step(dve.scalar_tensor_tensor(out=z1, in0=z0, scalar=-10.0 / 3.0, in1=z0, op0=ALU.add, op1=ALU.mult), 3)
            step(dve.scalar_tensor_tensor(out=y1, in0=z1, scalar=5.0, in1=y0, op0=ALU.add, op1=ALU.mult), 4)
            step(dve.scalar_tensor_tensor(out=z2, in0=y1, scalar=y1, in1=q, op0=ALU.mult, op1=ALU.mult), 5)
            step(dve.scalar_tensor_tensor(out=y_out, in0=z2, scalar=-64.0 / 3.0, in1=y1, op0=ALU.add, op1=ALU.mult), 6)

        def vector_steps(dve, r, k0, count, store, between=None):
            for i in range(count):
                k = k0 + i
                u = i % UNROLL
                turn = r * PER + k + 1
                prev = ring[:, (u - 1) % UNROLL, :]
                dve.wait_ge(sem("state"), turn)
                dve.tensor_tensor_reduce(sqj[:, :], prev, prev, 1.0 / S, EPS, ALU.mult, ALU.add, q_now).then_inc(sem("norm"), 1)
                dve.transpose(wT[:, :], prev).then_inc(sem("state_T"), 1)
                if between:
                    between(i)
                dve.wait_ge(sem("norm"), turn)
                if store and u % HALF == 0:
                    dve.wait_ge(sem("stored"), (r - FFN_ROUNDS) * (2 * L // HALF) + (k0 // HALF) * 2 + 2 * (i // HALF) + 2)

                def during(j):
                    if j == 1:
                        dve.tensor_copy(d_now[:, u % 2, :], Dv[:, ds(k, 1), :].squeeze(1))

                rsqrt(dve, rs[:, u:u + 1], turn, during)
                dve.wait_ge(sem("product"), turn)
                dve.scalar_tensor_tensor(out=ring[:, u, :], in0=psY, scalar=rs[:, u:u + 1], in1=d_now[:, u % 2, :],
                                         op0=ALU.mult, op1=ALU.add).then_inc(sem("state"), 1)

        def vector_boundary(dve, r, store):
            dve.wait_ge(sem("state"), r * PER + L + 1)
            dve.tensor_tensor_reduce(sqj[:, :], last, last, 1.0 / S, EPS, ALU.mult, ALU.add, q_now).then_inc(sem("norm"), 1)
            dve.tensor_copy(ends[:, 0, :], last)
            dve.tensor_copy(start_old[:, :], start_now[:, :])
            dve.wait_ge(sem("norm"), r * PER + L + 1)
            rsqrt(dve, Rho[:, L:L + 1], r * PER + L + 1)
            dve.tensor_scalar(ends[:, 1, :], last, Rho[:, L:L + 1], None, ALU.mult).then_inc(sem("state_T"), 1)
            dve.wait_ge(sem("product"), r * PER + L + 1)
            if store:
                dve.wait_ge(sem("stored"), (r + 1 - FFN_ROUNDS) * (2 * L // HALF) + 4)
            dve.tensor_copy(start_now[:, :], psS[:, S:2 * S]).then_inc(sem("new_start"), 1)
            dve.tensor_copy(last, psS[:, 0:S]).then_inc(sem("state"), 1)

        def tensor_step(pe, n):
            pe.wait_ge(sem("state_T"), n + 1)
            pe.sem_inc(sem("tick"), 1)
            for c in range(2):
                for a in range(4):
                    q = slice(32 * a, 32 * a + 32)
                    t = pe.matmul(psY[q], wT[q, 32 * c:32 * c + 32], Mrep[q, c, :], start=(c == 0), stop=(c == 1))
            t.then_inc(sem("product"), 1)

        def tensor_boundary(pe, r):
            pe.wait_ge(sem("state_T"), r * PER + L + 1)
            pe.matmul(psS, shift[:, :], ends[:, :, :].rearrange("p a s -> p (a s)"), start=True, stop=True).then_inc(sem("product"), 1)

        def vector_round(dve, r):
            peeled = isinstance(r, int)
            if peeled:
                def between(i):
                    if 3 <= i <= 3 + SUB:
                        vector_mix(dve, NB, i - 3)

                vector_steps(dve, r, 0, UNROLL, True, between)
            with dve.Fori(1 if peeled else 0, L // UNROLL) as j:
                vector_steps(dve, r, j * UNROLL, UNROLL, True)
            vector_boundary(dve, r, True)

        def tensor_round(pe, r, with_C=False):
            with pe.Fori(0, L // UNROLL) as j:
                for u in range(UNROLL):
                    tensor_step(pe, r * PER + j * UNROLL + u)
                    if with_C and u == 0:
                        n = (r - FFN_ROUNDS) * (L // UNROLL) + j
                        pe.wait_ge(sem("CT_copied"), n + 1)
                        pe.matmul(bE[0][:, :], C_wT[:, :, :].rearrange("p a n -> p (a n)"), xaT[:, ds(n, 1), :].squeeze(1), start=True, stop=True)\
                          .then_inc(sem("C_proj"), 1)
            tensor_boundary(pe, r)

        def pool_round(pool, r):
            with pool.Fori(0, L // UNROLL) as j:
                for h in range(2):
                    at = j * UNROLL + h * HALF
                    part = slice(h * HALF, (h + 1) * HALF)
                    pool.wait_ge(sem("state"), r * PER + j * UNROLL + (h + 1) * HALF + 1)
                    pool.tensor_copy(Wst[:, ds(at, HALF), :], ring[:, part, :]).then_inc(sem("stored"), 1)
                    pool.tensor_copy(Rho[:, ds(at, HALF)], rs[:, part]).then_inc(sem("stored"), 1)

        def rounds(eng, one_round):
            extra = {"with_C": True} if one_round is tensor_round else {}
            one_round(eng, FFN_ROUNDS, **extra)
            with eng.Fori(FFN_ROUNDS + 1, ROUNDS) as r:
                one_round(eng, r, **extra)
            if one_round is pool_round:
                for part in range(5):
                    pool_mix(eng, NB, part)
            if one_round is vector_round:
                eng.wait_ge(sem("new_start"), ROUNDS)
                eng.tensor_tensor(sqj[:, :], start_now[:, :], start_old[:, :], ALU.subtract).then_inc(sem("drift"), 1)
                eng.wait_ge(sem("drift"), 1)
                eng.tensor_reduce(drift[:, 0:1], sqj[:, :], AX_X, ALU.max, apply_absolute_value=True).then_inc(sem("drift_col"), 1)
                eng.wait_ge(sem("drift_row"), 1)
                eng.tensor_reduce(drift1[:, 0:1], psF, AX_X, ALU.max).then_inc(sem("drift"), 1)
                eng.wait_ge(sem("drift"), 2)
                eng.tensor_scalar(agreed[:, :], drift1[:, 0:1], TOLERANCE / abs(RSQRT_FACTOR), None, ALU.is_le).then_inc(sem("agreed"), 1)
            if one_round is tensor_round:
                eng.wait_ge(sem("drift_col"), 1)
                eng.transpose(psF, drift[:, 0:1], ident[:, :]).then_inc(sem("drift_row"), 1)
            eng.wait_ge(sem("agreed"), 1)
            settled = eng.value_load(agreed[0:1, 0:1], min_val=0, max_val=1)
            with eng.If(settled < 1):
                with eng.Fori(ROUNDS, SEG) as r:
                    one_round(eng, r)
            eng.end_ifs()

        xa_cur = zbuf[:, 0]
        xf_cur = sb("xf_cur", [P, 2, SUB, P], F32R)
        wdT_cur = zbuf[0:E, 1]
        gc_w_sum = gate_w[:, 0]
        junk = scratch[:, 0:2 * P].rearrange("p (a h) -> p a h", a=2)
        factor = gi_all[:, :, :].rearrange("p b (s h) -> p (b s) h", s=SUB)
        bH = banks[1:5]
        bE = banks[5:7]
        bR = banks[7]
        bR4 = bR[:, :].rearrange("p (s h) -> p s h", s=SUB)

        def vector_dot(dve, x, w, o, s, name):
            dve.tensor_tensor_reduce(junk[:, s % 2, :], x[:, s, :], w, 1.0, 0.0, ALU.mult, ALU.add, o[:, s:s + 1]).then_inc(sem(name), 1)

        def vector_mix(dve, n, s):
            if s == 0:
                dve.wait_ge(sem("difference"), n + 1)
            if s in (2, 3):
                dve.wait_ge(sem("dot_moe"), n * SUB + s - 1)
            if s < SUB:
                vector_dot(dve, diff, gc_w_all[:, P:2 * P], dot_d, s, "dot_moe")
            else:
                dve.wait_ge(sem("dot_moe"), (n + 1) * SUB)
                dve.wait_ge(sem("dot_abel"), (n + 1) * SUB)
                dve.tensor_tensor(gc, dot_a, dot_d, ALU.add).then_inc(sem("mix_dot"), 1)

        def scalar_mix(act, n, part):
            if part == 0:
                act.wait_ge(sem("mix_dot"), n + 1)
                act.activation(gg, gc, ACT.Tanh, scale=0.5, bias=half_gc_b).then_inc(sem("mix_tanh"), 1)
                act.wait_ge(sem("mix_tanh"), n + 1)
                act.activation(gg, gg, ACT.Copy, scale=0.5, bias=0.5).then_inc(sem("mix_gate"), 1)
                act.wait_ge(sem("mix_gate"), n + 1)
                for s in range(SUB):
                    t = act.activation(pulled[:, s, :], diff[:, s, :], ACT.Copy, scale=gg[:, s:s + 1])
                t.then_inc(sem("pulled"), 1)
            else:
                act.wait_ge(sem("ffn"), n + 1)
                act.activation(silu_t, base, ACT.Tanh, scale=0.5).then_inc(sem("silu_tanh"), 1)

        def pool_mix(pool, n, part):
            if part == 0:
                pool.wait_ge(sem("pulled"), n + 1)
                pool.wait_ge(sem("base"), n + 1)
                pool.tensor_tensor(base, base, pulled[:, :, :], ALU.add).then_inc(sem("ffn"), 1)
            elif part == 1:
                pool.wait_ge(sem("silu_tanh"), n + 1)
                pool.tensor_tensor(silu_t, silu_t, base, ALU.mult).then_inc(sem("silu_product"), 1)
            elif part == 2:
                pool.wait_ge(sem("silu_product"), n + 1)
                pool.tensor_tensor(base, silu_t, base, ALU.add).then_inc(sem("silu"), 1)
            elif part == 3:
                pool.wait_ge(sem("silu"), n + 1)
                pool.wait_ge(sem("gate"), n + 1)
                pool.tensor_tensor(gate_t, gate_t, base, ALU.mult).then_inc(sem("gate_product"), 1)
            else:
                pool.wait_ge(sem("gate_product"), n + 1)
                pool.tensor_tensor(factor[:, ds(n * SUB, SUB), :], gate_t, base, ALU.add).then_inc(sem("mixed"), 1)

        with nc.Block() as block:
            @block.sync
            def _(sp):
                for n in range(NB):
                    if n:
                        sp.wait_ge(sem("expert_bias"), 2 * n)
                        sp.wait_ge(sem("gate_pre"), n)
                    sp.dma_start(wdT_cur, wdT_all[:, n * SUB:(n + 1) * SUB, :]).then_inc(sem("wdT_cur"), 16)
                    sp.dma_start(xa_cur.rearrange("p s h -> p (s h)"), xaT[:, n, :]).then_inc(sem("xa_cur"), 16)

            @block.tensor
            def _(pe):
                with pe.Fori(0, FFN_ROUNDS) as r:
                    with pe.Fori(0, TPR) as t_:
                        n = r * TPR + t_
                        x_tile = [xf[:, a, ds(n, 1), :].squeeze(1) for a in range(2)]

                        def layer1(e):
                            pe.wait_ge(sem("hidden"), n * E + e + 1)
                            for k in range(K):
                                t = split_product(pe, bH[(e % 2) * 2 + k][:, :], [w[:, e, k * P:(k + 1) * P] for w in ew1], x_tile)
                            t.then_inc(sem("pre_hidden"), 1)

                        def layer2(e):
                            pe.wait_ge(sem("hidden"), n * E + e + 3)
                            pe.wait_ge(sem("scaled"), n * E + e + 1)
                            for s in range(SUB):
                                for k in range(K):
                                    t = pe.matmul(bE[e % 2][:, s * P:(s + 1) * P], hT[:, e % 2, k, s * P:(s + 1) * P], ew2[:, e, k, :],
                                                  start=(k == 0), stop=(k == K - 1))
                            t.then_inc(sem("expert_out"), 1)

                        def row_product(x, w, bias, name):
                            pe.matmul(bR[:, :], ones3[:, :], bias, start=True, stop=False)
                            for s in range(SUB):
                                t = pe.matmul(bR[:, s * P:(s + 1) * P], x[:, s, :], w, start=False, stop=(s == SUB - 1))
                            t.then_inc(sem(name), 1)

                        def experts_bias(subtiles):
                            if subtiles[0] == 0:
                                pe.wait_ge(sem("wdT_cur"), 16 * (n + 1))
                                pe.wait_ge(sem("gate"), n + 1)
                            for s in subtiles:
                                t = pe.matmul(bR[:, s * P:(s + 1) * P], wdT_cur[:, s, :], eb2r[:, :], start=True, stop=True)
                            t.then_inc(sem("expert_bias"), 1)

                        def abel_pre(subtiles):
                            if subtiles[0] == 0:
                                pe.wait_ge(sem("xf_cur"), n + 1)
                                pe.wait_ge(sem("sum_started"), n + 1)
                                pe.matmul(bR[:, :], ones3[:, :], abel_b3, start=True, stop=False)
                            for s in subtiles:
                                t = split_product(pe, bR[:, s * P:(s + 1) * P], [xf_cur[:, a, s, :] for a in range(2)], abel_w, False, s == SUB - 1)
                            t.then_inc(sem("abel_pre"), 1)

                        def gate_pre():
                            pe.wait_ge(sem("xa_cur"), 16 * (n + 1))
                            pe.wait_ge(sem("abel"), n + 1)
                            row_product(xa_cur, gate_wT[:, 0, :], gate_b3, "gate_pre")

                        layer1(0)
                        for i in range(TILE_STEPS):
                            tensor_step(pe, r * PER + t_ * TILE_STEPS + i)
                            if i % 2:
                                if i < TILE_STEPS - 1:
                                    layer2(i // 2)
                            elif i < TILE_STEPS - 2:
                                layer1(i // 2 + 1)
                            else:
                                layer2(E - 1)
                            if i in (0, 2):
                                experts_bias((i, i + 1))
                            if i in (6, 8):
                                abel_pre((i - 6, i - 5))
                            if i == TILE_STEPS - 1:
                                gate_pre()
                    tensor_boundary(pe, r)
                rounds(pe, tensor_round)

            @block.scalar
            def _(act):
                act.sem_inc(sem("hidden"), 2)
                act.sem_inc(sem("scaled"), 2)
                act.sem_inc(sem("gate"), 1)
                act.activation(junk_col[:, :], eps_col[:, :], ACT.Gelu)
                with act.Fori(0, NB) as n:
                    def gelus(e):
                        act.wait_ge(sem("pre_hidden"), n * E + e + 1)
                        if e >= 2:
                            act.wait_ge(sem("expert_out"), n * E + e - 1)
                        else:
                            act.wait_ge(sem("expert_out_seen"), n * E + e + 1)
                        for k in range(K):
                            t = act.activation(hT[:, e % 2, k, :], bH[(e % 2) * 2 + k][:, :], ACT.Gelu, bias=eb1_col[:, e, k:k + 1])
                        t.then_inc(sem("hidden"), 1)

                    def scale(e):
                        act.wait_ge(sem("expert_out"), n * E + e + 1)
                        act.wait_ge(sem("added"), n * E + e + 1)
                        for s in range(SUB):
                            w = wd[:, ds(n * SUB + s, 1), e:e + 1].squeeze(1)
                            t = act.activation(scaled[e % 2][:, s, :], bE[e % 2][:, s * P:(s + 1) * P], ACT.Copy, scale=w)
                        t.then_inc(sem("scaled"), 1)
                        act.sem_inc(sem("expert_out_seen"), 1)

                    gelus(0)
                    for a in range(2):
                        t = act.copy(xf_cur[:, a].rearrange("p s h -> p (s h)"), xf[:, a, ds(n, 1), :].squeeze(1))
                    t.then_inc(sem("xf_cur"), 1)
                    gelus(1)
                    scale(0)
                    act.wait_ge(sem("expert_bias"), 2 * (n + 1))
                    act.wait_ge(sem("difference"), n + 1)
                    act.copy(acc, bR4).then_inc(sem("sum_started"), 1)
                    gelus(2)
                    scale(1)
                    gelus(3)
                    scale(2)
                    gelus(4)
                    scalar_mix(act, n, 0)
                    act.wait_ge(sem("abel_pre"), 2 * (n + 1))
                    act.wait_ge(sem("dot_abel"), (n + 1) * SUB)
                    act.wait_ge(sem("base"), n + 1)
                    act.activation(abel, bR4, ACT.Gelu).then_inc(sem("abel"), 1)
                    scale(3)
                    gelus(5)
                    scale(4)
                    scalar_mix(act, n, 1)
                    gelus(6)
                    scale(5)
                    gelus(7)
                    scale(6)
                    act.wait_ge(sem("mixed"), n + 1)
                    for s in range(SUB):
                        q = n * SUB + s
                        t = act.activation(base[:, s, :], X[:, ds(q, 1), :].squeeze(1), ACT.Identity, scale=r1[:, ds(q, 1)], bias=nm1[:, ds(q, 1)])
                    t.then_inc(sem("residual"), 1)
                    act.wait_ge(sem("gate_pre"), n + 1)
                    act.activation(gate_t, bR4, ACT.Tanh, scale=0.5).then_inc(sem("gate"), 1)
                    scale(7)
                act.wait_ge(sem("scaled"), NB * E + 2)
                act.sem_inc(sem("CT_copied"), 1)
                scalar_mix(act, NB, 0)
                with act.Fori(0, NB) as n:
                    act.wait_ge(sem("C_proj"), n + 1)
                    for a in range(2):
                        half = slice(a * S, (a + 1) * S)
                        t = act.activation(CT[half, ds(n * 2, 2), :], bE[0][half, :].rearrange("p (m a h) -> p m a h", m=2, a=2)[:, :, a, :],
                                           ACT.Identity, bias=C_b_col[half])
                    t.then_inc(sem("CT_copied"), 1)
                scalar_mix(act, NB, 1)
                act.wait_ge(sem("agreed"), 1)

            @block.vector
            def _(dve):
                dve.memset(start_now[:, :], 0.0)
                dve.sem_inc(sem("dot_abel"), SUB)
                dve.tensor_tensor(gc_w_sum, gc_w_all[:, 0:P], gc_w_all[:, P:2 * P], ALU.add).then_inc(sem("gc_sum"), 1)
                dve.wait_ge(sem("gc_sum"), 1)
                dve.memset(last, 0.0).then_inc(sem("state"), 1)
                with dve.Fori(0, FFN_ROUNDS) as r:
                    with dve.Fori(0, TPR) as t_:
                        n = r * TPR + t_

                        def between(i):
                            if 3 <= i <= 3 + SUB:
                                vector_mix(dve, n, i - 3)
                            if 10 <= i < 10 + SUB:
                                dve.wait_ge(sem("abel"), n + 1)
                                vector_dot(dve, abel, gc_w_sum, dot_a, i - 10, "dot_abel")

                        vector_steps(dve, r, t_ * TILE_STEPS, TILE_STEPS, False, between)
                    vector_boundary(dve, r, False)
                rounds(dve, vector_round)

            @block.gpsimd
            def _(pool):
                pool.sem_inc(sem("stored"), 4)
                pool.sem_inc(sem("added"), 2)
                pool.sem_inc(sem("expert_out_seen"), 2)
                pool.sem_inc(sem("difference"), 1)
                pool.sem_inc(sem("base"), 1)
                with pool.Fori(0, NB) as n:
                    def add(e):
                        pool.wait_ge(sem("scaled"), n * E + e + 3)
                        if e == 0:
                            pool.wait_ge(sem("sum_started"), n + 1)
                        else:
                            pool.wait_ge(sem("added"), n * E + e + 2)
                        pool.tensor_tensor(acc, acc, scaled[e % 2], ALU.add).then_inc(sem("added"), 1)

                    add(0)
                    add(1)
                    add(2)
                    pool_mix(pool, n, 0)
                    add(3)
                    add(4)
                    pool_mix(pool, n, 1)
                    pool_mix(pool, n, 2)
                    add(5)
                    pool_mix(pool, n, 3)
                    pool_mix(pool, n, 4)
                    add(6)
                    add(7)
                    pool.wait_ge(sem("added"), n * E + E + 2)
                    pool.wait_ge(sem("abel"), n + 1)
                    pool.wait_ge(sem("pulled"), n + 1)
                    pool.wait_ge(sem("mix_dot"), n + 1)
                    pool.tensor_tensor(diff, acc, abel, ALU.subtract).then_inc(sem("difference"), 1)
                    pool.wait_ge(sem("residual"), n + 1)
                    pool.tensor_tensor(base, base, abel, ALU.add).then_inc(sem("base"), 1)
                rounds(pool, pool_round)

        csT = xaT[:, 0:4, :].rearrange("p a b -> p (a b)").rearrange("p (k n) -> p k n", n=P)
        outb = gi.rearrange("p b (s h) -> p b s h", s=SUB)
        with nc.Block() as block:
            @block.vector
            def _(dve):
                H2 = L // 4
                for g in range(4):
                    part = slice(g * H2, (g + 1) * H2)
                    r = Rho[:, g * H2 + 1:(g + 1) * H2 + 1]
                    dve.tensor_tensor(Wst[:, part, :], Wst[:, part, :], r.unsqueeze(2).broadcast_to([P, H2, S]), ALU.mult).then_inc(sem("normalised"), 1)
                for g in range(4):
                    part = slice(g * 4, (g + 1) * 4)
                    dve.wait_ge(sem("state_affine"), g + 1)
                    dve.tensor_tensor(csT[:, part, :], csT[:, part, :], CT[:, part, :], ALU.mult).then_inc(sem("csT"), 1)
                for n in range(NB):
                    dve.wait_ge(sem("ssm"), n + 1)
                    dve.scalar_tensor_tensor(out=outb[:, n], in0=banks[4 + n % 4][:, :].rearrange("p (s h) -> p s h", s=SUB), scalar=0.25,
                                             in1=factor[:, (n + 1) * SUB:(n + 2) * SUB, :], op0=ALU.mult, op1=ALU.mult).then_inc(sem("gated_ssm"), 1)
                    if n % 2:
                        dve.wait_ge(sem("gated_ssm"), n + 1)
                        dve.tensor_tensor(outb[:, n], outb[:, n], X[:, n * SUB:(n + 1) * SUB, :], ALU.add).then_inc(sem("odd_rows"), 1)

            @block.gpsimd
            def _(pool):
                for n in range(0, NB, 2):
                    pool.wait_ge(sem("gated_ssm"), n + 1)
                    pool.tensor_tensor(outb[:, n], outb[:, n], X[:, n * SUB:(n + 1) * SUB, :], ALU.add).then_inc(sem("even_rows"), 1)

            @block.tensor
            def _(pe):
                for g in range(4):
                    pe.wait_ge(sem("normalised"), g + 1)
                    for q in range(4 * g, 4 * g + 4):
                        t = pe.transpose(banks[g][:, (q % 4) * P:(q % 4 + 1) * P], Wst[:, 2 * q:2 * q + 2, :].rearrange("p k n -> p (k n)"), ident[:, :])
                    t.then_inc(sem("cs_T"), 1)
                for n in range(NB):
                    pe.wait_ge(sem("csT"), n // 2 + 1)
                    if n >= 4:
                        pe.wait_ge(sem("gated_ssm"), n - 3)
                    pe.matmul(banks[4 + n % 4][:, :], ones3[:, :], D_b3, start=True, stop=False)
                    for s in range(SUB):
                        t = pe.matmul(banks[4 + n % 4][:, s * P:(s + 1) * P], csT[:, 2 * n + s // 2, :], D_wT[:, s % 2, :],
                                      start=False, stop=(s == SUB - 1))
                    t.then_inc(sem("ssm"), 1)

            @block.scalar
            def _(act):
                for g in range(4):
                    act.wait_ge(sem("cs_T"), g + 1)
                    act.activation(csT[:, g * 4:g * 4 + 4, :], banks[g][:, :].rearrange("p (k n) -> p k n", k=4), ACT.Identity,
                                   scale=state_gain, bias=col["ln_st_b"]).then_inc(sem("state_affine"), 1)

            @block.sync
            def _(sp):
                rows_out = out.rearrange("b (q k) h -> (b q) k h", k=L)
                for n in range(NB):
                    sp.wait_ge(sem("odd_rows" if n % 2 else "even_rows"), n // 2 + 1)
                    sp.dma_start(rows_out[:, n * SUB:(n + 1) * SUB, :], outb[:, n]).then_inc(sem("out_stored"), 16)
                sp.wait_ge(sem("out_stored"), 16 * NB)


_INS = ["L0_attn_x", "L0_attn_A", "L0_attn_dt_A", "L0_attn_B_w", "L0_attn_B_b", "L0_attn_C_w", "L0_attn_C_b", "L0_attn_D_w",
        "L0_attn_D_b", "L0_attn_conv_w", "L0_attn_conv_b", "L0_attn_gate_w", "L0_attn_gate_b", "L0_attn_ln_in_g",
        "L0_attn_ln_in_b", "L0_attn_ln_st_g", "L0_attn_ln_st_b", "L0_ffn_ln_gamma", "L0_ffn_ln_beta", "L0_ffn_abel_w",
        "L0_ffn_abel_b", "L0_ffn_moe_gate_w", "L0_ffn_moe_gate_b", "L0_ffn_ew1", "L0_ffn_eb1", "L0_ffn_ew2", "L0_ffn_eb2",
        "L0_ffn_gens", "L0_ffn_gc_w", "L0_ffn_gc_b"]


def kernel(**inputs):
    import numpy as _np
    import concourse.bacc as _bacc
    from concourse import mybir as _mybir
    from concourse.bass_utils import run_bass_kernel_spmd as _run

    nc = _bacc.Bacc("TRN2", target_bir_lowering=False, num_devices=1)
    arrays, I = {}, {}
    for name in _INS:
        a = _np.ascontiguousarray(inputs[name])
        if a.ndim == 0 or name == "L0_attn_dt_A":
            a = a.reshape(1, 1)
        arrays[f"in_{name}"] = a
        I[name] = nc.dram_tensor(f"in_{name}", a.shape, _mybir.dt.from_np(a.dtype), kind="ExternalInput").ap()
    out = nc.dram_tensor("out_0", inputs["L0_attn_x"].shape, _mybir.dt.float32, kind="ExternalOutput").ap()
    build(nc, I, out)
    r = _run(nc, [arrays], core_ids=[0])
    return r.results[0]["out_0"]
```
